# Optimizing a Trainium2 kernel written in Bass

```python
import numpy as np
import jax
import jax.numpy as jnp

def _softmax(x, axis=-1):
    return jax.nn.softmax(x, axis=axis)

def _gelu(x):
    return jax.nn.gelu(x, approximate=True)

def _silu(x):
    return jax.nn.silu(x)

def _sigmoid(x):
    return jax.nn.sigmoid(x)

def _layernorm(x, axis=-1, eps=1e-05):
    m = jnp.mean(x, axis=axis, keepdims=True)
    v = jnp.var(x, axis=axis, keepdims=True)
    return (x - m) / jnp.sqrt(v + eps)

def _scatter_add(tgt, idx, src, axis=0):
    return tgt.at[idx].add(src)

def _segment_sum(src, seg, n):
    return jax.ops.segment_sum(src, seg, n)
kernel_name = 'mk_gnn_preln_d4_gnn_r64_208abf'

def setup_inputs(seed: int=0):
    np.random.seed(seed)
    _w = jnp.asarray

    def _rec_inputs():
        import jax
        import jax.numpy as jnp
        _gk = jax.random.key(seed)
        x = -0.0003713 + 1 * jax.random.normal(jax.random.fold_in(_gk, 1), (50000, 256), jnp.float32)
        src = jax.random.randint(jax.random.fold_in(_gk, 2), (12500,), 0, 50000, jnp.int32)
        dst = jnp.minimum((50000 * jax.random.uniform(jax.random.fold_in(_gk, 3), (12500,)) ** 2.0).astype(jnp.int32), 49999)
        _o = jnp.argsort(dst, stable=True)
        src = src[_o]
        dst = dst[_o]
        edge_attr_256 = -4.21973e-05 + 0.999841 * jax.random.normal(jax.random.fold_in(_gk, 13), (12500, 256), jnp.float32)
        edge_weight = jax.random.uniform(jax.random.fold_in(_gk, 15), (12500,), jnp.float32, 0.0, 1)
        return (x, src, dst, edge_attr_256, edge_weight)
    x, src, dst, edge_attr_256, edge_weight = _rec_inputs()

    def _L0_gnn_setup():
        import jax, jax.numpy as jnp
        import numpy as np
        N_NODES = 50000
        N_EDGES = 25000
        D_IN = 256
        D_OUT = 256
        K_HOPS = 2

        def spmm(edge_src, edge_dst, edge_val, h):
            msgs = edge_val[:, None] * h[edge_src]
            return jax.ops.segment_sum(msgs, edge_dst, num_segments=N_NODES)
        key = jax.random.key(seed)
        ks = jax.random.split(key, 6)
        x = jax.random.normal(ks[0], (N_NODES, D_IN), dtype=jnp.float32)
        edge_src = jax.random.randint(ks[1], (N_EDGES,), 0, N_NODES, dtype=jnp.int32)
        edge_dst = jax.random.randint(ks[2], (N_EDGES,), 0, N_NODES, dtype=jnp.int32)
        edge_val = jax.random.uniform(ks[3], (N_EDGES,), dtype=jnp.float32)
        stdv = 1.0 / np.sqrt(D_OUT)
        W = jax.random.uniform(ks[4], (K_HOPS, D_IN, D_OUT), dtype=jnp.float32, minval=-stdv, maxval=stdv)
        bias = jax.random.uniform(ks[5], (D_OUT,), dtype=jnp.float32, minval=-stdv, maxval=stdv)
        return {'x': x, 'edge_src': edge_src, 'edge_dst': edge_dst, 'edge_val': edge_val, 'W': W, 'bias': bias}
    _L0_gnn_all = _L0_gnn_setup()
    _L0_gnn_in = {k: v for k, v in _L0_gnn_all.items() if k in ('W', 'bias')}
    del _L0_gnn_all

    def _L1_gnn_setup():
        import jax, jax.numpy as jnp
        import numpy as np
        N_NODES = 50000
        N_EDGES = 25000
        H_SIZE = 256
        HEADS = 8
        HEAD_DIM = H_SIZE // HEADS
        NEG_SLOPE = 0.2
        key = jax.random.key(seed)
        k_x, k_e, k_w, k_as, k_ad, k_b = jax.random.split(key, 6)
        x = jax.random.normal(k_x, (N_NODES, H_SIZE), dtype=jnp.float32)
        edge_index = jax.random.randint(k_e, (2, N_EDGES), 0, N_NODES, dtype=jnp.int64)
        scale = 1.0 / np.sqrt(H_SIZE)
        W = jax.random.normal(k_w, (H_SIZE, HEADS, HEAD_DIM), dtype=jnp.float32) * scale
        att_src = jax.random.normal(k_as, (HEADS, HEAD_DIM), dtype=jnp.float32) * scale
        att_dst = jax.random.normal(k_ad, (HEADS, HEAD_DIM), dtype=jnp.float32) * scale
        bias = jnp.zeros((H_SIZE,), dtype=jnp.float32)
        return {'x': x, 'edge_index': edge_index, 'W': W, 'att_src': att_src, 'att_dst': att_dst, 'bias': bias}
    _L1_gnn_all = _L1_gnn_setup()
    _L1_gnn_in = {k: v for k, v in _L1_gnn_all.items() if k in ('W', 'att_src', 'att_dst', 'bias')}
    del _L1_gnn_all

    def _L2_gnn_setup():
        import jax, jax.numpy as jnp
        import numpy as np
        N_NODES = 100000
        N_EDGES = 50000
        DIM = 256
        LEAKY_SLOPE = 0.2
        EPS = 1e-12
        key = jax.random.key(seed)
        ks = jax.random.split(key, 8)
        embeddings = jax.random.normal(ks[0], (N_NODES, DIM), dtype=jnp.float32)
        edge_src = jax.random.randint(ks[1], (N_EDGES,), 0, N_NODES, dtype=jnp.int32)
        edge_dst = jax.random.randint(ks[2], (N_EDGES,), 0, N_NODES, dtype=jnp.int32)
        edge_val = jax.random.uniform(ks[3], (N_EDGES,), dtype=jnp.float32) / 32.0
        scale = 1.0 / np.sqrt(DIM)
        W1 = jax.random.normal(ks[4], (DIM, DIM), dtype=jnp.float32) * scale
        b1 = jax.random.normal(ks[5], (DIM,), dtype=jnp.float32) * 0.01
        W2 = jax.random.normal(ks[6], (DIM, DIM), dtype=jnp.float32) * scale
        b2 = jax.random.normal(ks[7], (DIM,), dtype=jnp.float32) * 0.01
        return {'embeddings': embeddings, 'edge_src': edge_src, 'edge_dst': edge_dst, 'edge_val': edge_val, 'W1': W1, 'b1': b1, 'W2': W2, 'b2': b2}
    _L2_gnn_all = _L2_gnn_setup()
    _L2_gnn_in = {k: v for k, v in _L2_gnn_all.items() if k in ('W1', 'b1', 'W2', 'b2')}
    del _L2_gnn_all

    def _L3_gnn_setup():
        import jax, jax.numpy as jnp
        import numpy as np
        N, E, D_IN, D_OUT = (50000, 300000, 256, 256)
        BN_EPS = 1e-05

        def ccorr(a, b):
            return jnp.fft.irfft(jnp.conj(jnp.fft.rfft(a, axis=-1)) * jnp.fft.rfft(b, axis=-1), n=a.shape[-1], axis=-1)
        key = jax.random.key(seed)
        ks = jax.random.split(key, 8)
        return {'node_ft': jax.random.normal(ks[0], (N, D_IN), dtype=jnp.float32), 'edge_ft': jax.random.normal(ks[1], (E, D_IN), dtype=jnp.float32), 'norm': jax.random.uniform(ks[2], (N, 1), dtype=jnp.float32), 'w_loop': jax.random.normal(ks[3], (D_IN, D_OUT), dtype=jnp.float32) * (1.414 / np.sqrt(D_IN)), 'w_in': jax.random.normal(ks[4], (D_IN, D_OUT), dtype=jnp.float32) * (1.414 / np.sqrt(D_IN)), 'loop_rel': jax.random.normal(ks[5], (1, D_IN), dtype=jnp.float32), 'w_bias': jnp.zeros((D_OUT,), dtype=jnp.float32), 'bn_gamma': jnp.ones((D_OUT,), dtype=jnp.float32), 'bn_beta': jnp.zeros((D_OUT,), dtype=jnp.float32), 'src': jax.random.randint(ks[6], (E,), 0, N, dtype=jnp.int32), 'dst': jax.random.randint(ks[7], (E,), 0, N, dtype=jnp.int32)}
    _L3_gnn_all = _L3_gnn_setup()
    _L3_gnn_in = {k: v for k, v in _L3_gnn_all.items() if k in ('w_loop', 'w_in', 'loop_rel', 'w_bias', 'bn_gamma', 'bn_beta')}
    del _L3_gnn_all
    return {'x': x, 'src': src, 'dst': dst, 'edge_attr_256': edge_attr_256, 'edge_weight': edge_weight, 'L0_gnn_W': _L0_gnn_in['W'], 'L0_gnn_bias': _L0_gnn_in['bias'], 'L1_gnn_W': _L1_gnn_in['W'], 'L1_gnn_att_src': _L1_gnn_in['att_src'], 'L1_gnn_att_dst': _L1_gnn_in['att_dst'], 'L1_gnn_bias': _L1_gnn_in['bias'], 'L2_gnn_W1': _L2_gnn_in['W1'], 'L2_gnn_b1': _L2_gnn_in['b1'], 'L2_gnn_W2': _L2_gnn_in['W2'], 'L2_gnn_b2': _L2_gnn_in['b2'], 'L3_gnn_w_loop': _L3_gnn_in['w_loop'], 'L3_gnn_w_in': _L3_gnn_in['w_in'], 'L3_gnn_loop_rel': _L3_gnn_in['loop_rel'], 'L3_gnn_w_bias': _L3_gnn_in['w_bias'], 'L3_gnn_bn_gamma': _L3_gnn_in['bn_gamma'], 'L3_gnn_bn_beta': _L3_gnn_in['bn_beta']}

def reference(x, src, dst, edge_attr_256, edge_weight, L0_gnn_W, L0_gnn_bias, L1_gnn_W, L1_gnn_att_src, L1_gnn_att_dst, L1_gnn_bias, L2_gnn_W1, L2_gnn_b1, L2_gnn_W2, L2_gnn_b2, L3_gnn_w_loop, L3_gnn_w_in, L3_gnn_loop_rel, L3_gnn_w_bias, L3_gnn_bn_gamma, L3_gnn_bn_beta):
    import jax
    import jax.numpy as jnp

    def _L0_gnn_ref(x, edge_src, edge_dst, edge_val, W, bias):
        import jax, jax.numpy as jnp
        import numpy as np
        N_NODES = 50000
        N_EDGES = 25000
        D_IN = 256
        D_OUT = 256
        K_HOPS = 2

        def spmm(edge_src, edge_dst, edge_val, h):
            msgs = edge_val[:, None] * h[edge_src]
            return jax.ops.segment_sum(msgs, edge_dst, num_segments=N_NODES)
        h = x
        output = jnp.zeros((N_NODES, D_OUT), dtype=x.dtype)
        for k in range(K_HOPS):
            h = spmm(edge_src, edge_dst, edge_val, h)
            output = output + h @ W[k]
        return output + bias

    def _L1_gnn_ref(x, edge_index, W, att_src, att_dst, bias):
        import jax, jax.numpy as jnp
        import numpy as np
        N_NODES = 50000
        N_EDGES = 25000
        H_SIZE = 256
        HEADS = 8
        HEAD_DIM = H_SIZE // HEADS
        NEG_SLOPE = 0.2
        'GATConv (concat heads) -> relu -> dropout(eval=identity).\n\n            x: [N, F]; edge_index: [2, E] with (src=row0, dst=row1) meaning message j->i.\n            '
        N = x.shape[0]
        h = jnp.einsum('nf,fhd->nhd', x, W)
        a_src = jnp.sum(h * att_src, axis=-1)
        a_dst = jnp.sum(h * att_dst, axis=-1)
        src = edge_index[0]
        dst = edge_index[1]
        e = jax.nn.leaky_relu(a_src[src] + a_dst[dst], NEG_SLOPE)
        e_max = jax.ops.segment_max(e, dst, num_segments=N)
        e_exp = jnp.exp(e - e_max[dst])
        denom = jax.ops.segment_sum(e_exp, dst, num_segments=N)
        alpha = e_exp / (denom[dst] + 1e-16)
        msg = h[src] * alpha[:, :, None]
        out = jax.ops.segment_sum(msg, dst, num_segments=N)
        out = out.reshape(N, -1) + bias
        return jax.nn.relu(out)

    def _L2_gnn_ref(embeddings, edge_src, edge_dst, edge_val, W1, b1, W2, b2):
        import jax, jax.numpy as jnp
        import numpy as np
        N_NODES = 100000
        N_EDGES = 50000
        DIM = 256
        LEAKY_SLOPE = 0.2
        EPS = 1e-12
        ego_emb = embeddings @ W1.T + b1
        messages = edge_val[:, None] * embeddings[edge_src]
        neighbor_emb = jax.ops.segment_sum(messages, edge_dst, num_segments=embeddings.shape[0])
        interaction_emb = neighbor_emb * embeddings
        side_emb = (neighbor_emb + interaction_emb) @ W2.T + b2
        out = ego_emb + side_emb
        out = jnp.where(out >= 0, out, LEAKY_SLOPE * out)
        norm = jnp.sqrt(jnp.sum(out * out, axis=1, keepdims=True))
        return out / jnp.maximum(norm, EPS)

    def _L3_gnn_ref(node_ft, edge_ft, norm, w_loop, w_in, loop_rel, w_bias, bn_gamma, bn_beta, src, dst):
        import jax, jax.numpy as jnp
        import numpy as np
        N, E, D_IN, D_OUT = (50000, 300000, 256, 256)
        BN_EPS = 1e-05

        def ccorr(a, b):
            return jnp.fft.irfft(jnp.conj(jnp.fft.rfft(a, axis=-1)) * jnp.fft.rfft(b, axis=-1), n=a.shape[-1], axis=-1)
        n_nodes = node_ft.shape[0]
        loop_msg = ccorr(node_ft, loop_rel) @ w_loop
        msg = ccorr(node_ft[src], edge_ft) @ w_in
        agg = jax.ops.segment_sum(msg, dst, num_segments=n_nodes) * norm
        h = agg + w_bias + loop_msg
        mean = jnp.mean(h, axis=0)
        var = jnp.var(h, axis=0)
        h = (h - mean) * jax.lax.rsqrt(var + BN_EPS) * bn_gamma + bn_beta
        return jnp.tanh(h)
    edge_index = jnp.stack([src, dst])
    deg = jnp.maximum(jax.ops.segment_sum(jnp.ones(dst.shape, jnp.float32), dst, num_segments=50000), 1.0)
    deg_isqrt = deg ** (-0.5)
    h = jnp.maximum(_layernorm(x, axis=-1), 0.0)
    x = x + _L0_gnn_ref(h, src, dst, edge_weight, L0_gnn_W, L0_gnn_bias)
    h = jnp.maximum(_layernorm(x, axis=-1), 0.0)
    x = x + _L1_gnn_ref(h, edge_index, L1_gnn_W, L1_gnn_att_src, L1_gnn_att_dst, L1_gnn_bias)
    h = jnp.maximum(_layernorm(x, axis=-1), 0.0)
    x = x + _L2_gnn_ref(h, src, dst, edge_weight, L2_gnn_W1, L2_gnn_b1, L2_gnn_W2, L2_gnn_b2)
    h = jnp.maximum(_layernorm(x, axis=-1), 0.0)
    x = x + _L3_gnn_ref(h, edge_attr_256, deg_isqrt[:, None], L3_gnn_w_loop, L3_gnn_w_in, L3_gnn_loop_rel, L3_gnn_w_bias, L3_gnn_bn_gamma, L3_gnn_bn_beta, src, dst)
    return x

_drawn_inputs = setup_inputs


def setup_inputs(seed=0):
    import zlib

    import numpy as np

    out = dict(_drawn_inputs(seed))
    spreads = {'L1_gnn_bias': (0.0, 0.1),
     'L3_gnn_w_bias': (0.0, 2.0),
     'L3_gnn_bn_gamma': (1.0, 0.2),
     'L3_gnn_bn_beta': (0.0, 0.1)}
    factors = {'L1_gnn_att_src': 21.539,
     'L1_gnn_att_dst': 200.0,
     'L2_gnn_b1': 64.0,
     'L2_gnn_W2': 10.338,
     'L2_gnn_b2': 64.0}
    for name, (base, spread) in spreads.items():
        noise = np.random.default_rng([zlib.crc32(name.encode()), seed]).standard_normal(out[name].shape)
        drawn = base * np.exp(spread * noise) if base else spread * noise
        out[name] = jnp.asarray(drawn.astype(out[name].dtype))
    for name, factor in factors.items():
        out[name] = (out[name] * factor).astype(out[name].dtype)
    return out
```

```python
from contextlib import ExitStack

import concourse.bass as bass
import numpy as np
from concourse import mybir
from concourse.alu_op_type import AluOpType as ALU

P = 128
N = 50000
E = 12500
D = 256
H = D // P
HEADS = 8
TILES = 4
GROUP = TILES * P
NODE_GROUPS = -(-N // GROUP)
EDGE_GROUPS = -(-E // GROUP)
NODE_PAD = NODE_GROUPS * GROUP
EDGE_PAD = EDGE_GROUPS * GROUP
EDGE_TILES = EDGE_PAD // P
TAIL_NODES = N - (NODE_GROUPS - 1) * GROUP
TAIL_PARTS = TAIL_NODES // TILES
NO_SLOT = 20000
NO_NODE = 60000
LN_EPS = 1e-5
BN_EPS = 1e-5
SLOPE = 0.2
FAR = 1.0e30

F32 = mybir.dt.float32
BF16 = mybir.dt.bfloat16
I32 = mybir.dt.int32
ACT = mybir.ActivationFunctionType
AX_X = mybir.AxisListType.X


class Step:

    def __init__(self, pair, offset):
        self.pair, self.offset = pair, offset
        self.parity = offset % 2

    def times(self, per, plus=0):
        return self.pair * (2 * per) + (self.offset * per + plus)

    def back(self, k):
        if isinstance(self.pair, int) and self.offset < k:
            return None
        return Step(self.pair, self.offset - k)


class Signal:

    def __init__(self, nc, ctx, name, per, twin):
        self.per, self.twin = per, twin
        self.sems = [ctx.enter_context(nc.semaphore(f"{name}_{i}")) for i in range(2 if twin else 1)]
        self.base = [0, 0]

    def sem(self, step):
        return self.sems[step.parity if self.twin else 0]

    def at(self, step):
        if self.twin:
            return self.sem(step), step.pair * self.per + (self.base[step.parity] + self.per * (step.offset // 2 + 1))
        return self.sem(step), step.times(self.per, self.base[0] + self.per)

    def close(self, n):
        if self.twin:
            self.base = [self.base[0] + self.per * ((n + 1) // 2), self.base[1] + self.per * (n // 2)]
        else:
            self.base[0] += self.per * n


def pipeline(eng, n, stages):
    most = max(lag for lag, _ in stages)
    lead = most + 2 + most % 2
    turns = (n - 1 - lead) // 2

    def tick(pair, i):
        for lag, stage in stages:
            if not isinstance(pair, int) or 0 <= i - lag < n:
                stage(Step(pair, i - lag))

    for i in range(lead):
        tick(0, i)
    with eng.Fori(0, turns) as q:
        tick(q, lead)
        tick(q, lead + 1)
    for i in range(lead + 2 * turns, n + most):
        tick(0, i)


def gnn_kernel(nc, x, src, dst, edge_attr, edge_weight, w_hops, bias0, w_gat, att_src, att_dst, bias1,
               w1_t, b1, w2_t, b2, w_loop, w_in, loop_rel, w_bias, bn_gamma, bn_beta,
               identity, to_freq, from_freq_t, head_rows, out):
    def dram(name, shape, dt=F32):
        return nc.dram_tensor(name, shape, dt).ap()

    slot_of_node = dram("slot_of_node", (NODE_PAD, 1), I32)
    same_flags = dram("same_flags", (1, EDGE_PAD), BF16)
    next_flags = dram("next_flags", (1, EDGE_PAD), BF16)
    rel_twice = dram("rel_twice", (1, 2 * D))
    row_cuts = dram("row_cuts", (3, D), BF16)
    hop1_rows = dram("hop1_rows", (EDGE_PAD, D))
    x1_part = dram("x1_part", (EDGE_PAD, D))
    x1_rows = dram("x1_rows", (EDGE_PAD, D))
    x2_rows = dram("x2_rows", (EDGE_PAD, D))
    x3_rows = dram("x3_rows", (EDGE_PAD, D))
    gat_columns = dram("gat_columns", (EDGE_GROUPS, P, H * GROUP))
    h2_columns = dram("h2_columns", (EDGE_GROUPS, P, H * GROUP))
    h3_columns = dram("h3_columns", (EDGE_GROUPS, P, H * GROUP))
    g_edge_columns = dram("g_edge_columns", (EDGE_GROUPS, P, H * GROUP))
    score_dst = dram("score_dst", (HEADS, EDGE_PAD))
    score_src = dram("score_src", (HEADS, EDGE_PAD))
    exp_rows = dram("exp_rows", (HEADS, EDGE_PAD))
    inv_rows = dram("inv_rows", (HEADS, EDGE_PAD))
    norm_row = dram("norm_row", (EDGE_TILES, P))
    x3_nodes = dram("x3_nodes", (N, D))
    g_node_columns = dram("g_node_columns", (NODE_GROUPS, P, H * GROUP))

    def by_group(rows):
        full = NODE_GROUPS - 1
        return rows[0:full * GROUP].rearrange("(g p j) d -> g p (j d)", p=P, j=TILES)

    def tail_group(rows):
        at = (NODE_GROUPS - 1) * GROUP
        return rows[at:at + TAIL_NODES].rearrange("(p j) d -> p (j d)", j=TILES)

    def edge_groups(rows):
        return rows.rearrange("(g j p) d -> g p j d", p=P, j=TILES)

    ctx = ExitStack()
    with ctx:
        signals = {}
        chain = ctx.enter_context(nc.semaphore("setup_chain"))
        loads = ctx.enter_context(nc.semaphore("setup_loads"))
        pool_turns = ctx.enter_context(nc.semaphore("pool_turns"))
        softmax_step = ctx.enter_context(nc.semaphore("softmax_step"))
        attr_tail = ctx.enter_context(nc.semaphore("attr_tail"))
        count = {"chain": 0, "loads": 0, "phase": 0}

        def link(eng, ins):
            count["chain"] += 1
            ins.then_inc(chain, 1)
            eng.wait_ge(chain, count["chain"])

        def move(eng, *pairs):
            for to, of in pairs:
                eng.dma_start(to, of).then_inc(loads, 16)
                count["loads"] += 16
            eng.wait_ge(loads, count["loads"])

        def tensors(stack):
            count["phase"] += 1
            phase = count["phase"]

            def sb(name, shape, dt=F32):
                return stack.enter_context(nc.sbuf_tensor(f"{name}_p{phase}", shape, dt))
            return sb

        sb = tensors(ctx)
        psum_a = ctx.enter_context(nc.psum_tensor("psum_a", [P, H, GROUP], F32))
        psum_b = ctx.enter_context(nc.psum_tensor("psum_b", [P, H, GROUP], F32))
        psum_c = ctx.enter_context(nc.psum_tensor("psum_c", [P, H, GROUP], F32))
        psum_d = ctx.enter_context(nc.psum_tensor("psum_d", [P, H, GROUP], F32))

        ident = sb("ident", [P, P])
        eps_ln = sb("eps_ln", [P, 1])
        eps_bn = sb("eps_bn", [P, 1])
        src_col = sb("src_col", [P, EDGE_TILES], I32)
        dst_col = sb("dst_col", [P, EDGE_TILES], I32)
        last_col = sb("last_col", [P, EDGE_TILES], I32)
        slot_col = sb("slot_col", [P, EDGE_TILES], I32)
        src_slot = sb("src_slot", [P, EDGE_TILES], I32)
        weight_col = sb("weight_col", [P, EDGE_TILES])
        norm_col = sb("norm_col", [P, EDGE_TILES])
        lone = sb("lone", [P, NODE_GROUPS * TILES])
        same = sb("same", [P, EDGE_PAD], BF16)
        w_hop0 = sb("w_hop0", [P, H, D])
        w_hop1 = sb("w_hop1", [P, H, D])
        gat_w = sb("gat_w", [P, H, D])
        gat_vs = sb("gat_vs", [P, H, HEADS])
        gat_vd = sb("gat_vd", [P, H, HEADS])
        head_sel = sb("head_sel", [HEADS, D])
        w1 = sb("w1", [P, H, D])
        w2 = sb("w2", [P, H, D])
        w_back = sb("w_back", [P, 3, D])
        w_self = sb("w_self", [P, H, D])
        freq = sb("freq", [P, H, D])
        bias0_row = sb("bias0_row", [P, D])
        lone_row = sb("lone_row", [P, D])
        bias1_col = sb("bias1_col", [P, H])
        bias_cuts = sb("bias_cuts", [3, 2 * D], BF16)
        ones_cuts = sb("ones_cuts", [3, P], BF16)
        wbias_col = sb("wbias_col", [P, H])
        gamma_col = sb("gamma_col", [P, H])
        beta_col = sb("beta_col", [P, H])
        node_stats = sb("node_stats", [P, H, (NODE_GROUPS + EDGE_GROUPS) * 6])
        bn_scale = sb("bn_scale", [P, H])
        bn_shift = sb("bn_shift", [P, H])

        with ExitStack() as own:
            sb = tensors(own)
            dst_i, next_i, prev_i, src_i = (sb(n, [EDGE_TILES, P], I32) for n in ("dst_i", "next_i", "prev_i", "src_i"))
            dst_f, next_f, prev_f, src_f, w_f, near_f, last_f = (
                sb(n, [EDGE_TILES, P]) for n in ("dst_f", "next_f", "prev_f", "src_f", "w_f", "near_f", "last_f"))
            same_b = sb("same_b", [EDGE_TILES, P], BF16)
            next_b = sb("next_b", [EDGE_TILES, P], BF16)
            fill = sb("fill", [P, NODE_PAD // P], I32)
            zero_i = sb("zero_i", [1, NODE_PAD - N], I32)
            node_slot = sb("node_slot", [P, NODE_GROUPS * TILES], I32)
            node_slot_f = sb("node_slot_f", [P, NODE_GROUPS * TILES])
            index4 = [sb(f"index4_{b}", [P, TILES], I32) for b in range(2)]
            value4 = [sb(f"value4_{b}", [P, TILES], I32) for b in range(2)]
            att_s = sb("att_s", [P, D])
            att_d = sb("att_d", [P, D])
            prod = sb("prod", [P, D])
            circ = sb("circ", [P, H, D])
            loop_w = sb("loop_w", [P, H, D])
            in_w = sb("in_w", [P, H, D])
            back_t = sb("back_t", [P, H, 3 * P])
            b_row = sb("b_row", [1, 2, D])
            b_rest = sb("b_rest", [1, D])
            b_cut = sb("b_cut", [1, 3, D], BF16)
            b_wide = sb("b_wide", [1, D])
            ones_row = sb("ones_row", [1, P])
            bias1_row = sb("bias1_row", [P, D])
            full = E // P
            rest = E - full * P

            with nc.Block() as block:
                @block.vector
                def _(dve):
                    dve.memset(eps_ln[:], LN_EPS)
                    dve.memset(eps_bn[:], BN_EPS)
                    dve.memset(ones_cuts[:], 1.0)
                    dve.memset(dst_i[:], NO_NODE)
                    dve.memset(next_i[:], NO_NODE)
                    dve.memset(prev_i[:], NO_NODE)
                    dve.memset(src_i[:], 0)
                    dve.memset(w_f[:], 0.0)
                    dve.memset(fill[:], NO_SLOT)
                    link(dve, dve.memset(zero_i[:], 0))

                @block.gpsimd
                def _(pool):
                    pool.iota(slot_col[:], [[P, EDGE_TILES]], base=0, channel_multiplier=1)

            with nc.Block() as block:
                @block.sync
                def _(sp):
                    def edge_rows(to, of):
                        return ((to[0:full, :], of[0:full * P].rearrange("(t p) -> t p", p=P)),
                                (to[full:full + 1, 0:rest], of[full * P:E].rearrange("(t p) -> t p", t=1)))

                    move(sp, (ident[:], identity),
                         *edge_rows(dst_i, dst), *edge_rows(src_i, src), *edge_rows(w_f, edge_weight),
                         (next_i[0:full, :], dst[1:full * P + 1].rearrange("(t p) -> t p", p=P)),
                         (next_i[full:full + 1, 0:rest - 1], dst[full * P + 1:E].rearrange("(t p) -> t p", t=1)),
                         (prev_i[0:1, 1:P], dst[0:P - 1].rearrange("(t p) -> t p", t=1)),
                         (prev_i[1:full, :], dst[P - 1:full * P - 1].rearrange("(t p) -> t p", p=P)),
                         (prev_i[full:full + 1, 0:rest], dst[full * P - 1:E - 1].rearrange("(t p) -> t p", t=1)),
                         (slot_of_node.rearrange("(p q) o -> p (q o)", p=P), fill[:]),
                         (rel_twice[:, 0:D], loop_rel), (rel_twice[:, D:2 * D], loop_rel),
                         *((to[:], of.rearrange("(k p) n -> p k n", p=P)) for to, of in (
                             (w_hop0, w_hops[0]), (w_hop1, w_hops[1]), (gat_w, w_gat), (w1, w1_t), (w2, w2_t),
                             (freq, to_freq), (loop_w, w_loop), (in_w, w_in), (back_t, from_freq_t))),
                         (head_sel[:], head_rows),
                         (b_row[:, 0, :], b1), (b_row[:, 1, :], b2),
                         *((to[:], of.to_broadcast([P, D])) for to, of in (
                             (att_s, att_src), (att_d, att_dst), (bias0_row, bias0), (bias1_row, bias1))))

                @block.scalar
                def _(act):
                    with nc.allow_non_contiguous_dma(reason="one value per partition"):
                        for to, of in ((bias1_col, bias1), (wbias_col, w_bias), (gamma_col, bn_gamma), (beta_col, bn_beta)):
                            act.dma_start(to[:], of.rearrange("o (k p) -> p (o k)", p=P)).then_inc(chain, 16)
                            count["chain"] += 16
                    act.wait_ge(chain, count["chain"])

            with nc.Block() as block:
                @block.sync
                def _(sp):
                    move(sp, (slot_of_node[N:NODE_PAD].rearrange("(o q) i -> o (q i)", o=1), zero_i[:]),
                         *((circ[:, k, :], bass.AP(rel_twice.tensor, k * P, [[1, P], [1, D]])) for k in range(H)))

                @block.vector
                def _(dve):
                    dve.tensor_copy(dst_f[:], dst_i[:])
                    dve.tensor_copy(next_f[:], next_i[:])
                    dve.tensor_copy(prev_f[:], prev_i[:])
                    link(dve, dve.tensor_copy(src_f[:], src_i[:]))
                    dve.tensor_tensor(same_b[:], dst_f[:], prev_f[:], ALU.is_equal)
                    dve.tensor_tensor(next_b[:], dst_f[:], next_f[:], ALU.is_equal)
                    link(dve, dve.tensor_scalar(near_f[:], dst_f[:], float(N - 1), None, ALU.min))
                    link(dve, dve.scalar_tensor_tensor(last_f[:], next_b[:], float(NO_NODE), dst_f[:], ALU.mult, ALU.add))
                    for att, v in ((att_s, gat_vs), (att_d, gat_vd)):
                        for k in range(H):
                            link(dve, dve.tensor_tensor(prod[:], gat_w[:, k, :], att[:], ALU.mult))
                            link(dve, dve.tensor_reduce(v[:, k, :], prod[:].rearrange("p (h d) -> p h d", h=HEADS), AX_X, ALU.add))
                    link(dve, dve.tensor_scalar(prod[:], bias1_row[:], 0.0, None, ALU.max))
                    link(dve, dve.tensor_tensor(lone_row[:], prod[:], bias0_row[:], ALU.add))
                    link(dve, dve.tensor_tensor(b_rest[:], b_row[:, 0, :], b_row[:, 1, :], ALU.add))
                    for cut in range(3):
                        link(dve, dve.tensor_copy(b_cut[:, cut, :], b_rest[:]))
                        link(dve, dve.tensor_copy(b_wide[:], b_cut[:, cut, :]))
                        link(dve, dve.tensor_tensor(b_rest[:], b_rest[:], b_wide[:], ALU.subtract))

            with nc.Block() as block:
                @block.tensor
                def _(pe):
                    for i, rows in enumerate((src_f, near_f, last_f, w_f)):
                        pe.transpose(psum_a[:, 0, i * P:i * P + EDGE_TILES], rows[:], ident[0:EDGE_TILES, 0:EDGE_TILES])
                    for half in range(H):
                        for k in range(H):
                            pe.matmul(psum_b[:, half, 0:D], circ[:, k, half * P:(half + 1) * P], loop_w[:, k, :],
                                      start=k == 0, stop=k == H - 1)
                    for part in range(3):
                        for k in range(H):
                            last = pe.matmul((psum_c if part < 2 else psum_d)[:, part % 2, 0:D],
                                             back_t[:, k, part * P:(part + 1) * P], in_w[:, k, :],
                                             start=k == 0, stop=k == H - 1)
                    link(pe, last)

                @block.sync
                def _(sp):
                    move(sp, (same_flags.rearrange("o (t p) -> (o t) p", p=P), same_b[:]),
                         (next_flags.rearrange("o (t p) -> (o t) p", p=P), next_b[:]),
                         (row_cuts.rearrange("(o c) d -> o c d", o=1), b_cut[:]))

            with nc.Block() as block:
                @block.vector
                def _(dve):
                    for i, to in enumerate((src_col, dst_col, last_col, weight_col)):
                        dve.tensor_copy(to[:], psum_a[:, 0, i * P:i * P + EDGE_TILES])
                    for half in range(H):
                        dve.tensor_copy(w_self[:, half, :], psum_b[:, half, 0:D])
                    for part in range(3):
                        last = dve.tensor_copy(w_back[:, part, :], (psum_c if part < 2 else psum_d)[:, part % 2, 0:D])
                    link(dve, last)

                @block.sync
                def _(sp):
                    move(sp, (same[:], same_flags.to_broadcast([P, EDGE_PAD])),
                         (bias_cuts[:, 0:D], row_cuts), (bias_cuts[:, D:2 * D], row_cuts))

            def signal(name, per=1, twin=False):
                if name not in signals:
                    signals[name] = Signal(nc, ctx, name, per, twin)
                assert (signals[name].per, signals[name].twin) == (per, twin), name
                used.append(signals[name])
                return signals[name]

            def close(n):
                for s in used:
                    s.close(n)
                used.clear()

            used = []
            slots_sent = signal("slots_sent", 16 * TILES, twin=True)
            slots_got = signal("slots_got", 16 * TILES, twin=True)
            index_copied = signal("index_copied", 2)
            slot_kept = signal("slot_kept")
            with nc.Block() as block:
                @block.gpsimd
                def _(pool):
                    def scatter(st):
                        b = st.parity
                        if st.back(2):
                            pool.wait_ge(*slots_sent.at(st.back(2)))
                        pool.tensor_copy(index4[b][:], last_col[:, bass.ds(st.times(TILES), TILES)]).then_inc(index_copied.sem(st), 1)
                        pool.tensor_copy(value4[b][:], slot_col[:, bass.ds(st.times(TILES), TILES)]).then_inc(index_copied.sem(st), 1)
                        pool.wait_ge(*index_copied.at(st))
                        pool.sem_inc(pool_turns, 1)
                        for j in range(TILES):
                            pool.indirect_dma_start(
                                slot_of_node, bass.IndirectOffsetOnAxis(index4[b][:, j:j + 1], 0), value4[b][:, j:j + 1], None,
                                bounds_check=N - 1, oob_is_err=False).then_inc(slots_sent.sem(st), 16)

                    pipeline(pool, EDGE_GROUPS, [(0, scatter)])
                    pool.wait_ge(*slots_sent.at(Step(0, EDGE_GROUPS - 1)))
                    pool.wait_ge(*slots_sent.at(Step(0, EDGE_GROUPS - 2)))

            index_copied.close(EDGE_GROUPS)
            with nc.Block() as block:
                @block.gpsimd
                def _(pool):
                    def gather(st):
                        b = st.parity
                        if st.back(2):
                            pool.wait_ge(*slot_kept.at(st.back(2)))
                        pool.tensor_copy(index4[b][:], src_col[:, bass.ds(st.times(TILES), TILES)]).then_inc(index_copied.sem(st), 2)
                        pool.wait_ge(*index_copied.at(st))
                        pool.sem_inc(pool_turns, 1)
                        for j in range(TILES):
                            pool.indirect_dma_start(
                                value4[b][:, j:j + 1], None, slot_of_node, bass.IndirectOffsetOnAxis(index4[b][:, j:j + 1], 0),
                                bounds_check=N - 1, oob_is_err=False).then_inc(slots_got.sem(st), 16)

                    pipeline(pool, EDGE_GROUPS, [(0, gather)])

                @block.vector
                def _(dve):
                    def keep(st):
                        dve.wait_ge(*slots_got.at(st))
                        dve.tensor_copy(src_slot[:, bass.ds(st.times(TILES), TILES)], value4[st.parity][:]).then_inc(slot_kept.sem(st), 1)

                    pipeline(dve, EDGE_GROUPS, [(0, keep)])
                    dve.wait_ge(*slot_kept.at(Step(0, EDGE_GROUPS - 1)))

                @block.sync
                def _(sp):
                    move(sp, (node_slot[:].rearrange("p (g j) -> p g j", j=TILES),
                              slot_of_node.rearrange("(g p j) o -> p g (j o)", p=P, j=TILES)))
            close(EDGE_GROUPS)

            with nc.Block() as block:
                @block.vector
                def _(dve):
                    link(dve, dve.tensor_copy(node_slot_f[:], node_slot[:]))
                    link(dve, dve.tensor_scalar(lone[:], node_slot_f[:], float(NO_SLOT), None, ALU.is_equal))

        class Norm:

            def __init__(self, sb, name, rows, rows_ready, psum, taken, scale=None, weight=None):
                self.rows, self.rows_ready, self.psum, self.taken = rows, rows_ready, psum, taken
                self.scale, self.weight = scale, weight
                two = range(2)
                self.stats = [sb(f"{name}_stats{b}", [P, TILES, 6]) for b in two]
                self.mean2 = [sb(f"{name}_mean2_{b}", [P, TILES]) for b in two]
                self.apart = [sb(f"{name}_apart{b}", [P, TILES]) for b in two]
                self.var = [sb(f"{name}_var{b}", [P, TILES]) for b in two]
                self.dev = [sb(f"{name}_dev{b}", [P, TILES]) for b in two]
                self.inv = [sb(f"{name}_inv{b}", [P, TILES]) for b in two]
                self.off = [sb(f"{name}_off{b}", [P, TILES]) for b in two]
                self.h = [sb(f"{name}_h{b}", [P, TILES, D]) for b in two]
                self.pair_done = signal(f"{name}_pair_done", 3)
                self.moments_done = signal(f"{name}_moments_done")
                self.dev_done = signal(f"{name}_dev_done")
                self.inv_done = signal(f"{name}_inv_done", 3 if scale else 2)
                self.h_done = signal(f"{name}_h_done")
                if weight:
                    self.weighted = signal(f"{name}_weighted")
                self.turned = signal(f"{name}_turned")

            def moments_of(self, dve, st):
                b = st.parity
                dve.wait_ge(*self.rows_ready.at(st))
                for j in range(TILES):
                    last = dve.bn_stats(self.stats[b][:, j, :], self.rows[b][:, j, :])
                sem, value = self.pair_done.at(st)
                last.then_inc(sem, 1)
                dve.wait_ge(sem, value - 2)
                even, odd = self.stats[b][:, :, 0:3], self.stats[b][:, :, 3:6]
                dve.tensor_tensor(self.apart[b][:], even[:, :, 1], odd[:, :, 1], ALU.subtract)
                dve.tensor_tensor(self.mean2[b][:], even[:, :, 1], odd[:, :, 1], ALU.add)
                dve.tensor_tensor(self.var[b][:], even[:, :, 2], odd[:, :, 2], ALU.add).then_inc(sem, 1)
                dve.wait_ge(sem, value - 1)
                dve.scalar_tensor_tensor(self.apart[b][:], self.apart[b][:], D / 4.0, self.apart[b][:], ALU.mult, ALU.mult)\
                   .then_inc(sem, 1)
                dve.wait_ge(sem, value)
                dve.tensor_tensor(self.var[b][:], self.var[b][:], self.apart[b][:], ALU.add).then_inc(self.moments_done.sem(st), 1)

            def deviation(self, act, st):
                b = st.parity
                act.wait_ge(*self.moments_done.at(st))
                act.activation(self.dev[b][:], self.var[b][:], ACT.Sqrt, bias=eps_ln[:], scale=1.0 / D).then_inc(self.dev_done.sem(st), 1)

            def inverse(self, dve, st):
                b, done = st.parity, self.inv_done
                sem, value = done.at(st)
                dve.wait_ge(*self.dev_done.at(st))
                if st.back(2):
                    dve.wait_ge(*self.h_done.at(st.back(2)))
                dve.reciprocal(self.inv[b][:], self.dev[b][:]).then_inc(sem, 1)
                dve.wait_ge(sem, value - done.per + 1)
                if self.scale:
                    dve.tensor_tensor(self.inv[b][:], self.inv[b][:], self.scale(st), ALU.mult).then_inc(sem, 1)
                    dve.wait_ge(sem, value - 1)
                dve.scalar_tensor_tensor(self.off[b][:], self.mean2[b][:], -0.5, self.inv[b][:], ALU.mult, ALU.mult)\
                   .then_inc(sem, 1)

            def normalise(self, act, st):
                b = st.parity
                act.wait_ge(*self.inv_done.at(st))
                if st.back(2):
                    act.wait_ge(*self.turned.at(st.back(2)))
                for j in range(TILES):
                    last = act.activation(self.h[b][:, j, :], self.rows[b][:, j, :], ACT.Relu,
                                          bias=self.off[b][:, j:j + 1], scale=self.inv[b][:, j:j + 1])
                last.then_inc(self.h_done.sem(st), 1)

            def weigh(self, dve, st):
                b = st.parity
                dve.wait_ge(*self.h_done.at(st))
                w = self.weight(st)
                for j in range(TILES):
                    last = dve.tensor_scalar(self.h[b][:, j, :], self.h[b][:, j, :], w(j), None, ALU.mult)
                last.then_inc(self.weighted.sem(st), 1)

            def turn(self, pe, st):
                b = st.parity
                pe.wait_ge(*(self.weighted if self.weight else self.h_done).at(st))
                if st.back(1):
                    pe.wait_ge(*self.taken.at(st.back(1)))
                for k in range(H):
                    for j in range(TILES):
                        last = pe.transpose(self.psum[:, k, j * P:(j + 1) * P], self.h[b][:, j, k * P:(k + 1) * P], ident[:])
                last.then_inc(self.turned.sem(st), 1)

        def rows_product(pe, to, columns, weights, start=True, stop=True):
            for j in range(TILES):
                for k in range(H):
                    last = pe.matmul(to[:, j // 2, (j % 2) * D:(j % 2 + 1) * D], columns[:, k, j * P:(j + 1) * P],
                                     weights[:, k, :], start=start and k == 0, stop=stop and k == H - 1,
                                     skip_group_check=True)
            return last

        def last_two(eng, sig, n):
            eng.wait_ge(*sig.at(Step(0, n - 2)))
            eng.wait_ge(*sig.at(Step(0, n - 1)))

        def tile_rows(t):
            return t[:].rearrange("p (j d) -> p j d", j=TILES)

        def pair_rows(psum):
            return psum[:].rearrange("p h (j d) -> p (h j) d", j=2)

        class Tail:

            def __init__(self, sb, product_done, base, base_ready, out_free):
                two = range(2)
                self.product_done, self.base, self.base_ready, self.out_free = product_done, base, base_ready, out_free
                self.leaky = [sb(f"tail_leaky{b}", [P, TILES, D]) for b in two]
                self.square = [sb(f"tail_square{b}", [P, TILES, D]) for b in two]
                self.total = [sb(f"tail_total{b}", [P, TILES]) for b in two]
                self.length = [sb(f"tail_length{b}", [P, TILES]) for b in two]
                self.inv = [sb(f"tail_inv{b}", [P, TILES]) for b in two]
                self.x3 = [sb(f"tail_x3{b}", [P, TILES, D]) for b in two]
                self.slope_done = signal("tail_slope_done")
                self.leaky_done = signal("tail_leaky_done")
                self.length_done = signal("tail_length_done", 2)
                self.inv_done = signal("tail_inv_done", 2)
                self.x3_done = signal("tail_x3_done")

            def slope(self, act, st):
                b = st.parity
                act.wait_ge(*self.product_done.at(st))
                if st.back(2):
                    act.wait_ge(*self.x3_done.at(st.back(2)))
                act.activation(self.leaky[b][:], pair_rows(psum_b), ACT.Copy, scale=SLOPE).then_inc(self.slope_done.sem(st), 1)

            def leak(self, dve, st):
                b = st.parity
                dve.wait_ge(*self.slope_done.at(st))
                dve.tensor_tensor(self.leaky[b][:], pair_rows(psum_b), self.leaky[b][:], ALU.max).then_inc(self.leaky_done.sem(st), 1)

            def square_up(self, act, st):
                b = st.parity
                act.wait_ge(*self.leaky_done.at(st))
                sem, value = self.length_done.at(st)
                for j in range(TILES):
                    last = act.activation(self.square[b][:, j, :], self.leaky[b][:, j, :], ACT.Square, accum_out=self.total[b][:, j:j + 1])
                last.then_inc(sem, 1)
                act.wait_ge(sem, value - 1)
                act.activation(self.length[b][:], self.total[b][:], ACT.Sqrt).then_inc(sem, 1)

            def residual(self, dve, st):
                b = st.parity
                dve.wait_ge(*self.length_done.at(st))
                sem, value = self.inv_done.at(st)
                dve.tensor_scalar(self.inv[b][:], self.length[b][:], 1e-12, None, ALU.max).then_inc(sem, 1)
                dve.wait_ge(sem, value - 1)
                dve.reciprocal(self.inv[b][:], self.inv[b][:]).then_inc(sem, 1)
                dve.wait_ge(sem, value)
                if self.base_ready:
                    dve.wait_ge(*self.base_ready.at(st))
                for sig in self.out_free:
                    if st.back(2):
                        dve.wait_ge(*sig.at(st.back(2)))
                for j in range(TILES):
                    last = dve.scalar_tensor_tensor(self.x3[b][:, j, :], self.leaky[b][:, j, :], self.inv[b][:, j:j + 1],
                                                    self.base[b][:, j, :], ALU.mult, ALU.add)
                last.then_inc(self.x3_done.sem(st), 1)

        with ExitStack() as own:
            sb = tensors(own)
            two = range(2)
            n = NODE_GROUPS
            x_in = [sb(f"x_in{b}", [P, TILES * D]) for b in two]
            x2 = [sb(f"x2_{b}", [P, TILES, D]) for b in two]
            h2c = [sb(f"h2c{b}", [P, H, GROUP]) for b in two]
            h3c = [sb(f"h3c{b}", [P, H, GROUP]) for b in two]
            gc = [sb(f"gc{b}", [P, H, GROUP]) for b in two]
            x_landed = signal("x_landed", 16, twin=True)
            x2_done = signal("x2_done")
            h2c_done = signal("h2c_done")
            y_done = signal("y_done")
            x3_stored = signal("x3_stored", 16, twin=True)
            h3c_done = signal("h3c_done")
            g_done = signal("g_done")
            g_stats = signal("g_stats")
            gc_done = signal("gc_done")
            g_stored = signal("g_stored", 16, twin=True)
            norm2 = Norm(sb, "norm2", x2, x2_done, psum_a, h2c_done)
            norm3 = Norm(sb, "norm3", None, None, psum_c, h3c_done,
                         scale=lambda st: lone[:, bass.ds(st.times(TILES), TILES)])
            tail = Tail(sb, y_done, x2, None, [x3_stored, norm3.h_done])
            norm3.rows, norm3.rows_ready = tail.x3, tail.x3_done

            x_groups, x3_groups = by_group(x), by_group(x3_nodes)

            with nc.Block() as block:
                @block.sync
                def _(sp):
                    def load(st):
                        if st.back(2):
                            sp.wait_ge(*x2_done.at(st.back(2)))
                        if isinstance(st.pair, int) and st.offset == n - 1:
                            sp.dma_start(x_in[st.parity][0:TAIL_PARTS, :], tail_group(x)).then_inc(x_landed.sem(st), 16)
                        else:
                            sp.dma_start(x_in[st.parity][:], x_groups[st.times(1)]).then_inc(x_landed.sem(st), 16)

                    def store_x3(st):
                        sp.wait_ge(*tail.x3_done.at(st))
                        rows = tail.x3[st.parity][:].rearrange("p j d -> p (j d)")
                        if isinstance(st.pair, int) and st.offset == n - 1:
                            sp.dma_start(tail_group(x3_nodes), rows[0:TAIL_PARTS]).then_inc(x3_stored.sem(st), 16)
                        else:
                            sp.dma_start(x3_groups[st.times(1)], rows).then_inc(x3_stored.sem(st), 16)

                    def store_g(st):
                        sp.wait_ge(*gc_done.at(st))
                        sp.dma_start(g_node_columns[st.times(1)], gc[st.parity][:].rearrange("p k n -> p (k n)"))\
                          .then_inc(g_stored.sem(st), 16)

                    pipeline(sp, n, [(0, load), (3, store_x3), (4, store_g)])
                    last_two(sp, x3_stored, n)
                    last_two(sp, g_stored, n)

                @block.gpsimd
                def _(pool):
                    def add(st):
                        b = st.parity
                        pool.wait_ge(*x_landed.at(st))
                        if st.back(2):
                            pool.wait_ge(*tail.x3_done.at(st.back(2)))
                        pool.tensor_tensor(x2[b][:], tile_rows(x_in[b]), lone_row[:].unsqueeze(1).to_broadcast([P, TILES, D]), ALU.add)\
                            .then_inc(x2_done.sem(st), 1)

                    pipeline(pool, n, [(1, add)])

                @block.scalar
                def _(act):
                    def h2_out(st):
                        act.wait_ge(*norm2.turned.at(st))
                        if st.back(2):
                            act.wait_ge(*y_done.at(st.back(2)))
                        act.activation(h2c[st.parity][:], psum_a[:], ACT.Copy).then_inc(h2c_done.sem(st), 1)

                    def g_out(st):
                        act.wait_ge(*g_done.at(st))
                        if st.back(2):
                            act.wait_ge(*g_stored.at(st.back(2)))
                            act.wait_ge(*g_stats.at(st.back(2)))
                        act.activation(gc[st.parity][:], psum_d[:], ACT.Copy).then_inc(gc_done.sem(st), 1)

                    pipeline(act, n, [(1, lambda st: norm2.deviation(act, st)),
                                      (3, lambda st: norm3.deviation(act, st)),
                                      (1, lambda st: norm2.normalise(act, st)),
                                      (4, g_out),
                                      (3, lambda st: norm3.normalise(act, st)),
                                      (1, h2_out),
                                      (2, lambda st: tail.slope(act, st)),
                                      (2, lambda st: tail.square_up(act, st))])

                @block.vector
                def _(dve):
                    def h3_out(st):
                        dve.wait_ge(*norm3.turned.at(st))
                        if st.back(2):
                            dve.wait_ge(*g_done.at(st.back(2)))
                        dve.tensor_copy(h3c[st.parity][:], psum_c[:]).then_inc(h3c_done.sem(st), 1)

                    def stats(st):
                        dve.wait_ge(*gc_done.at(st))
                        for k in range(H):
                            last = dve.bn_stats(node_stats[:, k, bass.ds(st.times(6), 6)], gc[st.parity][:, k, :])
                        last.then_inc(g_stats.sem(st), 1)

                    pipeline(dve, n, [(1, lambda st: norm2.moments_of(dve, st)),
                                      (3, lambda st: norm3.moments_of(dve, st)),
                                      (1, lambda st: norm2.inverse(dve, st)),
                                      (3, lambda st: norm3.inverse(dve, st)),
                                      (4, stats),
                                      (3, h3_out),
                                      (2, lambda st: tail.leak(dve, st)),
                                      (2, lambda st: tail.residual(dve, st))])
                    dve.wait_ge(*g_stats.at(Step(0, n - 1)))

                @block.tensor
                def _(pe):
                    def product(st):
                        pe.wait_ge(*h2c_done.at(st))
                        if st.back(1):
                            pe.wait_ge(*tail.leaky_done.at(st.back(1)))
                        for half in range(2):
                            pe.matmul(psum_b[:, half, :], ones_cuts[:], bias_cuts[:], start=True, stop=False, skip_group_check=True)
                        rows_product(pe, psum_b, h2c[st.parity], w1, start=False).then_inc(y_done.sem(st), 1)

                    def self_product(st):
                        pe.wait_ge(*h3c_done.at(st))
                        if st.back(1):
                            pe.wait_ge(*gc_done.at(st.back(1)))
                        for half in range(H):
                            for k in range(H):
                                last = pe.matmul(psum_d[:, half, :], w_self[:, k, half * P:(half + 1) * P], h3c[st.parity][:, k, :],
                                                 start=k == 0, stop=k == H - 1)
                        last.then_inc(g_done.sem(st), 1)

                    pipeline(pe, n, [(1, lambda st: norm2.turn(pe, st)),
                                     (4, self_product),
                                     (3, lambda st: norm3.turn(pe, st)),
                                     (2, product)])
            close(n)

        class Gather:

            def __init__(self, sb, name, table, index, free, bound, base=None, over=None, over_index=None, zero=False):
                self.table, self.index, self.free, self.bound = table, index, free, bound
                self.base, self.over, self.over_index, self.zero = base, over, over_index, zero
                self.rows = [sb(f"{name}_rows{b}", [P, TILES, D]) for b in range(2)]
                self.at = [sb(f"{name}_at{b}", [P, TILES], I32) for b in range(2)]
                self.index_done = signal(f"{name}_index_done")
                self.landed = signal(f"{name}_landed", 16 * TILES, twin=True)
                if zero:
                    self.zeroed = signal(f"{name}_zeroed")
                if over is not None:
                    self.over_at = [sb(f"{name}_over_at{b}", [P, TILES], I32) for b in range(2)]
                    self.over_index_done = signal(f"{name}_over_index_done")
                    self.added = signal(f"{name}_added")
                    self.over_landed = signal(f"{name}_over_landed", 16 * TILES, twin=True)
                self.ready = self.over_landed if over is not None else self.landed

            def fetch(self, pool, st):
                b = st.parity
                for sig in self.free:
                    if st.back(2):
                        pool.wait_ge(*sig.at(st.back(2)))
                pool.tensor_copy(self.at[b][:], self.index[:, bass.ds(st.times(TILES), TILES)]).then_inc(self.index_done.sem(st), 1)
                if self.zero:
                    pool.memset(self.rows[b][:], 0.0).then_inc(self.zeroed.sem(st), 1)
                    pool.wait_ge(*self.zeroed.at(st))
                pool.wait_ge(*self.index_done.at(st))
                pool.sem_inc(pool_turns, 1)
                for j in range(TILES):
                    pool.indirect_dma_start(self.rows[b][:, j, :], None, self.table,
                                            bass.IndirectOffsetOnAxis(self.at[b][:, j:j + 1], 0),
                                            bounds_check=self.bound, oob_is_err=False).then_inc(self.landed.sem(st), 16)

            def add_base(self, dve, st):
                b = st.parity
                dve.wait_ge(*self.landed.at(st))
                dve.tensor_tensor(self.rows[b][:], self.rows[b][:], self.base[:].unsqueeze(1).to_broadcast([P, TILES, D]), ALU.add)\
                   .then_inc(self.added.sem(st), 1)

            def overlay(self, pool, st):
                b = st.parity
                pool.tensor_copy(self.over_at[b][:], self.over_index[:, bass.ds(st.times(TILES), TILES)])\
                    .then_inc(self.over_index_done.sem(st), 1)
                pool.wait_ge(*self.over_index_done.at(st))
                pool.wait_ge(*self.added.at(st))
                pool.sem_inc(pool_turns, 1)
                for j in range(TILES):
                    pool.indirect_dma_start(self.rows[b][:, j, :], None, self.over,
                                            bass.IndirectOffsetOnAxis(self.over_at[b][:, j:j + 1], 0),
                                            bounds_check=EDGE_PAD - 1, oob_is_err=False).then_inc(self.over_landed.sem(st), 16)

        class Sums:

            def __init__(self, sb, name, source, ready, free, parts=H):
                self.source, self.ready, self.free, self.parts = source, ready, free, parts
                self.columns = [sb(f"{name}_sums{b}", [P, parts, GROUP]) for b in range(2)]
                self.done = signal(f"{name}_sums_done")

            def scan(self, dve, st):
                b = st.parity
                dve.wait_ge(*self.ready.at(st))
                for sig in self.free:
                    if st.back(2):
                        dve.wait_ge(*sig.at(st.back(2)))
                if st.back(1):
                    dve.wait_ge(*self.done.at(st.back(1)))
                for k in range(self.parts):
                    carry = self.columns[1 - b][:, k, GROUP - 1:GROUP] if st.back(1) else 0.0
                    source = self.source[b][:, k, :] if isinstance(self.source, list) else self.source[:, k, :]
                    last = dve.tensor_tensor_scan(self.columns[b][:, k, :], same[:, bass.ds(st.times(GROUP), GROUP)], source,
                                                  carry, ALU.mult, ALU.add)
                last.then_inc(self.done.sem(st), 1)

        def tile_weight(st):
            return lambda j: weight_col[:, bass.ds(st.times(TILES, j), 1)]

        def turn_back(pe, psum, columns):
            for j in range(TILES):
                for k in range(H):
                    last = pe.transpose(psum[:, j // 2, (j % 2) * D + k * P:(j % 2) * D + (k + 1) * P],
                                        columns[:, k, j * P:(j + 1) * P], ident[:])
            return last

        def columns_product(pe, to, weights, columns, start=True, stop=True):
            parts = columns.shape[1]
            for half in range(H):
                for k in range(parts):
                    last = pe.matmul(to[:, half, :], weights[:, k, half * P:(half + 1) * P], columns[:, k, :],
                                     start=start and k == 0, stop=stop and k == parts - 1, skip_group_check=True)
            return last

        n = EDGE_GROUPS
        two = range(2)

        with ExitStack() as own:
            sb = tensors(own)
            back_done = signal("back_done")
            part_done = signal("part_done")
            hop_stored = signal("hop_stored", 16, twin=True)
            part_stored = signal("part_stored", 16, twin=True)
            rows_back = [sb(f"rows_back{b}", [P, TILES, D]) for b in two]
            part = [sb(f"part{b}", [P, TILES, D]) for b in two]
            product_done = signal("product_done")
            back_turned = signal("back_turned")
            added_up = signal("added_up")
            norm = Norm(sb, "norm", None, None, psum_a, None, weight=tile_weight)
            src_rows = Gather(sb, "src", x, src_col, [norm.h_done], N - 1)
            dst_rows = Gather(sb, "dst", x, dst_col, [part_done], N - 1)
            norm.rows, norm.rows_ready = src_rows.rows, src_rows.ready
            sums = Sums(sb, "hop", psum_a, norm.turned, [product_done])
            norm.taken = sums.done
            with nc.Block() as block:
                @block.gpsimd
                def _(pool):
                    pipeline(pool, n, [(0, lambda st: src_rows.fetch(pool, st)), (0, lambda st: dst_rows.fetch(pool, st))])

                @block.scalar
                def _(act):
                    def back(st):
                        act.wait_ge(*back_turned.at(st))
                        if st.back(2):
                            act.wait_ge(*hop_stored.at(st.back(2)))
                        act.activation(rows_back[st.parity][:], pair_rows(psum_c), ACT.Copy).then_inc(back_done.sem(st), 1)

                    pipeline(act, n, [(1, lambda st: norm.deviation(act, st)), (1, lambda st: norm.normalise(act, st)), (2, back)])

                @block.vector
                def _(dve):
                    def add_up(st):
                        b = st.parity
                        dve.wait_ge(*product_done.at(st))
                        dve.wait_ge(*dst_rows.ready.at(st))
                        if st.back(2):
                            dve.wait_ge(*part_stored.at(st.back(2)))
                        dve.tensor_tensor(part[b][:], pair_rows(psum_b), dst_rows.rows[b][:], ALU.add).then_inc(added_up.sem(st), 1)
                        dve.wait_ge(*added_up.at(st))
                        dve.tensor_tensor(part[b][:], part[b][:], bias0_row[:].unsqueeze(1).to_broadcast([P, TILES, D]), ALU.add)\
                           .then_inc(part_done.sem(st), 1)

                    pipeline(dve, n, [(1, lambda st: norm.moments_of(dve, st)), (1, lambda st: norm.inverse(dve, st)),
                                      (2, add_up), (1, lambda st: norm.weigh(dve, st)), (1, lambda st: sums.scan(dve, st))])

                @block.tensor
                def _(pe):
                    def product(st):
                        pe.wait_ge(*sums.done.at(st))
                        if st.back(1):
                            pe.wait_ge(*back_done.at(st.back(1)))
                            pe.wait_ge(*added_up.at(st.back(1)))
                        turn_back(pe, psum_c, sums.columns[st.parity]).then_inc(back_turned.sem(st), 1)
                        rows_product(pe, psum_b, sums.columns[st.parity], w_hop0).then_inc(product_done.sem(st), 1)

                    pipeline(pe, n, [(2, product), (1, lambda st: norm.turn(pe, st))])

                @block.sync
                def _(sp):
                    def store(st):
                        sp.wait_ge(*back_done.at(st))
                        sp.dma_start(edge_groups(hop1_rows)[st.times(1)], rows_back[st.parity][:]).then_inc(hop_stored.sem(st), 16)
                        sp.wait_ge(*part_done.at(st))
                        sp.dma_start(edge_groups(x1_part)[st.times(1)], part[st.parity][:]).then_inc(part_stored.sem(st), 16)

                    pipeline(sp, n, [(2, store)])
                    last_two(sp, hop_stored, n)
                    last_two(sp, part_stored, n)
            close(n)

        with ExitStack() as own:
            sb = tensors(own)
            weighted = signal("weighted")
            turned = signal("turned")
            product_done = signal("product_done")
            part_landed = signal("part_landed", 16, twin=True)
            x1_done = signal("x1_done")
            x1_stored = signal("x1_stored", 16, twin=True)
            h1c_done = signal("h1c_done")
            score_done = signal("score_done")
            score_out = signal("score_out")
            score_stored = signal("score_stored", 16, twin=True)
            part = [sb(f"part{b}", [P, TILES, D]) for b in two]
            x1 = [sb(f"x1_{b}", [P, TILES, D]) for b in two]
            scaled = [sb(f"scaled{b}", [P, TILES, D]) for b in two]
            h1c = [sb(f"h1c{b}", [P, H, GROUP]) for b in two]
            score = [sb(f"score{b}", [HEADS, GROUP]) for b in two]
            hop_rows = Gather(sb, "src", hop1_rows, src_slot, [weighted], EDGE_PAD - 1, zero=True)
            sums = Sums(sb, "hop", psum_a, turned, [product_done])
            norm = Norm(sb, "norm_dst", x1, x1_done, psum_c, h1c_done)
            with nc.Block() as block:
                @block.gpsimd
                def _(pool):
                    pipeline(pool, n, [(0, lambda st: hop_rows.fetch(pool, st))])

                @block.scalar
                def _(act):
                    def h1_out(st):
                        act.wait_ge(*norm.turned.at(st))
                        if st.back(2):
                            act.wait_ge(*score_done.at(st.back(2)))
                        act.activation(h1c[st.parity][:], psum_c[:], ACT.Copy).then_inc(h1c_done.sem(st), 1)

                    def out_score(st):
                        act.wait_ge(*score_done.at(st))
                        if st.back(2):
                            act.wait_ge(*score_stored.at(st.back(2)))
                        act.activation(score[st.parity][:], psum_d[0:HEADS, 0, :], ACT.Copy).then_inc(score_out.sem(st), 1)

                    pipeline(act, n, [(3, lambda st: norm.deviation(act, st)), (3, lambda st: norm.normalise(act, st)),
                                      (3, h1_out), (4, out_score)])

                @block.vector
                def _(dve):
                    def weigh(st):
                        b = st.parity
                        dve.wait_ge(*hop_rows.ready.at(st))
                        if st.back(2):
                            dve.wait_ge(*turned.at(st.back(2)))
                        for j in range(TILES):
                            last = dve.tensor_scalar(scaled[b][:, j, :], hop_rows.rows[b][:, j, :], tile_weight(st)(j), None, ALU.mult)
                        last.then_inc(weighted.sem(st), 1)

                    def add_up(st):
                        b = st.parity
                        dve.wait_ge(*product_done.at(st))
                        dve.wait_ge(*part_landed.at(st))
                        if st.back(2):
                            dve.wait_ge(*x1_stored.at(st.back(2)))
                            dve.wait_ge(*norm.h_done.at(st.back(2)))
                        dve.tensor_tensor(x1[b][:], pair_rows(psum_b), part[b][:], ALU.add).then_inc(x1_done.sem(st), 1)

                    pipeline(dve, n, [(1, weigh), (3, lambda st: norm.moments_of(dve, st)), (3, lambda st: norm.inverse(dve, st)),
                                      (1, lambda st: sums.scan(dve, st)), (2, add_up)])

                @block.tensor
                def _(pe):
                    def turn(st):
                        pe.wait_ge(*weighted.at(st))
                        if st.back(1):
                            pe.wait_ge(*sums.done.at(st.back(1)))
                        for k in range(H):
                            for j in range(TILES):
                                last = pe.transpose(psum_a[:, k, j * P:(j + 1) * P], scaled[st.parity][:, j, k * P:(k + 1) * P], ident[:])
                        last.then_inc(turned.sem(st), 1)

                    def product(st):
                        pe.wait_ge(*sums.done.at(st))
                        if st.back(1):
                            pe.wait_ge(*x1_done.at(st.back(1)))
                        rows_product(pe, psum_b, sums.columns[st.parity], w_hop1).then_inc(product_done.sem(st), 1)

                    def scores(st):
                        pe.wait_ge(*h1c_done.at(st))
                        if st.back(1):
                            pe.wait_ge(*score_out.at(st.back(1)))
                        for k in range(H):
                            last = pe.matmul(psum_d[0:HEADS, 0, :], gat_vd[:, k, :], h1c[st.parity][:, k, :], start=k == 0, stop=k == H - 1)
                        last.then_inc(score_done.sem(st), 1)

                    pipeline(pe, n, [(1, turn), (3, lambda st: norm.turn(pe, st)), (2, product), (4, scores)])

                @block.sync
                def _(sp):
                    def load(st):
                        if st.back(2):
                            sp.wait_ge(*x1_done.at(st.back(2)))
                        sp.dma_start(part[st.parity][:], edge_groups(x1_part)[st.times(1)]).then_inc(part_landed.sem(st), 16)

                    def store(st):
                        sp.wait_ge(*x1_done.at(st))
                        sp.dma_start(edge_groups(x1_rows)[st.times(1)], x1[st.parity][:]).then_inc(x1_stored.sem(st), 16)

                    def store_score(st):
                        sp.wait_ge(*score_out.at(st))
                        sp.dma_start(score_dst[:, bass.ds(st.times(GROUP), GROUP)], score[st.parity][:]).then_inc(score_stored.sem(st), 16)

                    pipeline(sp, n, [(1, load), (3, store), (5, store_score)])
                    last_two(sp, x1_stored, n)
                    last_two(sp, score_stored, n)
            close(n)

        with ExitStack() as own:
            sb = tensors(own)
            h1c_done = signal("h1c_done")
            gat_done = signal("gat_done")
            gat_out = signal("gat_out")
            gat_stored = signal("gat_stored", 16, twin=True)
            score_out = signal("score_out")
            score_stored = signal("score_stored", 16, twin=True)
            h1c = [sb(f"h1c{b}", [P, H, GROUP]) for b in two]
            gat = [sb(f"gat{b}", [P, H, GROUP]) for b in two]
            score = [sb(f"score{b}", [HEADS, GROUP]) for b in two]
            norm = Norm(sb, "norm_src", None, None, psum_a, h1c_done)
            src_rows = Gather(sb, "src", x, src_col, [norm.h_done], N - 1, base=bias0_row, over=x1_rows, over_index=src_slot)
            norm.rows, norm.rows_ready = src_rows.rows, src_rows.ready
            with nc.Block() as block:
                @block.gpsimd
                def _(pool):
                    pipeline(pool, n, [(0, lambda st: src_rows.fetch(pool, st)), (1, lambda st: src_rows.overlay(pool, st))])

                @block.scalar
                def _(act):
                    def h1_out(st):
                        act.wait_ge(*norm.turned.at(st))
                        if st.back(2):
                            act.wait_ge(*gat_done.at(st.back(2)))
                        act.activation(h1c[st.parity][:], psum_a[:], ACT.Copy).then_inc(h1c_done.sem(st), 1)

                    def out_score(st):
                        act.wait_ge(*gat_done.at(st))
                        if st.back(2):
                            act.wait_ge(*score_stored.at(st.back(2)))
                        act.activation(score[st.parity][:], psum_d[0:HEADS, 0, :], ACT.Copy).then_inc(score_out.sem(st), 1)

                    pipeline(act, n, [(2, lambda st: norm.deviation(act, st)), (2, lambda st: norm.normalise(act, st)),
                                      (3, out_score), (2, h1_out)])

                @block.vector
                def _(dve):
                    def out_gat(st):
                        dve.wait_ge(*gat_done.at(st))
                        if st.back(2):
                            dve.wait_ge(*gat_stored.at(st.back(2)))
                        dve.tensor_copy(gat[st.parity][:], psum_b[:]).then_inc(gat_out.sem(st), 1)

                    pipeline(dve, n, [(1, lambda st: src_rows.add_base(dve, st)), (2, lambda st: norm.moments_of(dve, st)),
                                      (3, out_gat), (2, lambda st: norm.inverse(dve, st))])

                @block.tensor
                def _(pe):
                    def product(st):
                        pe.wait_ge(*h1c_done.at(st))
                        if st.back(1):
                            pe.wait_ge(*gat_out.at(st.back(1)))
                            pe.wait_ge(*score_out.at(st.back(1)))
                        for k in range(H):
                            pe.matmul(psum_d[0:HEADS, 0, :], gat_vs[:, k, :], h1c[st.parity][:, k, :], start=k == 0, stop=k == H - 1)
                        columns_product(pe, psum_b, gat_w, h1c[st.parity]).then_inc(gat_done.sem(st), 1)

                    pipeline(pe, n, [(3, product), (2, lambda st: norm.turn(pe, st))])

                @block.sync
                def _(sp):
                    def store(st):
                        sp.wait_ge(*score_out.at(st))
                        sp.dma_start(score_src[:, bass.ds(st.times(GROUP), GROUP)], score[st.parity][:]).then_inc(score_stored.sem(st), 16)
                        sp.wait_ge(*gat_out.at(st))
                        sp.dma_start(gat_columns[st.times(1)], gat[st.parity][:].rearrange("p k n -> p (k n)"))\
                          .then_inc(gat_stored.sem(st), 16)

                    pipeline(sp, n, [(3, store)])
                    last_two(sp, gat_stored, n)
                    last_two(sp, score_stored, n)
            close(n)

        with ExitStack() as own:
            sb = tensors(own)
            a = sb("softmax_a", [HEADS, EDGE_PAD])
            b = sb("softmax_b", [HEADS, EDGE_PAD])
            nxt = sb("softmax_next", [HEADS, EDGE_PAD], BF16)
            reset = sb("softmax_reset", [HEADS, EDGE_PAD // 5])
            norm_t = sb("norm_t", [EDGE_TILES, P])

            def spread(dve):
                link(dve, dve.scalar_tensor_tensor(b[:], nxt[:], 0.0, b[:], ALU.is_equal, ALU.mult))
                link(dve, dve.tensor_tensor_scan(b[:, ::-1], nxt[:, ::-1], b[:, ::-1], 0.0, ALU.mult, ALU.add))

            with nc.Block() as block:
                @block.sync
                def _(sp):
                    move(sp, (a[:], score_src), (b[:], score_dst), (nxt[:], next_flags.to_broadcast([HEADS, EDGE_PAD])))

            with nc.Block() as block:
                @block.vector
                def _(dve):
                    spread(dve)
                    link(dve, dve.tensor_tensor(a[:], a[:], b[:], ALU.add))
                    link(dve, dve.scalar_tensor_tensor(a[:], a[:], SLOPE, a[:], ALU.mult, ALU.max))
                    wide = EDGE_PAD // 5
                    for i in range(5):
                        piece = slice(i * wide, (i + 1) * wide)
                        link(dve, dve.tensor_scalar(reset[:], same[0:HEADS, piece], FAR, -FAR, ALU.mult, ALU.add))
                        link(dve, dve.tensor_tensor_scan(b[:, piece], reset[:], a[:, piece],
                                                         b[:, i * wide - 1:i * wide] if i else -FAR, ALU.add, ALU.max))
                    spread(dve)
                    link(dve, dve.tensor_tensor(a[:], a[:], b[:], ALU.subtract))

            with nc.Block() as block:
                @block.scalar
                def _(act):
                    link(act, act.activation(a[:], a[:], ACT.Exp))

            with nc.Block() as block:
                @block.sync
                def _(sp):
                    move(sp, (exp_rows, a[:]))

                @block.vector
                def _(dve):
                    dve.tensor_tensor_scan(b[:], same[0:HEADS, :], a[:], 0.0, ALU.mult, ALU.add).then_inc(softmax_step, 1)
                    dve.wait_ge(softmax_step, 1)
                    dve.tensor_scalar(b[:], b[:], 1e-16, None, ALU.add).then_inc(softmax_step, 1)
                    dve.wait_ge(softmax_step, 2)
                    dve.reciprocal(b[:], b[:]).then_inc(softmax_step, 1)
                    dve.wait_ge(softmax_step, 3)

            with nc.Block() as block:
                @block.sync
                def _(sp):
                    move(sp, (inv_rows, b[:]))

                @block.vector
                def _(dve):
                    link(dve, dve.memset(a[:], 1.0))

            with nc.Block() as block:
                @block.vector
                def _(dve):
                    link(dve, dve.tensor_tensor_scan(b[:], same[0:HEADS, :], a[:], 0.0, ALU.mult, ALU.add))
                    spread(dve)
                    link(dve, dve.tensor_scalar(b[:], b[:], 1.0, None, ALU.max))

            with nc.Block() as block:
                @block.sync
                def _(sp):
                    move(sp, (norm_row.rearrange("(o t) p -> o (t p)", o=1), b[0:1, :]))
                    move(sp, (norm_t[:], norm_row))

            with nc.Block() as block:
                @block.scalar
                def _(act):
                    link(act, act.activation(norm_t[:], norm_t[:], ACT.Sqrt))

            with nc.Block() as block:
                @block.vector
                def _(dve):
                    link(dve, dve.reciprocal(norm_t[:], norm_t[:]))

            with nc.Block() as block:
                @block.tensor
                def _(pe):
                    link(pe, pe.transpose(psum_a[:, 0, 0:EDGE_TILES], norm_t[:], ident[0:EDGE_TILES, 0:EDGE_TILES]))

            with nc.Block() as block:
                @block.vector
                def _(dve):
                    link(dve, dve.tensor_copy(norm_col[:], psum_a[:, 0, 0:EDGE_TILES]))

        with ExitStack() as own:
            sb = tensors(own)
            gat_landed = signal("gat_landed", 16, twin=True)
            parts_landed = signal("parts_landed", 32, twin=True)
            part_landed = signal("part_landed", 16, twin=True)
            spread_done = signal("spread_done")
            message_done = signal("message_done")
            divided = signal("divided")
            relu_done = signal("relu_done")
            back_turned = signal("back_turned")
            x2e_done = signal("x2e_done")
            x2e_stored = signal("x2e_stored", 16, twin=True)
            h2c_done = signal("h2c_done")
            h2c_stored = signal("h2c_stored", 16, twin=True)
            gat = [sb(f"gat{i}", [P, H, GROUP]) for i in two]
            exps = [sb(f"exps{i}", [HEADS, GROUP]) for i in two]
            invs = [sb(f"invs{i}", [HEADS, GROUP]) for i in two]
            message = [sb(f"message{i}", [P, H, GROUP]) for i in two]
            ratio = [sb(f"ratio{i}", [P, H, GROUP]) for i in two]
            part = [sb(f"part{i}", [P, TILES, D]) for i in two]
            x2e = [sb(f"x2e{i}", [P, TILES, D]) for i in two]
            h2c = [sb(f"h2c{i}", [P, H, GROUP]) for i in two]
            sums = Sums(sb, "gat", message, message_done, [divided])
            norm = Norm(sb, "norm2", x2e, x2e_done, psum_d, h2c_done)
            with nc.Block() as block:
                @block.scalar
                def _(act):
                    def relu(st):
                        i = st.parity
                        act.wait_ge(*divided.at(st))
                        sem, value = relu_done.at(st)
                        for k in range(H):
                            last = act.activation(ratio[i][:, k, :], ratio[i][:, k, :], ACT.Relu, bias=bias1_col[:, k:k + 1])
                        last.then_inc(sem, 1)

                    def h2_out(st):
                        act.wait_ge(*norm.turned.at(st))
                        if st.back(2):
                            act.wait_ge(*h2c_stored.at(st.back(2)))
                        act.activation(h2c[st.parity][:], psum_d[:], ACT.Copy).then_inc(h2c_done.sem(st), 1)

                    pipeline(act, n, [(2, lambda st: norm.deviation(act, st)), (2, lambda st: norm.normalise(act, st)),
                                      (1, relu), (2, h2_out)])

                @block.vector
                def _(dve):
                    def weigh(st):
                        i = st.parity
                        dve.wait_ge(*gat_landed.at(st))
                        dve.wait_ge(*spread_done.at(st))
                        dve.tensor_tensor(message[i][:], gat[i][:], psum_a[:], ALU.mult).then_inc(message_done.sem(st), 1)

                    def divide(st):
                        i = st.parity
                        dve.wait_ge(*sums.done.at(st))
                        if st.back(2):
                            dve.wait_ge(*back_turned.at(st.back(2)))
                        dve.tensor_tensor(ratio[i][:], sums.columns[i][:], psum_b[:], ALU.mult).then_inc(divided.sem(st), 1)

                    def add_up(st):
                        i = st.parity
                        dve.wait_ge(*back_turned.at(st))
                        dve.wait_ge(*part_landed.at(st))
                        if st.back(2):
                            dve.wait_ge(*x2e_stored.at(st.back(2)))
                            dve.wait_ge(*norm.h_done.at(st.back(2)))
                        dve.tensor_tensor(x2e[i][:], pair_rows(psum_c), part[i][:], ALU.add).then_inc(x2e_done.sem(st), 1)

                    pipeline(dve, n, [(2, add_up), (2, lambda st: norm.moments_of(dve, st)),
                                      (1, weigh), (2, lambda st: norm.inverse(dve, st)),
                                      (1, lambda st: sums.scan(dve, st)), (1, divide)])

                @block.tensor
                def _(pe):
                    def spread_heads(st):
                        i = st.parity
                        pe.wait_ge(*parts_landed.at(st))
                        if st.back(1):
                            pe.wait_ge(*divided.at(st.back(1)))
                        for psum, rows in ((psum_a, exps), (psum_b, invs)):
                            for k in range(H):
                                last = pe.matmul(psum[:, k, :], head_sel[:, k * P:(k + 1) * P], rows[i][:], start=True, stop=True)
                        last.then_inc(spread_done.sem(st), 1)

                    def back(st):
                        pe.wait_ge(*relu_done.at(st))
                        if st.back(1):
                            pe.wait_ge(*x2e_done.at(st.back(1)))
                        turn_back(pe, psum_c, ratio[st.parity]).then_inc(back_turned.sem(st), 1)

                    pipeline(pe, n, [(1, spread_heads), (2, lambda st: norm.turn(pe, st)), (1, back)])

                @block.sync
                def _(sp):
                    def load(st):
                        i = st.parity
                        if st.back(2):
                            sp.wait_ge(*divided.at(st.back(2)))
                        sp.dma_start(exps[i][:], exp_rows[:, bass.ds(st.times(GROUP), GROUP)]).then_inc(parts_landed.sem(st), 16)
                        sp.dma_start(invs[i][:], inv_rows[:, bass.ds(st.times(GROUP), GROUP)]).then_inc(parts_landed.sem(st), 16)
                        sp.dma_start(gat[i][:].rearrange("p k n -> p (k n)"), gat_columns[st.times(1)]).then_inc(gat_landed.sem(st), 16)
                        if st.back(2):
                            sp.wait_ge(*x2e_done.at(st.back(2)))
                        sp.dma_start(part[i][:], edge_groups(x1_rows)[st.times(1)]).then_inc(part_landed.sem(st), 16)

                    def store(st):
                        i = st.parity
                        sp.wait_ge(*x2e_done.at(st))
                        sp.dma_start(edge_groups(x2_rows)[st.times(1)], x2e[i][:]).then_inc(x2e_stored.sem(st), 16)
                        sp.wait_ge(*h2c_done.at(st))
                        sp.dma_start(h2_columns[st.times(1)], h2c[i][:].rearrange("p k n -> p (k n)")).then_inc(h2c_stored.sem(st), 16)

                    pipeline(sp, n, [(0, load), (2, store)])
                    last_two(sp, x2e_stored, n)
                    last_two(sp, h2c_stored, n)
            close(n)

        with ExitStack() as own:
            sb = tensors(own)
            h2c_landed = signal("h2c_landed", 16, twin=True)
            part_landed = signal("part_landed", 16, twin=True)
            side_done = signal("side_done")
            y_done = signal("y_done")
            x3_stored = signal("x3_stored", 16, twin=True)
            x3_sent = signal("x3_sent", 16 * TILES, twin=True)
            last_copied = signal("last_copied")
            h3c_done = signal("h3c_done")
            h3c_stored = signal("h3c_stored", 16, twin=True)
            h2c = [sb(f"h2c{i}", [P, H, GROUP]) for i in two]
            side = [sb(f"side{i}", [P, H, GROUP]) for i in two]
            part = [sb(f"part{i}", [P, TILES, D]) for i in two]
            h3c = [sb(f"h3c{i}", [P, H, GROUP]) for i in two]
            last_at = [sb(f"last_at{i}", [P, TILES], I32) for i in two]
            norm = Norm(sb, "norm", None, None, psum_a, None, weight=tile_weight)
            src_rows = Gather(sb, "src", x, src_col, [norm.h_done], N - 1, base=lone_row, over=x2_rows, over_index=src_slot)
            norm.rows, norm.rows_ready = src_rows.rows, src_rows.ready
            sums = Sums(sb, "hop", psum_a, norm.turned, [side_done])
            norm.taken = sums.done
            norm3 = Norm(sb, "norm_dst", None, None, psum_c, h3c_done)
            tail = Tail(sb, y_done, part, part_landed, [x3_stored, x3_sent, norm3.h_done])
            norm3.rows, norm3.rows_ready = tail.x3, tail.x3_done
            with nc.Block() as block:
                @block.gpsimd
                def _(pool):
                    def send(st):
                        i = st.parity
                        if st.back(2):
                            pool.wait_ge(*x3_sent.at(st.back(2)))
                        pool.tensor_copy(last_at[i][:], last_col[:, bass.ds(st.times(TILES), TILES)]).then_inc(last_copied.sem(st), 1)
                        pool.wait_ge(*last_copied.at(st))
                        pool.wait_ge(*tail.x3_done.at(st))
                        pool.sem_inc(pool_turns, 1)
                        for j in range(TILES):
                            pool.indirect_dma_start(x3_nodes, bass.IndirectOffsetOnAxis(last_at[i][:, j:j + 1], 0),
                                                    tail.x3[i][:, j, :], None, bounds_check=N - 1, oob_is_err=False)\
                                .then_inc(x3_sent.sem(st), 16)

                    pipeline(pool, n, [(0, lambda st: src_rows.fetch(pool, st)), (1, lambda st: src_rows.overlay(pool, st)), (4, send)])
                    last_two(pool, x3_sent, n)

                @block.scalar
                def _(act):
                    def h3_out(st):
                        act.wait_ge(*norm3.turned.at(st))
                        if st.back(2):
                            act.wait_ge(*h3c_stored.at(st.back(2)))
                        act.activation(h3c[st.parity][:], psum_c[:], ACT.Copy).then_inc(h3c_done.sem(st), 1)

                    pipeline(act, n, [(2, lambda st: norm.deviation(act, st)), (4, lambda st: norm3.deviation(act, st)),
                                      (2, lambda st: norm.normalise(act, st)), (4, lambda st: norm3.normalise(act, st)),
                                      (3, lambda st: tail.slope(act, st)), (4, h3_out),
                                      (3, lambda st: tail.square_up(act, st))])

                @block.vector
                def _(dve):
                    def interact(st):
                        i = st.parity
                        dve.wait_ge(*sums.done.at(st))
                        dve.wait_ge(*h2c_landed.at(st))
                        if st.back(2):
                            dve.wait_ge(*y_done.at(st.back(2)))
                        dve.scalar_tensor_tensor(side[i][:], h2c[i][:], 1.0, sums.columns[i][:], ALU.add, ALU.mult)\
                           .then_inc(side_done.sem(st), 1)

                    pipeline(dve, n, [(1, lambda st: src_rows.add_base(dve, st)),
                                      (2, lambda st: norm.moments_of(dve, st)), (4, lambda st: norm3.moments_of(dve, st)),
                                      (2, lambda st: norm.inverse(dve, st)), (4, lambda st: norm3.inverse(dve, st)),
                                      (3, lambda st: tail.leak(dve, st)), (2, lambda st: norm.weigh(dve, st)),
                                      (3, lambda st: tail.residual(dve, st)),
                                      (2, lambda st: sums.scan(dve, st)), (2, interact)])

                @block.tensor
                def _(pe):
                    def product(st):
                        pe.wait_ge(*side_done.at(st))
                        if st.back(1):
                            pe.wait_ge(*tail.leaky_done.at(st.back(1)))
                        for half in range(2):
                            pe.matmul(psum_b[:, half, :], ones_cuts[:], bias_cuts[:], start=True, stop=False, skip_group_check=True)
                        rows_product(pe, psum_b, h2c[st.parity], w1, start=False, stop=False)
                        rows_product(pe, psum_b, side[st.parity], w2, start=False).then_inc(y_done.sem(st), 1)

                    pipeline(pe, n, [(3, product), (2, lambda st: norm.turn(pe, st)), (4, lambda st: norm3.turn(pe, st))])

                @block.sync
                def _(sp):
                    def load(st):
                        i = st.parity
                        if st.back(2):
                            sp.wait_ge(*y_done.at(st.back(2)))
                            sp.wait_ge(*tail.x3_done.at(st.back(2)))
                        sp.dma_start(h2c[i][:].rearrange("p k n -> p (k n)"), h2_columns[st.times(1)]).then_inc(h2c_landed.sem(st), 16)
                        sp.dma_start(part[i][:], edge_groups(x2_rows)[st.times(1)]).then_inc(part_landed.sem(st), 16)

                    def store(st):
                        i = st.parity
                        sp.wait_ge(*tail.x3_done.at(st))
                        sp.dma_start(edge_groups(x3_rows)[st.times(1)], tail.x3[i][:]).then_inc(x3_stored.sem(st), 16)

                    def store_columns(st):
                        i = st.parity
                        sp.wait_ge(*h3c_done.at(st))
                        sp.dma_start(h3_columns[st.times(1)], h3c[i][:].rearrange("p k n -> p (k n)")).then_inc(h3c_stored.sem(st), 16)

                    pipeline(sp, n, [(2, load), (4, store), (5, store_columns)])
                    last_two(sp, x3_stored, n)
                    last_two(sp, h3c_stored, n)
            close(n)

        with ExitStack() as own:
            sb = tensors(own)
            attr_landed = signal("attr_landed", 16, twin=True)
            attr_turned = signal("attr_turned")
            attr_out = signal("attr_out")
            hsc_done = signal("hsc_done")
            freq_done = signal("freq_done")
            attr_freq_out = signal("attr_freq_out")
            crossed = signal("crossed")
            multiplied = signal("multiplied")
            h3c_landed = signal("h3c_landed", 16, twin=True)
            g_done = signal("g_done")
            g_masked = signal("g_masked")
            g_counted = signal("g_counted")
            ge_stored = signal("ge_stored", 16, twin=True)
            attr = [sb(f"attr{i}", [P, TILES, D]) for i in two]
            attr_c = [sb(f"attr_c{i}", [P, H, GROUP]) for i in two]
            hsc = [sb(f"hsc{i}", [P, H, GROUP]) for i in two]
            attr_f = [sb(f"attr_f{i}", [P, H, GROUP]) for i in two]
            cross = sb("cross", [P, 2, GROUP])
            products = [sb(f"products{i}", [P, 3, GROUP]) for i in two]
            h3c = [sb(f"h3c{i}", [P, H, GROUP]) for i in two]
            ge = [sb(f"ge{i}", [P, H, GROUP]) for i in two]
            nxt = sb("next_wide", [P, EDGE_PAD], BF16)
            norm = Norm(sb, "norm3", None, None, psum_a, attr_out,
                        scale=lambda st: norm_col[:, bass.ds(st.times(TILES), TILES)])
            src_rows = Gather(sb, "src", x3_nodes, src_col, [norm.h_done], N - 1)
            norm.rows, norm.rows_ready = src_rows.rows, src_rows.ready
            sums = Sums(sb, "freq", products, multiplied, [g_done], parts=3)
            with nc.Block() as block:
                @block.sync
                def _(sp):
                    move(sp, (nxt[:], next_flags.to_broadcast([P, EDGE_PAD])))

                @block.vector
                def _(dve):
                    for i in two:
                        last = dve.memset(attr[i][:], 0.0)
                    link(dve, last)

            with nc.Block() as block:
                @block.gpsimd
                def _(pool):
                    pipeline(pool, n, [(0, lambda st: src_rows.fetch(pool, st))])

                @block.scalar
                def _(act):
                    def hs_out(st):
                        act.wait_ge(*norm.turned.at(st))
                        if st.back(2):
                            act.wait_ge(*freq_done.at(st.back(2)))
                        act.activation(hsc[st.parity][:], psum_a[:], ACT.Copy).then_inc(hsc_done.sem(st), 1)

                    def attr_back(st):
                        act.wait_ge(*attr_turned.at(st))
                        act.activation(attr_c[st.parity][:], psum_a[:], ACT.Copy).then_inc(attr_out.sem(st), 1)

                    def freq_out(st):
                        act.wait_ge(*freq_done.at(st))
                        if st.back(2):
                            act.wait_ge(*multiplied.at(st.back(2)))
                        act.activation(attr_f[st.parity][:], psum_d[:], ACT.Copy).then_inc(attr_freq_out.sem(st), 1)

                    pipeline(act, n, [(1, lambda st: norm.deviation(act, st)), (2, freq_out), (1, lambda st: norm.normalise(act, st)),
                                      (1, hs_out), (1, attr_back)])

                @block.vector
                def _(dve):
                    def multiply(st):
                        i = st.parity
                        dve.wait_ge(*attr_freq_out.at(st))
                        re, im = attr_f[i][:, 0, :], attr_f[i][:, 1, :]
                        dve.tensor_tensor(cross[:, 0, :], psum_c[:, 0, :], im, ALU.mult)
                        dve.tensor_tensor(cross[:, 1, :], psum_c[:, 1, :], re, ALU.mult).then_inc(crossed.sem(st), 1)
                        dve.tensor_tensor(products[i][:, 0, :], psum_c[:, 0, :], re, ALU.mult)
                        dve.tensor_tensor(products[i][:, 1, :], psum_c[:, 1, :], im, ALU.mult)
                        dve.wait_ge(*crossed.at(st))
                        dve.tensor_tensor(products[i][:, 2, :], cross[:, 0, :], cross[:, 1, :], ALU.subtract)\
                           .then_inc(multiplied.sem(st), 1)

                    def mask(st):
                        i = st.parity
                        dve.wait_ge(*g_done.at(st))
                        if st.back(2):
                            dve.wait_ge(*ge_stored.at(st.back(2)))
                        for k in range(H):
                            last = dve.scalar_tensor_tensor(ge[i][:, k, :], nxt[:, bass.ds(st.times(GROUP), GROUP)], 0.0,
                                                            psum_b[:, k, :], ALU.is_equal, ALU.mult)
                        last.then_inc(g_masked.sem(st), 1)
                        dve.wait_ge(*g_masked.at(st))
                        for k in range(H):
                            last = dve.bn_stats(node_stats[:, k, bass.ds(st.times(6, 6 * NODE_GROUPS), 6)], ge[i][:, k, :])
                        last.then_inc(g_counted.sem(st), 1)

                    pipeline(dve, n, [(1, lambda st: norm.moments_of(dve, st)), (1, lambda st: norm.inverse(dve, st)),
                                      (3, mask), (2, multiply), (2, lambda st: sums.scan(dve, st))])
                    dve.wait_ge(*g_counted.at(Step(0, n - 1)))

                @block.tensor
                def _(pe):
                    def turn_attr(st):
                        i = st.parity
                        pe.wait_ge(*attr_landed.at(st))
                        pe.wait_ge(*hsc_done.at(st))
                        for k in range(H):
                            for j in range(TILES):
                                last = pe.transpose(psum_a[:, k, j * P:(j + 1) * P], attr[i][:, j, k * P:(k + 1) * P], ident[:])
                        last.then_inc(attr_turned.sem(st), 1)

                    def transform(st):
                        i = st.parity
                        pe.wait_ge(*attr_out.at(st))
                        if st.back(1):
                            pe.wait_ge(*multiplied.at(st.back(1)))
                        columns_product(pe, psum_c, freq, hsc[i])
                        columns_product(pe, psum_d, freq, attr_c[i]).then_inc(freq_done.sem(st), 1)

                    def from_freq(st):
                        i = st.parity
                        pe.wait_ge(*sums.done.at(st))
                        pe.wait_ge(*h3c_landed.at(st))
                        if st.back(1):
                            pe.wait_ge(*g_masked.at(st.back(1)))
                        for half in range(H):
                            cut = slice(half * P, (half + 1) * P)
                            for k in range(3):
                                pe.matmul(psum_b[:, half, :], w_back[:, k, cut], sums.columns[i][:, k, :], start=k == 0, stop=False)
                            for k in range(H):
                                last = pe.matmul(psum_b[:, half, :], w_self[:, k, cut], h3c[i][:, k, :], start=False, stop=k == H - 1)
                        last.then_inc(g_done.sem(st), 1)

                    pipeline(pe, n, [(2, transform), (1, lambda st: norm.turn(pe, st)), (3, from_freq), (1, turn_attr)])

                @block.sync
                def _(sp):
                    def load(st):
                        i = st.parity
                        if st.back(2):
                            sp.wait_ge(*attr_turned.at(st.back(2)))
                        if isinstance(st.pair, int) and st.offset == n - 1:
                            at = (n - 1) * GROUP
                            whole = (E - at) // P
                            sp.dma_start(attr[i][:, 0:whole, :], edge_attr[at:at + whole * P].rearrange("(j p) d -> p j d", p=P))\
                              .then_inc(attr_landed.sem(st), 16)
                            sp.dma_start(attr[i][0:E - at - whole * P, whole, :], edge_attr[at + whole * P:E]).then_inc(attr_tail, 16)
                            sp.wait_ge(attr_tail, 16)
                        else:
                            sp.dma_start(attr[i][:], attr_groups[st.times(1)]).then_inc(attr_landed.sem(st), 16)

                    def load_h3(st):
                        i = st.parity
                        if st.back(2):
                            sp.wait_ge(*g_done.at(st.back(2)))
                        sp.dma_start(h3c[i][:].rearrange("p k n -> p (k n)"), h3_columns[st.times(1)]).then_inc(h3c_landed.sem(st), 16)

                    def store(st):
                        i = st.parity
                        sp.wait_ge(*g_masked.at(st))
                        sp.dma_start(g_edge_columns[st.times(1)], ge[i][:].rearrange("p k n -> p (k n)")).then_inc(ge_stored.sem(st), 16)

                    attr_groups = edge_groups(edge_attr[0:(n - 1) * GROUP])
                    pipeline(sp, n, [(0, load), (2, load_h3), (3, store)])
                    last_two(sp, ge_stored, n)
            close(n)

        with ExitStack() as own:
            sb = tensors(own)
            total = sb("bn_total", [P, H, 2])
            mean = sb("bn_mean", [P, H])
            square = sb("bn_square", [P, H])
            var = sb("bn_var", [P, H])
            rows = float(NODE_PAD + EDGE_PAD) / N
            with nc.Block() as block:
                @block.vector
                def _(dve):
                    for k in range(H):
                        last = dve.bn_aggr(total[:, k, :], node_stats[:, k, :])
                    link(dve, last)
                    link(dve, dve.tensor_tensor(square[:], total[:, :, 0], total[:, :, 0], ALU.mult))
                    link(dve, dve.tensor_tensor(var[:], total[:, :, 1], square[:], ALU.add))
                    link(dve, dve.tensor_scalar(var[:], var[:], rows, None, ALU.mult))
                    link(dve, dve.tensor_scalar(mean[:], total[:, :, 0], rows, None, ALU.mult))
                    link(dve, dve.tensor_tensor(square[:], mean[:], mean[:], ALU.mult))
                    link(dve, dve.tensor_tensor(var[:], var[:], square[:], ALU.subtract))
                    link(dve, dve.tensor_tensor(mean[:], mean[:], wbias_col[:], ALU.add))

            with nc.Block() as block:
                @block.scalar
                def _(act):
                    link(act, act.activation(var[:], var[:], ACT.Sqrt, bias=eps_bn[:]))

            with nc.Block() as block:
                @block.vector
                def _(dve):
                    link(dve, dve.reciprocal(var[:], var[:]))
                    link(dve, dve.tensor_tensor(bn_scale[:], var[:], gamma_col[:], ALU.mult))
                    link(dve, dve.tensor_tensor(mean[:], wbias_col[:], mean[:], ALU.subtract))
                    link(dve, dve.tensor_tensor(mean[:], mean[:], bn_scale[:], ALU.mult))
                    link(dve, dve.tensor_tensor(bn_shift[:], mean[:], beta_col[:], ALU.add))

        def last_pass(n, columns, load_rows, finish, scatter):
            with ExitStack() as own:
                sb = tensors(own)
                c_landed = signal("c_landed", 16, twin=True)
                r_landed = signal("r_landed", 16, twin=True)
                tanh_done = signal("tanh_done")
                out_turned = signal("out_turned")
                out_done = signal("out_done")
                out_stored = signal("nodes_stored" if not scatter else "out_sent", 16 * TILES if scatter else 16, twin=True)
                last_copied = signal("last_copied")
                c_in = [sb(f"c_in{i}", [P, H, GROUP]) for i in two]
                r_in = [sb(f"r_in{i}", [P, TILES, D]) for i in two]
                act_c = [sb(f"act_c{i}", [P, H, GROUP]) for i in two]
                o_rows = [sb(f"o_rows{i}", [P, TILES, D]) for i in two]
                last_at = [sb(f"last_at{i}", [P, TILES], I32) for i in two]
                psums = [psum_a, psum_b]
                with nc.Block() as block:
                    @block.sync
                    def _(sp):
                        def load(st):
                            i = st.parity
                            if st.back(2):
                                sp.wait_ge(*tanh_done.at(st.back(2)))
                            sp.dma_start(c_in[i][:].rearrange("p k n -> p (k n)"), columns[st.times(1)]).then_inc(c_landed.sem(st), 16)
                            if st.back(2):
                                sp.wait_ge(*out_done.at(st.back(2)))
                            load_rows(sp, st, r_in[i]).then_inc(r_landed.sem(st), 16)

                        pipeline(sp, n, [(0, load)])

                    @block.scalar
                    def _(act):
                        def tanh(st):
                            i = st.parity
                            act.wait_ge(*c_landed.at(st))
                            if st.back(2):
                                act.wait_ge(*out_turned.at(st.back(2)))
                            for k in range(H):
                                last = act.activation(act_c[i][:, k, :], c_in[i][:, k, :], ACT.Tanh,
                                                      bias=bn_shift[:, k:k + 1], scale=bn_scale[:, k:k + 1])
                            last.then_inc(tanh_done.sem(st), 1)

                        pipeline(act, n, [(1, tanh)])

                    @block.tensor
                    def _(pe):
                        def back(st):
                            pe.wait_ge(*tanh_done.at(st))
                            if st.back(2):
                                pe.wait_ge(*out_done.at(st.back(2)))
                            turn_back(pe, psums[st.parity], act_c[st.parity]).then_inc(out_turned.sem(st), 1)

                        pipeline(pe, n, [(1, back)])

                    @block.vector
                    def _(dve):
                        def add(st):
                            i = st.parity
                            dve.wait_ge(*out_turned.at(st))
                            dve.wait_ge(*r_landed.at(st))
                            if st.back(2):
                                dve.wait_ge(*out_stored.at(st.back(2)))
                            dve.tensor_tensor(o_rows[i][:], pair_rows(psums[i]), r_in[i][:], ALU.add).then_inc(out_done.sem(st), 1)

                        pipeline(dve, n, [(2, add)])

                    @block.gpsimd
                    def _(pool):
                        def send(st):
                            i = st.parity
                            if scatter:
                                if st.back(2):
                                    pool.wait_ge(*out_stored.at(st.back(2)))
                                pool.tensor_copy(last_at[i][:], last_col[:, bass.ds(st.times(TILES), TILES)]).then_inc(last_copied.sem(st), 1)
                                pool.wait_ge(*last_copied.at(st))
                            pool.wait_ge(*out_done.at(st))
                            finish(pool, st, o_rows[i], last_at[i], out_stored)

                        pipeline(pool, n, [(2, send)])
                        last_two(pool, out_stored, n)
                if not scatter:
                    used.remove(last_copied)
                close(n)

        def load_nodes(sp, st, to):
            flat = to[:].rearrange("p j d -> p (j d)")
            if isinstance(st.pair, int) and st.offset == NODE_GROUPS - 1:
                return sp.dma_start(flat[0:TAIL_PARTS], tail_group(x3_nodes))
            return sp.dma_start(flat, by_group(x3_nodes)[st.times(1)])

        def store_nodes(pool, st, rows, _, stored):
            flat = rows[:].rearrange("p j d -> p (j d)")
            if isinstance(st.pair, int) and st.offset == NODE_GROUPS - 1:
                pool.dma_start(tail_group(out), flat[0:TAIL_PARTS]).then_inc(stored.sem(st), 16)
            else:
                pool.dma_start(by_group(out)[st.times(1)], flat).then_inc(stored.sem(st), 16)

        def send_edges(pool, st, rows, at, sent):
            pool.sem_inc(pool_turns, 1)
            for j in range(TILES):
                pool.indirect_dma_start(out, bass.IndirectOffsetOnAxis(at[:, j:j + 1], 0), rows[:, j, :], None,
                                        bounds_check=N - 1, oob_is_err=False).then_inc(sent.sem(st), 16)

        last_pass(NODE_GROUPS, g_node_columns, load_nodes, store_nodes, scatter=False)
        last_pass(EDGE_GROUPS, g_edge_columns,
                  lambda sp, st, to: sp.dma_start(to[:], edge_groups(x3_rows)[st.times(1)]), send_edges, scatter=True)


def constants():
    k, i = np.arange(P)[:, None], np.arange(D)[None, :]
    cos, sin = np.cos(2 * np.pi * k * i / D), np.sin(2 * np.pi * k * i / D)
    nyquist = (-1.0) ** i
    imaginary = -sin
    imaginary[0] = nyquist
    to_freq = np.concatenate([cos, imaginary]).T
    by_real = 2 * cos / D
    by_real[0] /= 2
    by_imaginary = 2 * cos / D
    by_imaginary[0] = nyquist / D
    from_freq = np.concatenate([by_real, by_imaginary, -2 * sin / D])
    heads = np.repeat(np.eye(HEADS), D // HEADS, axis=1)
    return {"identity": np.eye(P), "to_freq": to_freq, "from_freq_t": from_freq.T, "head_rows": heads}


def kernel(**inputs):
    from concourse import bacc
    from concourse.bass_utils import run_bass_kernel_spmd

    a = {k: np.asarray(v) for k, v in inputs.items()}
    row = lambda v: v.reshape(1, -1)
    arrays = {
        "x": a["x"], "src": a["src"], "dst": a["dst"], "edge_attr": a["edge_attr_256"], "edge_weight": a["edge_weight"],
        "w_hops": a["L0_gnn_W"], "bias0": row(a["L0_gnn_bias"]), "w_gat": a["L1_gnn_W"].reshape(D, D),
        "att_src": row(a["L1_gnn_att_src"]), "att_dst": row(a["L1_gnn_att_dst"]), "bias1": row(a["L1_gnn_bias"]),
        "w1_t": a["L2_gnn_W1"].T, "b1": row(a["L2_gnn_b1"]), "w2_t": a["L2_gnn_W2"].T, "b2": row(a["L2_gnn_b2"]),
        "w_loop": a["L3_gnn_w_loop"], "w_in": a["L3_gnn_w_in"], "loop_rel": a["L3_gnn_loop_rel"],
        "w_bias": row(a["L3_gnn_w_bias"]), "bn_gamma": row(a["L3_gnn_bn_gamma"]), "bn_beta": row(a["L3_gnn_bn_beta"]),
    }
    arrays |= {k: v.astype(np.float32) for k, v in constants().items()}
    nc = bacc.Bacc("TRN2", target_bir_lowering=False, num_devices=1)
    feed, args = {}, []
    for name, value in arrays.items():
        value = np.ascontiguousarray(value)
        feed[f"in_{name}"] = value
        args.append(nc.dram_tensor(f"in_{name}", value.shape, mybir.dt.from_np(value.dtype), kind="ExternalInput").ap())
    out = nc.dram_tensor("out_rows", (N, D), F32, kind="ExternalOutput").ap()
    gnn_kernel(nc, *args, out)
    result = run_bass_kernel_spmd(nc, [feed], core_ids=[0])
    return result.results[0]["out_rows"]
```

```python
from contextlib import ExitStack

import concourse.bass as bass
import numpy as np
from concourse import mybir
from concourse.alu_op_type import AluOpType as ALU

P = 128
N = 50000
E = 12500
D = 256
H = D // P
HEADS = 8
TILES = 4
GROUP = TILES * P
NODE_GROUPS = -(-N // GROUP)
EDGE_GROUPS = -(-E // GROUP)
NODE_PAD = NODE_GROUPS * GROUP
EDGE_PAD = EDGE_GROUPS * GROUP
EDGE_TILES = EDGE_PAD // P
TAIL_NODES = N - (NODE_GROUPS - 1) * GROUP
TAIL_PARTS = TAIL_NODES // TILES
RING = 4
NO_SLOT = 20000
NO_NODE = 60000
LN_EPS = 1e-5
BN_EPS = 1e-5
SLOPE = 0.2
FAR = 1.0e30

F32 = mybir.dt.float32
BF16 = mybir.dt.bfloat16
I32 = mybir.dt.int32
ACT = mybir.ActivationFunctionType
AX_X = mybir.AxisListType.X


class Step:

    def __init__(self, turn, offset, span=RING):
        self.turn, self.offset, self.span = turn, offset, span
        self.parity = offset % 2

    def times(self, per, plus=0):
        return self.turn * (self.span * per) + (self.offset * per + plus)

    def back(self, k):
        if isinstance(self.turn, int) and self.offset < k:
            return None
        return Step(self.turn, self.offset - k, self.span)


class Signal:

    def __init__(self, nc, ctx, name, per, ring):
        self.per, self.ring = per, ring
        self.sems = [ctx.enter_context(nc.semaphore(f"{name}_{i}")) for i in range(ring)]
        self.base = [0] * ring

    def sem(self, step):
        return self.sems[step.offset % self.ring]

    def at(self, step):
        i = step.offset % self.ring
        return self.sems[i], step.turn * (self.per * step.span // self.ring) + (
            self.base[i] + self.per * (step.offset // self.ring + 1))

    def close(self, n):
        for i in range(self.ring):
            self.base[i] += self.per * len(range(i, n, self.ring))


def pipeline(eng, n, stages, span=RING):
    most = max(lag for lag, _ in stages)
    lead = -(-(most + RING) // span) * span
    turns = (n - lead) // span

    def tick(turn, i):
        for lag, stage in stages:
            if not isinstance(turn, int) or 0 <= i - lag < n:
                stage(Step(turn, i - lag, span))

    for i in range(lead):
        tick(0, i)
    turns -= lead + turns * span == n
    with eng.Fori(0, turns) as q:
        for i in range(span):
            tick(q, lead + i)
    for i in range(lead + span * turns, n + most):
        tick(0, i)


def gnn_kernel(nc, x, src, dst, edge_attr, edge_weight, w_hops, bias0, w_gat, att_src, att_dst, bias1,
               w1_t, b1, w2_t, b2, w_loop, w_in, loop_rel, w_bias, bn_gamma, bn_beta,
               identity, to_freq, from_freq_t, head_rows, out):
    def dram(name, shape, dt=F32):
        return nc.dram_tensor(name, shape, dt).ap()

    slot_of_node = dram("slot_of_node", (NODE_PAD, 1), I32)
    same_flags = dram("same_flags", (1, EDGE_PAD), BF16)
    next_flags = dram("next_flags", (1, EDGE_PAD), BF16)
    rel_twice = dram("rel_twice", (1, 2 * D))
    row_cuts = dram("row_cuts", (3, D), BF16)
    xs_rows = dram("xs_rows", (EDGE_PAD, D))
    xd_rows = dram("xd_rows", (EDGE_PAD, D))
    xs_gat = dram("xs_gat", (EDGE_PAD, D))
    xs_lone = dram("xs_lone", (EDGE_PAD, D))
    hop1_rows = dram("hop1_rows", (EDGE_PAD, D))
    x1_part = dram("x1_part", (EDGE_PAD, D))
    x1_rows = dram("x1_rows", (EDGE_PAD, D))
    x2_rows = dram("x2_rows", (EDGE_PAD, D))
    x3_rows = dram("x3_rows", (EDGE_PAD, D))
    gat_columns = dram("gat_columns", (EDGE_GROUPS, P, H * GROUP))
    h2_columns = dram("h2_columns", (EDGE_GROUPS, P, H * GROUP))
    h3_columns = dram("h3_columns", (EDGE_GROUPS, P, H * GROUP))
    g_edge_columns = dram("g_edge_columns", (EDGE_GROUPS, P, H * GROUP))
    score_dst = dram("score_dst", (HEADS, EDGE_PAD))
    score_src = dram("score_src", (HEADS, EDGE_PAD))
    exp_rows = dram("exp_rows", (HEADS, EDGE_PAD))
    inv_rows = dram("inv_rows", (HEADS, EDGE_PAD))
    norm_row = dram("norm_row", (EDGE_TILES, P))
    x3_nodes = dram("x3_nodes", (N, D))
    g_node_columns = dram("g_node_columns", (NODE_GROUPS, P, H * GROUP))

    def by_group(rows):
        full = NODE_GROUPS - 1
        return rows[0:full * GROUP].rearrange("(g p j) d -> g p (j d)", p=P, j=TILES)

    def tail_group(rows):
        at = (NODE_GROUPS - 1) * GROUP
        return rows[at:at + TAIL_NODES].rearrange("(p j) d -> p (j d)", j=TILES)

    def edge_tiles(rows):
        return rows.rearrange("(t p) d -> t p d", p=P)

    def edge_groups(rows):
        return rows.rearrange("(g j p) d -> g p j d", p=P, j=TILES)

    ctx = ExitStack()
    with ctx:
        signals = {}
        chain = ctx.enter_context(nc.semaphore("setup_chain"))
        loads = ctx.enter_context(nc.semaphore("setup_loads"))
        pool_turns = ctx.enter_context(nc.semaphore("pool_turns"))
        softmax_step = ctx.enter_context(nc.semaphore("softmax_step"))
        attr_tail = ctx.enter_context(nc.semaphore("attr_tail"))
        count = {"chain": 0, "loads": 0, "phase": 0}

        def link(eng, ins):
            count["chain"] += 1
            ins.then_inc(chain, 1)
            eng.wait_ge(chain, count["chain"])

        def move(eng, *pairs):
            for to, of in pairs:
                eng.dma_start(to, of).then_inc(loads, 16)
                count["loads"] += 16
            eng.wait_ge(loads, count["loads"])

        def tensors(stack):
            count["phase"] += 1
            phase = count["phase"]

            def sb(name, shape, dt=F32):
                return stack.enter_context(nc.sbuf_tensor(f"{name}_p{phase}", shape, dt))
            return sb

        sb = tensors(ctx)
        psum_a = ctx.enter_context(nc.psum_tensor("psum_a", [P, H, GROUP], F32))
        psum_b = ctx.enter_context(nc.psum_tensor("psum_b", [P, H, GROUP], F32))
        psum_c = ctx.enter_context(nc.psum_tensor("psum_c", [P, H, GROUP], F32))
        psum_d = ctx.enter_context(nc.psum_tensor("psum_d", [P, H, GROUP], F32))

        ident = sb("ident", [P, P])
        eps_ln = sb("eps_ln", [P, 1])
        eps_bn = sb("eps_bn", [P, 1])
        src_col = sb("src_col", [P, EDGE_TILES], I32)
        dst_col = sb("dst_col", [P, EDGE_TILES], I32)
        last_col = sb("last_col", [P, EDGE_TILES], I32)
        slot_col = sb("slot_col", [P, EDGE_TILES], I32)
        src_slot = sb("src_slot", [P, EDGE_TILES], I32)
        weight_col = sb("weight_col", [P, EDGE_TILES])
        norm_col = sb("norm_col", [P, EDGE_TILES])
        lone = sb("lone", [P, NODE_GROUPS * TILES])
        same = sb("same", [P, EDGE_PAD], BF16)
        w_hop0 = sb("w_hop0", [P, H, D])
        w_hop1 = sb("w_hop1", [P, H, D])
        gat_w = sb("gat_w", [P, H, D])
        gat_vs = sb("gat_vs", [P, H, HEADS])
        gat_vd = sb("gat_vd", [P, H, HEADS])
        head_sel = sb("head_sel", [HEADS, D])
        w1 = sb("w1", [P, H, D])
        w2 = sb("w2", [P, H, D])
        w_back = sb("w_back", [P, 3, D])
        w_self = sb("w_self", [P, H, D])
        freq = sb("freq", [P, H, D])
        bias0_row = sb("bias0_row", [P, D])
        lone_row = sb("lone_row", [P, D])
        bias1_col = sb("bias1_col", [P, H])
        bias_cuts = sb("bias_cuts", [3, 2 * D], BF16)
        ones_cuts = sb("ones_cuts", [3, P], BF16)
        wbias_col = sb("wbias_col", [P, H])
        gamma_col = sb("gamma_col", [P, H])
        beta_col = sb("beta_col", [P, H])
        node_stats = sb("node_stats", [P, H, (NODE_GROUPS + EDGE_GROUPS) * 6])
        bn_scale = sb("bn_scale", [P, H])
        bn_shift = sb("bn_shift", [P, H])

        with ExitStack() as own:
            sb = tensors(own)
            dst_i, next_i, prev_i, src_i = (sb(n, [EDGE_TILES, P], I32) for n in ("dst_i", "next_i", "prev_i", "src_i"))
            dst_f, next_f, prev_f, src_f, w_f, near_f, last_f = (
                sb(n, [EDGE_TILES, P]) for n in ("dst_f", "next_f", "prev_f", "src_f", "w_f", "near_f", "last_f"))
            same_b = sb("same_b", [EDGE_TILES, P], BF16)
            next_b = sb("next_b", [EDGE_TILES, P], BF16)
            fill = sb("fill", [P, NODE_PAD // P], I32)
            zero_i = sb("zero_i", [1, NODE_PAD - N], I32)
            node_slot = sb("node_slot", [P, NODE_GROUPS * TILES], I32)
            node_slot_f = sb("node_slot_f", [P, NODE_GROUPS * TILES])
            index4 = [sb(f"index4_{b}", [P, TILES], I32) for b in range(2)]
            value4 = [sb(f"value4_{b}", [P, TILES], I32) for b in range(2)]
            att_s = sb("att_s", [P, D])
            att_d = sb("att_d", [P, D])
            prod = sb("prod", [P, D])
            circ = sb("circ", [P, H, D])
            loop_w = sb("loop_w", [P, H, D])
            in_w = sb("in_w", [P, H, D])
            back_t = sb("back_t", [P, H, 3 * P])
            b_row = sb("b_row", [1, 2, D])
            b_rest = sb("b_rest", [1, D])
            b_cut = sb("b_cut", [1, 3, D], BF16)
            b_wide = sb("b_wide", [1, D])
            ones_row = sb("ones_row", [1, P])
            bias1_row = sb("bias1_row", [P, D])
            full = E // P
            rest = E - full * P

            with nc.Block() as block:
                @block.vector
                def _(dve):
                    dve.memset(eps_ln[:], LN_EPS)
                    dve.memset(eps_bn[:], BN_EPS)
                    dve.memset(ones_cuts[:], 1.0)
                    dve.memset(dst_i[:], NO_NODE)
                    dve.memset(next_i[:], NO_NODE)
                    dve.memset(prev_i[:], NO_NODE)
                    dve.memset(src_i[:], 0)
                    dve.memset(w_f[:], 0.0)
                    dve.memset(fill[:], NO_SLOT)
                    link(dve, dve.memset(zero_i[:], 0))

                @block.gpsimd
                def _(pool):
                    pool.iota(slot_col[:], [[P, EDGE_TILES]], base=0, channel_multiplier=1)

            with nc.Block() as block:
                @block.sync
                def _(sp):
                    def edge_rows(to, of):
                        return ((to[0:full, :], of[0:full * P].rearrange("(t p) -> t p", p=P)),
                                (to[full:full + 1, 0:rest], of[full * P:E].rearrange("(t p) -> t p", t=1)))

                    move(sp, (ident[:], identity),
                         *edge_rows(dst_i, dst), *edge_rows(src_i, src), *edge_rows(w_f, edge_weight),
                         (next_i[0:full, :], dst[1:full * P + 1].rearrange("(t p) -> t p", p=P)),
                         (next_i[full:full + 1, 0:rest - 1], dst[full * P + 1:E].rearrange("(t p) -> t p", t=1)),
                         (prev_i[0:1, 1:P], dst[0:P - 1].rearrange("(t p) -> t p", t=1)),
                         (prev_i[1:full, :], dst[P - 1:full * P - 1].rearrange("(t p) -> t p", p=P)),
                         (prev_i[full:full + 1, 0:rest], dst[full * P - 1:E - 1].rearrange("(t p) -> t p", t=1)),
                         (slot_of_node.rearrange("(p q) o -> p (q o)", p=P), fill[:]),
                         (xs_rows[NODE_GROUPS * P:EDGE_PAD], x[0:EDGE_PAD - NODE_GROUPS * P]),
                         (xd_rows[NODE_GROUPS * P:EDGE_PAD], x[0:EDGE_PAD - NODE_GROUPS * P]),
                         (rel_twice[:, 0:D], loop_rel), (rel_twice[:, D:2 * D], loop_rel),
                         *((to[:], of.rearrange("(k p) n -> p k n", p=P)) for to, of in (
                             (w_hop0, w_hops[0]), (w_hop1, w_hops[1]), (gat_w, w_gat), (w1, w1_t), (w2, w2_t),
                             (freq, to_freq), (loop_w, w_loop), (in_w, w_in), (back_t, from_freq_t))),
                         (head_sel[:], head_rows),
                         (b_row[:, 0, :], b1), (b_row[:, 1, :], b2),
                         *((to[:], of.to_broadcast([P, D])) for to, of in (
                             (att_s, att_src), (att_d, att_dst), (bias0_row, bias0), (bias1_row, bias1))))

                @block.scalar
                def _(act):
                    with nc.allow_non_contiguous_dma(reason="one value per partition"):
                        for to, of in ((bias1_col, bias1), (wbias_col, w_bias), (gamma_col, bn_gamma), (beta_col, bn_beta)):
                            act.dma_start(to[:], of.rearrange("o (k p) -> p (o k)", p=P)).then_inc(chain, 16)
                            count["chain"] += 16
                    act.wait_ge(chain, count["chain"])

            with nc.Block() as block:
                @block.sync
                def _(sp):
                    move(sp, (slot_of_node[N:NODE_PAD].rearrange("(o q) i -> o (q i)", o=1), zero_i[:]),
                         *((circ[:, k, :], bass.AP(rel_twice.tensor, k * P, [[1, P], [1, D]])) for k in range(H)))

                @block.vector
                def _(dve):
                    dve.tensor_copy(dst_f[:], dst_i[:])
                    dve.tensor_copy(next_f[:], next_i[:])
                    dve.tensor_copy(prev_f[:], prev_i[:])
                    link(dve, dve.tensor_copy(src_f[:], src_i[:]))
                    dve.tensor_tensor(same_b[:], dst_f[:], prev_f[:], ALU.is_equal)
                    dve.tensor_tensor(next_b[:], dst_f[:], next_f[:], ALU.is_equal)
                    link(dve, dve.tensor_scalar(near_f[:], dst_f[:], float(N - 1), None, ALU.min))
                    link(dve, dve.scalar_tensor_tensor(last_f[:], next_b[:], float(NO_NODE), dst_f[:], ALU.mult, ALU.add))
                    for att, v in ((att_s, gat_vs), (att_d, gat_vd)):
                        for k in range(H):
                            link(dve, dve.tensor_tensor(prod[:], gat_w[:, k, :], att[:], ALU.mult))
                            link(dve, dve.tensor_reduce(v[:, k, :], prod[:].rearrange("p (h d) -> p h d", h=HEADS), AX_X, ALU.add))
                    link(dve, dve.tensor_scalar(prod[:], bias1_row[:], 0.0, None, ALU.max))
                    link(dve, dve.tensor_tensor(lone_row[:], prod[:], bias0_row[:], ALU.add))
                    link(dve, dve.tensor_tensor(b_rest[:], b_row[:, 0, :], b_row[:, 1, :], ALU.add))
                    for cut in range(3):
                        link(dve, dve.tensor_copy(b_cut[:, cut, :], b_rest[:]))
                        link(dve, dve.tensor_copy(b_wide[:], b_cut[:, cut, :]))
                        link(dve, dve.tensor_tensor(b_rest[:], b_rest[:], b_wide[:], ALU.subtract))

            with nc.Block() as block:
                @block.tensor
                def _(pe):
                    for i, rows in enumerate((src_f, near_f, last_f, w_f)):
                        pe.transpose(psum_a[:, 0, i * P:i * P + EDGE_TILES], rows[:], ident[0:EDGE_TILES, 0:EDGE_TILES])
                    for half in range(H):
                        for k in range(H):
                            pe.matmul(psum_b[:, half, 0:D], circ[:, k, half * P:(half + 1) * P], loop_w[:, k, :],
                                      start=k == 0, stop=k == H - 1)
                    for part in range(3):
                        for k in range(H):
                            last = pe.matmul((psum_c if part < 2 else psum_d)[:, part % 2, 0:D],
                                             back_t[:, k, part * P:(part + 1) * P], in_w[:, k, :],
                                             start=k == 0, stop=k == H - 1)
                    link(pe, last)

                @block.sync
                def _(sp):
                    move(sp, (same_flags.rearrange("o (t p) -> (o t) p", p=P), same_b[:]),
                         (next_flags.rearrange("o (t p) -> (o t) p", p=P), next_b[:]),
                         (row_cuts.rearrange("(o c) d -> o c d", o=1), b_cut[:]))

            with nc.Block() as block:
                @block.vector
                def _(dve):
                    for i, to in enumerate((src_col, dst_col, last_col, weight_col)):
                        dve.tensor_copy(to[:], psum_a[:, 0, i * P:i * P + EDGE_TILES])
                    for half in range(H):
                        dve.tensor_copy(w_self[:, half, :], psum_b[:, half, 0:D])
                    for part in range(3):
                        last = dve.tensor_copy(w_back[:, part, :], (psum_c if part < 2 else psum_d)[:, part % 2, 0:D])
                    link(dve, last)

                @block.sync
                def _(sp):
                    move(sp, (same[:], same_flags.to_broadcast([P, EDGE_PAD])),
                         (bias_cuts[:, 0:D], row_cuts), (bias_cuts[:, D:2 * D], row_cuts))

            def signal(name, per=1, ring=1):
                if name not in signals:
                    signals[name] = Signal(nc, ctx, name, per, ring)
                assert (signals[name].per, signals[name].ring) == (per, ring), name
                used.append(signals[name])
                return signals[name]

            def close(n):
                for s in used:
                    s.close(n)
                used.clear()

            used = []
            slots_sent = signal("slots_sent", 16 * TILES, ring=2)
            index_copied = signal("index_copied", 2)
            with nc.Block() as block:
                @block.gpsimd
                def _(pool):
                    def scatter(st):
                        b = st.parity
                        if st.back(2):
                            pool.wait_ge(*slots_sent.at(st.back(2)))
                        pool.tensor_copy(index4[b][:], last_col[:, bass.ds(st.times(TILES), TILES)]).then_inc(index_copied.sem(st), 1)
                        pool.tensor_copy(value4[b][:], slot_col[:, bass.ds(st.times(TILES), TILES)]).then_inc(index_copied.sem(st), 1)
                        pool.wait_ge(*index_copied.at(st))
                        pool.sem_inc(pool_turns, 1)
                        for j in range(TILES):
                            pool.indirect_dma_start(
                                slot_of_node, bass.IndirectOffsetOnAxis(index4[b][:, j:j + 1], 0), value4[b][:, j:j + 1], None,
                                bounds_check=N - 1, oob_is_err=False).then_inc(slots_sent.sem(st), 16)

                    pipeline(pool, EDGE_GROUPS, [(0, scatter)])
                    pool.wait_ge(*slots_sent.at(Step(0, EDGE_GROUPS - 1)))
                    pool.wait_ge(*slots_sent.at(Step(0, EDGE_GROUPS - 2)))

            with nc.Block() as block:
                @block.vector
                def _(dve):
                    link(dve, dve.memset(src_slot[:], NO_SLOT))

                @block.sync
                def _(sp):
                    move(sp, (node_slot[:].rearrange("p (g j) -> p g j", j=TILES),
                              slot_of_node.rearrange("(g p j) o -> p g (j o)", p=P, j=TILES)))
            close(EDGE_GROUPS)

            with nc.Block() as block:
                @block.vector
                def _(dve):
                    link(dve, dve.tensor_copy(node_slot_f[:], node_slot[:]))
                    link(dve, dve.tensor_scalar(lone[:], node_slot_f[:], float(NO_SLOT), None, ALU.is_equal))

        class Norm:

            def __init__(self, sb, name, rows, rows_ready, psum, taken, scale=None, weight=None):
                self.rows, self.rows_ready, self.psum, self.taken = rows, rows_ready, psum, taken
                self.scale, self.weight = scale, weight
                two = range(2)
                self.stats = [sb(f"{name}_stats{b}", [P, TILES, 6]) for b in two]
                self.mean2 = [sb(f"{name}_mean2_{b}", [P, TILES]) for b in two]
                self.apart = [sb(f"{name}_apart{b}", [P, TILES]) for b in two]
                self.var = [sb(f"{name}_var{b}", [P, TILES]) for b in two]
                self.dev = [sb(f"{name}_dev{b}", [P, TILES]) for b in two]
                self.inv = [sb(f"{name}_inv{b}", [P, TILES]) for b in two]
                self.off = [sb(f"{name}_off{b}", [P, TILES]) for b in two]
                self.h = [sb(f"{name}_h{b}", [P, TILES, D]) for b in two]
                self.pair_done = signal(f"{name}_pair_done", 3)
                self.moments_done = signal(f"{name}_moments_done")
                self.dev_done = signal(f"{name}_dev_done")
                self.inv_done = signal(f"{name}_scaled_inv_done", 3) if scale else signal(f"{name}_inv_done", 2)
                self.h_done = signal(f"{name}_h_done")
                if weight:
                    self.weighted = signal(f"{name}_weighted")
                self.turned = signal(f"{name}_turned")

            def moments_of(self, dve, st):
                b = st.parity
                dve.wait_ge(*self.rows_ready.at(st))
                for j in range(TILES):
                    last = dve.bn_stats(self.stats[b][:, j, :], self.rows[st.offset % len(self.rows)][:, j, :])
                sem, value = self.pair_done.at(st)
                last.then_inc(sem, 1)
                dve.wait_ge(sem, value - 2)
                even, odd = self.stats[b][:, :, 0:3], self.stats[b][:, :, 3:6]
                dve.tensor_tensor(self.apart[b][:], even[:, :, 1], odd[:, :, 1], ALU.subtract)
                dve.tensor_tensor(self.mean2[b][:], even[:, :, 1], odd[:, :, 1], ALU.add)
                dve.tensor_tensor(self.var[b][:], even[:, :, 2], odd[:, :, 2], ALU.add).then_inc(sem, 1)
                dve.wait_ge(sem, value - 1)
                dve.scalar_tensor_tensor(self.apart[b][:], self.apart[b][:], D / 4.0, self.apart[b][:], ALU.mult, ALU.mult)\
                   .then_inc(sem, 1)
                dve.wait_ge(sem, value)
                dve.tensor_tensor(self.var[b][:], self.var[b][:], self.apart[b][:], ALU.add).then_inc(self.moments_done.sem(st), 1)

            def deviation(self, act, st):
                b = st.parity
                act.wait_ge(*self.moments_done.at(st))
                act.activation(self.dev[b][:], self.var[b][:], ACT.Sqrt, bias=eps_ln[:], scale=1.0 / D).then_inc(self.dev_done.sem(st), 1)

            def inverse(self, dve, st):
                b, done = st.parity, self.inv_done
                sem, value = done.at(st)
                dve.wait_ge(*self.dev_done.at(st))
                if st.back(2):
                    dve.wait_ge(*self.h_done.at(st.back(2)))
                dve.reciprocal(self.inv[b][:], self.dev[b][:]).then_inc(sem, 1)
                dve.wait_ge(sem, value - done.per + 1)
                if self.scale:
                    dve.tensor_tensor(self.inv[b][:], self.inv[b][:], self.scale(st), ALU.mult).then_inc(sem, 1)
                    dve.wait_ge(sem, value - 1)
                dve.scalar_tensor_tensor(self.off[b][:], self.mean2[b][:], -0.5, self.inv[b][:], ALU.mult, ALU.mult)\
                   .then_inc(sem, 1)

            def normalise(self, dve, st):
                b = st.parity
                dve.wait_ge(*self.inv_done.at(st))
                if st.back(2):
                    dve.wait_ge(*self.turned.at(st.back(2)))
                rows = self.rows[st.offset % len(self.rows)]
                for j in range(TILES):
                    last = dve.tensor_scalar(self.h[b][:, j, :], rows[:, j, :], self.inv[b][:, j:j + 1],
                                             self.off[b][:, j:j + 1], ALU.mult, ALU.add)
                last.then_inc(self.h_done.sem(st), 1)

            def normalise_relu(self, act, st):
                b = st.parity
                act.wait_ge(*self.inv_done.at(st))
                if st.back(2):
                    act.wait_ge(*self.turned.at(st.back(2)))
                for j in range(TILES):
                    last = act.activation(self.h[b][:, j, :], self.rows[st.offset % len(self.rows)][:, j, :], ACT.Relu,
                                          bias=self.off[b][:, j:j + 1], scale=self.inv[b][:, j:j + 1])
                last.then_inc(self.h_done.sem(st), 1)

            def weigh(self, dve, st):
                b = st.parity
                dve.wait_ge(*self.h_done.at(st))
                w = self.weight(st)
                for j in range(TILES):
                    last = dve.tensor_scalar(self.h[b][:, j, :], self.h[b][:, j, :], w(j), None, ALU.mult)
                last.then_inc(self.weighted.sem(st), 1)

            def turn(self, pe, st):
                b = st.parity
                pe.wait_ge(*(self.weighted if self.weight else self.h_done).at(st))
                if st.back(1):
                    pe.wait_ge(*self.taken.at(st.back(1)))
                for k in range(H):
                    for j in range(TILES):
                        last = pe.transpose(self.psum[:, k, j * P:(j + 1) * P], self.h[b][:, j, k * P:(k + 1) * P], ident[:])
                last.then_inc(self.turned.sem(st), 1)

        def rows_product(pe, to, columns, weights, start=True, stop=True):
            for j in range(TILES):
                for k in range(H):
                    last = pe.matmul(to[:, j // 2, (j % 2) * D:(j % 2 + 1) * D], columns[:, k, j * P:(j + 1) * P],
                                     weights[:, k, :], start=start and k == 0, stop=stop and k == H - 1,
                                     skip_group_check=True)
            return last

        def columns_product(pe, to, weights, columns, start=True, stop=True):
            parts = columns.shape[1]
            for half in range(H):
                for k in range(parts):
                    last = pe.matmul(to[:, half, :], weights[:, k, half * P:(half + 1) * P], columns[:, k, :],
                                     start=start and k == 0, stop=stop and k == parts - 1, skip_group_check=True)
            return last

        def last_two(eng, sig, n):
            eng.wait_ge(*sig.at(Step(0, n - 2)))
            eng.wait_ge(*sig.at(Step(0, n - 1)))

        def tile_rows(t):
            return t[:].rearrange("p (j d) -> p j d", j=TILES)

        def pair_rows(psum):
            return psum[:].rearrange("p h (j d) -> p (h j) d", j=2)

        class Tail:

            def __init__(self, sb, product_done, base, base_ready, out_free):
                two = range(2)
                self.product_done, self.base, self.base_ready, self.out_free = product_done, base, base_ready, out_free
                self.leaky = [sb(f"tail_leaky{b}", [P, TILES, D]) for b in two]
                self.square = [sb(f"tail_square{b}", [P, TILES, D]) for b in two]
                self.total = [sb(f"tail_total{b}", [P, TILES]) for b in two]
                self.length = [sb(f"tail_length{b}", [P, TILES]) for b in two]
                self.inv = [sb(f"tail_inv{b}", [P, TILES]) for b in two]
                self.x3 = [sb(f"tail_x3{b}", [P, TILES, D]) for b in two]
                self.slope_done = signal("tail_slope_done")
                self.leaky_done = signal("tail_leaky_done")
                self.length_done = signal("tail_length_done", 2)
                self.inv_done = signal("tail_inv_done", 2)
                self.x3_done = signal("tail_x3_done")

            def slope(self, act, st):
                b = st.parity
                act.wait_ge(*self.product_done.at(st))
                if st.back(2):
                    act.wait_ge(*self.x3_done.at(st.back(2)))
                act.activation(self.leaky[b][:], pair_rows(psum_b), ACT.Copy, scale=SLOPE).then_inc(self.slope_done.sem(st), 1)

            def leak(self, dve, st):
                b = st.parity
                dve.wait_ge(*self.slope_done.at(st))
                dve.tensor_tensor(self.leaky[b][:], pair_rows(psum_b), self.leaky[b][:], ALU.max).then_inc(self.leaky_done.sem(st), 1)

            def square_up(self, act, st):
                b = st.parity
                act.wait_ge(*self.leaky_done.at(st))
                sem, value = self.length_done.at(st)
                for j in range(TILES):
                    last = act.activation(self.square[b][:, j, :], self.leaky[b][:, j, :], ACT.Square, accum_out=self.total[b][:, j:j + 1])
                last.then_inc(sem, 1)
                act.wait_ge(sem, value - 1)
                act.activation(self.length[b][:], self.total[b][:], ACT.Sqrt).then_inc(sem, 1)

            def inverse(self, dve, st):
                b = st.parity
                dve.wait_ge(*self.length_done.at(st))
                sem, value = self.inv_done.at(st)
                if st.back(2):
                    dve.wait_ge(*self.x3_done.at(st.back(2)))
                dve.tensor_scalar(self.inv[b][:], self.length[b][:], 1e-12, None, ALU.max).then_inc(sem, 1)
                dve.wait_ge(sem, value - 1)
                dve.reciprocal(self.inv[b][:], self.inv[b][:]).then_inc(sem, 1)

            def residual(self, dve, st):
                b = st.parity
                dve.wait_ge(*self.inv_done.at(st))
                if self.base_ready:
                    dve.wait_ge(*self.base_ready.at(st))
                for sig in self.out_free:
                    if st.back(2):
                        dve.wait_ge(*sig.at(st.back(2)))
                for j in range(TILES):
                    last = dve.scalar_tensor_tensor(self.x3[b][:, j, :], self.leaky[b][:, j, :], self.inv[b][:, j:j + 1],
                                                    self.base[b][:, j, :], ALU.mult, ALU.add)
                last.then_inc(self.x3_done.sem(st), 1)

        with ExitStack() as own:
            sb = tensors(own)
            two = range(2)
            n = NODE_GROUPS
            x_in = [sb(f"x_in{b}", [P, TILES * D]) for b in two]
            x2 = [sb(f"x2_{b}", [P, TILES, D]) for b in range(RING)]
            h2c = [sb(f"h2c{b}", [P, H, GROUP]) for b in two]
            h3c = [sb(f"h3c{b}", [P, H, GROUP]) for b in two]
            gc = [sb(f"gc{b}", [P, H, GROUP]) for b in two]
            x_landed = signal("x_landed", 16, ring=2)
            x2_done = signal("x2_done")
            h2c_done = signal("h2c_done")
            y_done = signal("y_done")
            x3_stored = signal("x3_stored", 16, ring=2)
            h3c_done = signal("h3c_done")
            g_done = signal("g_done")
            g_stats = signal("g_stats")
            gc_done = signal("gc_done")
            g_stored = signal("g_stored", 16, ring=2)
            norm2 = Norm(sb, "norm", x2, x2_done, psum_a, h2c_done)
            norm3 = Norm(sb, "norm3", None, None, psum_c, h3c_done,
                         scale=lambda st: lone[:, bass.ds(st.times(TILES), TILES)])
            tail = Tail(sb, y_done, x2, None, [x3_stored, norm3.h_done])
            scaled = signal("scaled")
            norm3.rows, norm3.rows_ready = tail.x3, tail.x3_done

            x_groups, x3_groups = by_group(x), by_group(x3_nodes)
            edges_copied = signal("edges_copied", 2)
            edges_fetched = signal("edges_fetched", 48, ring=RING)
            edges_stored = signal("edges_stored", 32, ring=RING)
            slot_kept = signal("slot_kept")
            src_at, dst_at, slot_of = ([sb(f"{name}{b}", [P, 1], I32) for b in range(RING)] for name in ("src_at", "dst_at", "slot_of"))
            x_src, x_dst = ([sb(f"{name}{b}", [P, D]) for b in range(RING)] for name in ("x_src", "x_dst"))

            with nc.Block() as block:
                @block.sync
                def _(sp):
                    def load(st):
                        if st.back(2):
                            sp.wait_ge(*x2_done.at(st.back(2)))
                        if isinstance(st.turn, int) and st.offset == n - 1:
                            sp.dma_start(x_in[st.parity][0:TAIL_PARTS, :], tail_group(x)).then_inc(x_landed.sem(st), 16)
                        else:
                            sp.dma_start(x_in[st.parity][:], x_groups[st.times(1)]).then_inc(x_landed.sem(st), 16)

                    def store_edges(st):
                        b = st.offset % RING
                        sp.wait_ge(*edges_fetched.at(st))
                        sp.dma_start(edge_tiles(xs_rows)[st.times(1)], x_src[b][:]).then_inc(edges_stored.sem(st), 16)
                        sp.dma_start(edge_tiles(xd_rows)[st.times(1)], x_dst[b][:]).then_inc(edges_stored.sem(st), 16)

                    def store_x3(st):
                        sp.wait_ge(*tail.x3_done.at(st))
                        rows = tail.x3[st.parity][:].rearrange("p j d -> p (j d)")
                        if isinstance(st.turn, int) and st.offset == n - 1:
                            sp.dma_start(tail_group(x3_nodes), rows[0:TAIL_PARTS]).then_inc(x3_stored.sem(st), 16)
                        else:
                            sp.dma_start(x3_groups[st.times(1)], rows).then_inc(x3_stored.sem(st), 16)

                    def store_g(st):
                        sp.wait_ge(*gc_done.at(st))
                        sp.dma_start(g_node_columns[st.times(1)], gc[st.parity][:].rearrange("p k n -> p (k n)"))\
                          .then_inc(g_stored.sem(st), 16)

                    pipeline(sp, n, [(0, load), (6, store_x3), (2, store_edges), (10, store_g)])
                    last_two(sp, x3_stored, n)
                    last_two(sp, g_stored, n)
                    for i in range(RING):
                        sp.wait_ge(*edges_stored.at(Step(0, n - 1 - i)))

                @block.gpsimd
                def _(pool):
                    def add(st):
                        pool.wait_ge(*x_landed.at(st))
                        if st.back(RING):
                            pool.wait_ge(*tail.x3_done.at(st.back(RING)))
                        pool.tensor_tensor(x2[st.offset % RING][:], tile_rows(x_in[st.parity]), lone_row[:].unsqueeze(1).to_broadcast([P, TILES, D]), ALU.add)\
                            .then_inc(x2_done.sem(st), 1)

                    def residual(st):
                        b = st.parity
                        pool.wait_ge(*scaled.at(st))
                        if st.back(2):
                            pool.wait_ge(*x3_stored.at(st.back(2)))
                            pool.wait_ge(*norm3.h_done.at(st.back(2)))
                        pool.tensor_tensor(tail.x3[b][:], tail.leaky[b][:], x2[st.offset % RING][:], ALU.add)\
                            .then_inc(tail.x3_done.sem(st), 1)

                    def fetch_edges(st):
                        b = st.offset % RING
                        if st.back(RING):
                            pool.wait_ge(*edges_stored.at(st.back(RING)))
                            pool.wait_ge(*slot_kept.at(st.back(RING)))
                        pool.tensor_copy(src_at[b][:], src_col[:, bass.ds(st.times(1), 1)]).then_inc(edges_copied.sem(st), 1)
                        pool.tensor_copy(dst_at[b][:], dst_col[:, bass.ds(st.times(1), 1)]).then_inc(edges_copied.sem(st), 1)
                        pool.wait_ge(*edges_copied.at(st))
                        pool.sem_inc(pool_turns, 1)
                        for to, at, table in ((x_src[b], src_at[b], x), (x_dst[b], dst_at[b], x), (slot_of[b], src_at[b], slot_of_node)):
                            pool.indirect_dma_start(to[:], None, table, bass.IndirectOffsetOnAxis(at[:], 0),
                                                    bounds_check=N - 1, oob_is_err=False).then_inc(edges_fetched.sem(st), 16)

                    pipeline(pool, n, [(0, fetch_edges), (5, residual), (1, add)])

                @block.scalar
                def _(act):
                    def h2_out(st):
                        act.wait_ge(*norm2.turned.at(st))
                        if st.back(2):
                            act.wait_ge(*y_done.at(st.back(2)))
                        act.activation(h2c[st.parity][:], psum_a[:], ACT.Relu).then_inc(h2c_done.sem(st), 1)

                    def g_out(st):
                        act.wait_ge(*g_done.at(st))
                        if st.back(2):
                            act.wait_ge(*g_stored.at(st.back(2)))
                            act.wait_ge(*g_stats.at(st.back(2)))
                        act.activation(gc[st.parity][:], psum_d[:], ACT.Copy).then_inc(gc_done.sem(st), 1)

                    def h3_out(st):
                        act.wait_ge(*norm3.turned.at(st))
                        if st.back(2):
                            act.wait_ge(*g_done.at(st.back(2)))
                        act.activation(h3c[st.parity][:], psum_c[:], ACT.Relu).then_inc(h3c_done.sem(st), 1)

                    def shorten(st):
                        b = st.parity
                        act.wait_ge(*tail.inv_done.at(st))
                        for j in range(TILES):
                            last = act.activation(tail.leaky[b][:, j, :], tail.leaky[b][:, j, :], ACT.Copy,
                                                  scale=tail.inv[b][:, j:j + 1])
                        last.then_inc(scaled.sem(st), 1)

                    pipeline(act, n, [(9, g_out), (8, h3_out), (5, shorten),
                                      (2, lambda st: norm2.deviation(act, st)),
                                      (3, h2_out),
                                      (4, lambda st: tail.slope(act, st)),
                                      (6, lambda st: norm3.deviation(act, st)),
                                      (4, lambda st: tail.square_up(act, st))])

                @block.vector
                def _(dve):
                    def stats(st):
                        dve.wait_ge(*gc_done.at(st))
                        for k in range(H):
                            last = dve.bn_stats(node_stats[:, k, bass.ds(st.times(6), 6)], gc[st.parity][:, k, :])
                        last.then_inc(g_stats.sem(st), 1)

                    def keep_slots(st):
                        dve.wait_ge(*edges_fetched.at(st))
                        dve.tensor_copy(src_slot[:, bass.ds(st.times(1), 1)], slot_of[st.offset % RING][:]).then_inc(slot_kept.sem(st), 1)

                    pipeline(dve, n, [(5, lambda st: tail.inverse(dve, st)),
                                      (2, lambda st: norm2.moments_of(dve, st)),
                                      (6, lambda st: norm3.moments_of(dve, st)),
                                      (4, lambda st: tail.leak(dve, st)),
                                      (2, lambda st: norm2.inverse(dve, st)),
                                      (2, lambda st: norm2.normalise(dve, st)),
                                      (6, lambda st: norm3.inverse(dve, st)),
                                      (6, lambda st: norm3.normalise(dve, st)),
                                      (9, stats), (2, keep_slots)])
                    dve.wait_ge(*g_stats.at(Step(0, n - 1)))
                    dve.wait_ge(*slot_kept.at(Step(0, n - 1)))

                @block.tensor
                def _(pe):
                    def product(st):
                        pe.wait_ge(*h2c_done.at(st))
                        if st.back(1):
                            pe.wait_ge(*tail.leaky_done.at(st.back(1)))
                        for half in range(2):
                            pe.matmul(psum_b[:, half, :], ones_cuts[:], bias_cuts[:], start=True, stop=False, skip_group_check=True)
                        rows_product(pe, psum_b, h2c[st.parity], w1, start=False).then_inc(y_done.sem(st), 1)

                    def self_product(st):
                        pe.wait_ge(*h3c_done.at(st))
                        if st.back(1):
                            pe.wait_ge(*gc_done.at(st.back(1)))
                        columns_product(pe, psum_d, w_self, h3c[st.parity]).then_inc(g_done.sem(st), 1)

                    pipeline(pe, n, [(4, product), (3, lambda st: norm2.turn(pe, st)),
                                     (8, self_product), (7, lambda st: norm3.turn(pe, st))])
            close(n)

        class Gather:

            def __init__(self, sb, name, table, index, free, bound, zero=False):
                self.table, self.index, self.free, self.bound, self.zero = table, index, free, bound, zero
                self.rows = [sb(f"{name}_rows{b}", [P, TILES, D]) for b in range(RING)]
                self.at = [sb(f"{name}_at{b}", [P, TILES], I32) for b in range(RING)]
                self.index_done = signal("index_done")
                self.ready = signal("gathered", 16 * TILES, ring=RING)
                if zero:
                    self.zeroed = signal(f"{name}_zeroed")

            def fetch(self, pool, st):
                b = st.offset % RING
                for sig in self.free:
                    if st.back(RING):
                        pool.wait_ge(*sig.at(st.back(RING)))
                pool.tensor_copy(self.at[b][:], self.index[:, bass.ds(st.times(TILES), TILES)]).then_inc(self.index_done.sem(st), 1)
                if self.zero:
                    pool.memset(self.rows[b][:], 0.0).then_inc(self.zeroed.sem(st), 1)
                    pool.wait_ge(*self.zeroed.at(st))
                pool.wait_ge(*self.index_done.at(st))
                pool.sem_inc(pool_turns, 1)
                for j in range(TILES):
                    pool.indirect_dma_start(self.rows[b][:, j, :], None, self.table,
                                            bass.IndirectOffsetOnAxis(self.at[b][:, j:j + 1], 0),
                                            bounds_check=self.bound, oob_is_err=False).then_inc(self.ready.sem(st), 16)

        class Sources:

            def __init__(self, sb, name, table, free, over=None):
                self.table, self.free, self.over = table, free, over
                self.rows = [sb(f"{name}_rows{b}", [P, TILES, D]) for b in range(RING)]
                self.landed = self.ready = signal(f"{name}_loaded", 16, ring=RING)
                if over is not None:
                    self.over_at = [sb(f"{name}_over_at{b}", [P, TILES], I32) for b in range(RING)]
                    self.over_index_done = signal("index_done")
                    self.ready = signal("gathered", 16 * TILES, ring=RING)

            def load(self, sp, st):
                for sig in self.free:
                    if st.back(RING):
                        sp.wait_ge(*sig.at(st.back(RING)))
                sp.dma_start(self.rows[st.offset % RING][:], edge_groups(self.table)[st.times(1)]).then_inc(self.landed.sem(st), 16)

            def overlay(self, pool, st):
                b = st.offset % RING
                if st.back(RING):
                    pool.wait_ge(*self.ready.at(st.back(RING)))
                pool.tensor_copy(self.over_at[b][:], src_slot[:, bass.ds(st.times(TILES), TILES)])\
                    .then_inc(self.over_index_done.sem(st), 1)
                pool.wait_ge(*self.over_index_done.at(st))
                pool.wait_ge(*self.landed.at(st))
                pool.sem_inc(pool_turns, 1)
                for j in range(TILES):
                    pool.indirect_dma_start(self.rows[b][:, j, :], None, self.over,
                                            bass.IndirectOffsetOnAxis(self.over_at[b][:, j:j + 1], 0),
                                            bounds_check=EDGE_PAD - 1, oob_is_err=False).then_inc(self.ready.sem(st), 16)

        class Sums:

            def __init__(self, sb, name, source, ready, free, parts=H):
                self.source, self.ready, self.free, self.parts = source, ready, free, parts
                self.columns = [sb(f"{name}_sums{b}", [P, parts, GROUP]) for b in range(2)]
                self.done = signal(f"{name}_sums_done")

            def scan(self, dve, st):
                b = st.parity
                dve.wait_ge(*self.ready.at(st))
                for sig in self.free:
                    if st.back(2):
                        dve.wait_ge(*sig.at(st.back(2)))
                if st.back(1):
                    dve.wait_ge(*self.done.at(st.back(1)))
                for k in range(self.parts):
                    carry = self.columns[1 - b][:, k, GROUP - 1:GROUP] if st.back(1) else 0.0
                    source = self.source[b][:, k, :] if isinstance(self.source, list) else self.source[:, k, :]
                    last = dve.tensor_tensor_scan(self.columns[b][:, k, :], same[:, bass.ds(st.times(GROUP), GROUP)], source,
                                                  carry, ALU.mult, ALU.add)
                last.then_inc(self.done.sem(st), 1)

        def tile_weight(st):
            return lambda j: weight_col[:, bass.ds(st.times(TILES, j), 1)]

        def turn_back(pe, psum, columns):
            for j in range(TILES):
                for k in range(H):
                    last = pe.transpose(psum[:, j // 2, (j % 2) * D + k * P:(j % 2) * D + (k + 1) * P],
                                        columns[:, k, j * P:(j + 1) * P], ident[:])
            return last

        n = EDGE_GROUPS
        two = range(2)

        with ExitStack() as own:
            sb = tensors(own)
            back_done = signal("back_done")
            part_done = signal("part_done")
            hop_stored = signal("hop_stored", 16, ring=2)
            part_stored = signal("part_stored", 16, ring=2)
            rows_back = [sb(f"rows_back{b}", [P, TILES, D]) for b in two]
            part = [sb(f"part{b}", [P, TILES, D]) for b in two]
            product_done = signal("product_done")
            back_turned = signal("back_turned")
            added_up = signal("added_up")
            norm = Norm(sb, "norm", None, None, psum_a, None, weight=tile_weight)
            bases_done = signal("bases_done", 2)
            bases_stored = signal("bases_stored", 32, ring=2)
            src_rows = Sources(sb, "src", xs_rows, [norm.h_done])
            dst_rows = Sources(sb, "dst", xd_rows, [part_done])
            base_gat = [sb(f"base_gat{b}", [P, TILES, D]) for b in two]
            base_lone = [sb(f"base_lone{b}", [P, TILES, D]) for b in two]
            norm.rows, norm.rows_ready = src_rows.rows, src_rows.ready
            sums = Sums(sb, "hop", psum_a, norm.turned, [product_done])
            norm.taken = sums.done
            with nc.Block() as block:
                @block.gpsimd
                def _(pool):
                    def bases(st):
                        b = st.parity
                        pool.wait_ge(*src_rows.ready.at(st))
                        if st.back(2):
                            pool.wait_ge(*bases_stored.at(st.back(2)))
                        for to, row in ((base_gat[b], bias0_row), (base_lone[b], lone_row)):
                            pool.tensor_tensor(to[:], src_rows.rows[st.offset % RING][:],
                                               row[:].unsqueeze(1).to_broadcast([P, TILES, D]), ALU.add).then_inc(bases_done.sem(st), 1)

                    pipeline(pool, n, [(1, bases)])

                @block.scalar
                def _(act):
                    def back(st):
                        act.wait_ge(*back_turned.at(st))
                        if st.back(2):
                            act.wait_ge(*hop_stored.at(st.back(2)))
                        act.activation(rows_back[st.parity][:], pair_rows(psum_c), ACT.Copy).then_inc(back_done.sem(st), 1)

                    pipeline(act, n, [(2, lambda st: norm.normalise_relu(act, st)), (5, back), (1, lambda st: norm.deviation(act, st))])

                @block.vector
                def _(dve):
                    def add_up(st):
                        b = st.parity
                        dve.wait_ge(*product_done.at(st))
                        dve.wait_ge(*dst_rows.ready.at(st))
                        if st.back(2):
                            dve.wait_ge(*part_stored.at(st.back(2)))
                        dve.tensor_tensor(part[b][:], pair_rows(psum_b), dst_rows.rows[st.offset % RING][:], ALU.add).then_inc(added_up.sem(st), 1)
                        dve.wait_ge(*added_up.at(st))
                        dve.tensor_tensor(part[b][:], part[b][:], bias0_row[:].unsqueeze(1).to_broadcast([P, TILES, D]), ALU.add)\
                           .then_inc(part_done.sem(st), 1)

                    pipeline(dve, n, [(5, add_up), (3, lambda st: sums.scan(dve, st)), (1, lambda st: norm.moments_of(dve, st)),
                                      (2, lambda st: norm.weigh(dve, st)), (1, lambda st: norm.inverse(dve, st))])

                @block.tensor
                def _(pe):
                    def product(st):
                        pe.wait_ge(*sums.done.at(st))
                        if st.back(1):
                            pe.wait_ge(*back_done.at(st.back(1)))
                            pe.wait_ge(*added_up.at(st.back(1)))
                        turn_back(pe, psum_c, sums.columns[st.parity]).then_inc(back_turned.sem(st), 1)
                        rows_product(pe, psum_b, sums.columns[st.parity], w_hop0).then_inc(product_done.sem(st), 1)

                    pipeline(pe, n, [(3, lambda st: norm.turn(pe, st)), (4, product)])

                @block.sync
                def _(sp):
                    def store(st):
                        sp.wait_ge(*back_done.at(st))
                        sp.dma_start(edge_groups(hop1_rows)[st.times(1)], rows_back[st.parity][:]).then_inc(hop_stored.sem(st), 16)
                        sp.wait_ge(*part_done.at(st))
                        sp.dma_start(edge_groups(x1_part)[st.times(1)], part[st.parity][:]).then_inc(part_stored.sem(st), 16)

                    def store_bases(st):
                        sp.wait_ge(*bases_done.at(st))
                        for to, rows in ((xs_gat, base_gat), (xs_lone, base_lone)):
                            sp.dma_start(edge_groups(to)[st.times(1)], rows[st.parity][:]).then_inc(bases_stored.sem(st), 16)

                    pipeline(sp, n, [(0, lambda st: src_rows.load(sp, st)), (3, lambda st: dst_rows.load(sp, st)),
                                     (2, store_bases), (6, store)])
                    last_two(sp, bases_stored, n)
                    last_two(sp, hop_stored, n)
                    last_two(sp, part_stored, n)
            close(n)

        with ExitStack() as own:
            sb = tensors(own)
            weighted = signal("weighted")
            turned = signal("turned")
            product_done = signal("product_done")
            part_landed = signal("part_landed", 16, ring=2)
            x1_done = signal("x1_done")
            x1_stored = signal("x1_stored", 16, ring=2)
            h1c_done = signal("h1c_done")
            score_done = signal("score_done")
            score_out = signal("score_out")
            score_stored = signal("score_stored", 16, ring=2)
            part = [sb(f"part{b}", [P, TILES, D]) for b in two]
            x1 = [sb(f"x1_{b}", [P, TILES, D]) for b in two]
            scaled = [sb(f"scaled{b}", [P, TILES, D]) for b in two]
            h1c = [sb(f"h1c{b}", [P, H, GROUP]) for b in two]
            score = [sb(f"score{b}", [HEADS, GROUP]) for b in two]
            hop_rows = Gather(sb, "src", hop1_rows, src_slot, [weighted], EDGE_PAD - 1, zero=True)
            sums = Sums(sb, "hop", psum_a, turned, [product_done])
            norm = Norm(sb, "norm", x1, x1_done, psum_c, h1c_done)
            with nc.Block() as block:
                @block.gpsimd
                def _(pool):
                    pipeline(pool, n, [(0, lambda st: hop_rows.fetch(pool, st))])

                @block.scalar
                def _(act):
                    def h1_out(st):
                        act.wait_ge(*norm.turned.at(st))
                        if st.back(2):
                            act.wait_ge(*score_done.at(st.back(2)))
                        act.activation(h1c[st.parity][:], psum_c[:], ACT.Copy).then_inc(h1c_done.sem(st), 1)

                    def out_score(st):
                        act.wait_ge(*score_done.at(st))
                        if st.back(2):
                            act.wait_ge(*score_stored.at(st.back(2)))
                        act.activation(score[st.parity][:], psum_d[0:HEADS, 0, :], ACT.Copy).then_inc(score_out.sem(st), 1)

                    pipeline(act, n, [(8, out_score), (5, lambda st: norm.normalise_relu(act, st)), (6, h1_out),
                                      (4, lambda st: norm.deviation(act, st))])

                @block.vector
                def _(dve):
                    def weigh(st):
                        b = st.parity
                        dve.wait_ge(*hop_rows.ready.at(st))
                        if st.back(2):
                            dve.wait_ge(*turned.at(st.back(2)))
                        for j in range(TILES):
                            last = dve.tensor_scalar(scaled[b][:, j, :], hop_rows.rows[st.offset % RING][:, j, :], tile_weight(st)(j), None, ALU.mult)
                        last.then_inc(weighted.sem(st), 1)

                    def add_up(st):
                        b = st.parity
                        dve.wait_ge(*product_done.at(st))
                        dve.wait_ge(*part_landed.at(st))
                        if st.back(2):
                            dve.wait_ge(*x1_stored.at(st.back(2)))
                            dve.wait_ge(*norm.h_done.at(st.back(2)))
                        dve.tensor_tensor(x1[b][:], pair_rows(psum_b), part[b][:], ALU.add).then_inc(x1_done.sem(st), 1)

                    pipeline(dve, n, [(4, add_up), (4, lambda st: norm.moments_of(dve, st)), (2, lambda st: sums.scan(dve, st)),
                                      (1, weigh), (4, lambda st: norm.inverse(dve, st))])

                @block.tensor
                def _(pe):
                    def turn(st):
                        pe.wait_ge(*weighted.at(st))
                        if st.back(1):
                            pe.wait_ge(*sums.done.at(st.back(1)))
                        for k in range(H):
                            for j in range(TILES):
                                last = pe.transpose(psum_a[:, k, j * P:(j + 1) * P], scaled[st.parity][:, j, k * P:(k + 1) * P], ident[:])
                        last.then_inc(turned.sem(st), 1)

                    def product(st):
                        pe.wait_ge(*sums.done.at(st))
                        if st.back(1):
                            pe.wait_ge(*x1_done.at(st.back(1)))
                        rows_product(pe, psum_b, sums.columns[st.parity], w_hop1).then_inc(product_done.sem(st), 1)

                    def scores(st):
                        pe.wait_ge(*h1c_done.at(st))
                        if st.back(1):
                            pe.wait_ge(*score_out.at(st.back(1)))
                        for k in range(H):
                            last = pe.matmul(psum_d[0:HEADS, 0, :], gat_vd[:, k, :], h1c[st.parity][:, k, :], start=k == 0, stop=k == H - 1)
                        last.then_inc(score_done.sem(st), 1)

                    pipeline(pe, n, [(2, turn), (6, lambda st: norm.turn(pe, st)), (7, scores), (3, product)])

                @block.sync
                def _(sp):
                    def load(st):
                        if st.back(2):
                            sp.wait_ge(*x1_done.at(st.back(2)))
                        sp.dma_start(part[st.parity][:], edge_groups(x1_part)[st.times(1)]).then_inc(part_landed.sem(st), 16)

                    def store(st):
                        sp.wait_ge(*x1_done.at(st))
                        sp.dma_start(edge_groups(x1_rows)[st.times(1)], x1[st.parity][:]).then_inc(x1_stored.sem(st), 16)

                    def store_score(st):
                        sp.wait_ge(*score_out.at(st))
                        sp.dma_start(score_dst[:, bass.ds(st.times(GROUP), GROUP)], score[st.parity][:]).then_inc(score_stored.sem(st), 16)

                    pipeline(sp, n, [(3, load), (5, store), (9, store_score)])
                    last_two(sp, x1_stored, n)
                    last_two(sp, score_stored, n)
            close(n)

        with ExitStack() as own:
            sb = tensors(own)
            h1c_done = signal("h1c_done")
            gat_done = signal("gat_done")
            gat_out = signal("gat_out")
            gat_stored = signal("gat_stored", 16, ring=2)
            score_out = signal("score_out")
            score_stored = signal("score_stored", 16, ring=2)
            h1c = [sb(f"h1c{b}", [P, H, GROUP]) for b in two]
            gat = [sb(f"gat{b}", [P, H, GROUP]) for b in two]
            score = [sb(f"score{b}", [HEADS, GROUP]) for b in two]
            norm = Norm(sb, "norm", None, None, psum_a, h1c_done)
            src_rows = Sources(sb, "src", xs_gat, [norm.h_done], over=x1_rows)
            norm.rows, norm.rows_ready = src_rows.rows, src_rows.ready
            with nc.Block() as block:
                @block.gpsimd
                def _(pool):
                    pipeline(pool, n, [(1, lambda st: src_rows.overlay(pool, st))])

                @block.scalar
                def _(act):
                    def h1_out(st):
                        act.wait_ge(*norm.turned.at(st))
                        if st.back(2):
                            act.wait_ge(*gat_done.at(st.back(2)))
                        act.activation(h1c[st.parity][:], psum_a[:], ACT.Copy).then_inc(h1c_done.sem(st), 1)

                    def out_score(st):
                        act.wait_ge(*gat_done.at(st))
                        if st.back(2):
                            act.wait_ge(*score_stored.at(st.back(2)))
                        act.activation(score[st.parity][:], psum_d[0:HEADS, 0, :], ACT.Copy).then_inc(score_out.sem(st), 1)

                    pipeline(act, n, [(6, out_score), (3, lambda st: norm.normalise_relu(act, st)), (4, h1_out),
                                      (2, lambda st: norm.deviation(act, st))])

                @block.vector
                def _(dve):
                    def out_gat(st):
                        dve.wait_ge(*gat_done.at(st))
                        if st.back(2):
                            dve.wait_ge(*gat_stored.at(st.back(2)))
                        dve.tensor_copy(gat[st.parity][:], psum_b[:]).then_inc(gat_out.sem(st), 1)

                    pipeline(dve, n, [(6, out_gat), (2, lambda st: norm.moments_of(dve, st)), (2, lambda st: norm.inverse(dve, st))])

                @block.tensor
                def _(pe):
                    def product(st):
                        pe.wait_ge(*h1c_done.at(st))
                        if st.back(1):
                            pe.wait_ge(*gat_out.at(st.back(1)))
                            pe.wait_ge(*score_out.at(st.back(1)))
                        for k in range(H):
                            pe.matmul(psum_d[0:HEADS, 0, :], gat_vs[:, k, :], h1c[st.parity][:, k, :], start=k == 0, stop=k == H - 1)
                        columns_product(pe, psum_b, gat_w, h1c[st.parity]).then_inc(gat_done.sem(st), 1)

                    pipeline(pe, n, [(4, lambda st: norm.turn(pe, st)), (5, product)])

                @block.sync
                def _(sp):
                    def store(st):
                        sp.wait_ge(*score_out.at(st))
                        sp.dma_start(score_src[:, bass.ds(st.times(GROUP), GROUP)], score[st.parity][:]).then_inc(score_stored.sem(st), 16)
                        sp.wait_ge(*gat_out.at(st))
                        sp.dma_start(gat_columns[st.times(1)], gat[st.parity][:].rearrange("p k n -> p (k n)"))\
                          .then_inc(gat_stored.sem(st), 16)

                    pipeline(sp, n, [(0, lambda st: src_rows.load(sp, st)), (7, store)])
                    last_two(sp, gat_stored, n)
                    last_two(sp, score_stored, n)
            close(n)

        with ExitStack() as own:
            sb = tensors(own)
            a = sb("softmax_a", [HEADS, EDGE_PAD])
            b = sb("softmax_b", [HEADS, EDGE_PAD])
            nxt = sb("softmax_next", [HEADS, EDGE_PAD], BF16)
            reset = sb("softmax_reset", [HEADS, EDGE_PAD // 5])
            norm_t = sb("norm_t", [EDGE_TILES, P])

            def spread(dve):
                link(dve, dve.scalar_tensor_tensor(b[:], nxt[:], 0.0, b[:], ALU.is_equal, ALU.mult))
                link(dve, dve.tensor_tensor_scan(b[:, ::-1], nxt[:, ::-1], b[:, ::-1], 0.0, ALU.mult, ALU.add))

            with nc.Block() as block:
                @block.sync
                def _(sp):
                    move(sp, (a[:], score_src), (b[:], score_dst), (nxt[:], next_flags.to_broadcast([HEADS, EDGE_PAD])))

            with nc.Block() as block:
                @block.vector
                def _(dve):
                    spread(dve)
                    link(dve, dve.tensor_tensor(a[:], a[:], b[:], ALU.add))
                    link(dve, dve.scalar_tensor_tensor(a[:], a[:], SLOPE, a[:], ALU.mult, ALU.max))
                    wide = EDGE_PAD // 5
                    for i in range(5):
                        piece = slice(i * wide, (i + 1) * wide)
                        link(dve, dve.tensor_scalar(reset[:], same[0:HEADS, piece], FAR, -FAR, ALU.mult, ALU.add))
                        link(dve, dve.tensor_tensor_scan(b[:, piece], reset[:], a[:, piece],
                                                         b[:, i * wide - 1:i * wide] if i else -FAR, ALU.add, ALU.max))
                    spread(dve)
                    link(dve, dve.tensor_tensor(a[:], a[:], b[:], ALU.subtract))

            with nc.Block() as block:
                @block.scalar
                def _(act):
                    link(act, act.activation(a[:], a[:], ACT.Exp))

            with nc.Block() as block:
                @block.sync
                def _(sp):
                    move(sp, (exp_rows, a[:]))

                @block.vector
                def _(dve):
                    dve.tensor_tensor_scan(b[:], same[0:HEADS, :], a[:], 0.0, ALU.mult, ALU.add).then_inc(softmax_step, 1)
                    dve.wait_ge(softmax_step, 1)
                    dve.tensor_scalar(b[:], b[:], 1e-16, None, ALU.add).then_inc(softmax_step, 1)
                    dve.wait_ge(softmax_step, 2)
                    dve.reciprocal(b[:], b[:]).then_inc(softmax_step, 1)
                    dve.wait_ge(softmax_step, 3)

            with nc.Block() as block:
                @block.sync
                def _(sp):
                    move(sp, (inv_rows, b[:]))

                @block.vector
                def _(dve):
                    link(dve, dve.memset(a[:], 1.0))

            with nc.Block() as block:
                @block.vector
                def _(dve):
                    link(dve, dve.tensor_tensor_scan(b[:], same[0:HEADS, :], a[:], 0.0, ALU.mult, ALU.add))
                    spread(dve)
                    link(dve, dve.tensor_scalar(b[:], b[:], 1.0, None, ALU.max))

            with nc.Block() as block:
                @block.sync
                def _(sp):
                    move(sp, (norm_row.rearrange("(o t) p -> o (t p)", o=1), b[0:1, :]))
                    move(sp, (norm_t[:], norm_row))

            with nc.Block() as block:
                @block.scalar
                def _(act):
                    link(act, act.activation(norm_t[:], norm_t[:], ACT.Sqrt))

            with nc.Block() as block:
                @block.vector
                def _(dve):
                    link(dve, dve.reciprocal(norm_t[:], norm_t[:]))

            with nc.Block() as block:
                @block.tensor
                def _(pe):
                    link(pe, pe.transpose(psum_a[:, 0, 0:EDGE_TILES], norm_t[:], ident[0:EDGE_TILES, 0:EDGE_TILES]))

            with nc.Block() as block:
                @block.vector
                def _(dve):
                    link(dve, dve.tensor_copy(norm_col[:], psum_a[:, 0, 0:EDGE_TILES]))

        with ExitStack() as own:
            sb = tensors(own)
            gat_landed = signal("gat_landed", 16, ring=2)
            exps_landed = signal("exps_landed", 16, ring=2)
            invs_landed = signal("invs_landed", 16, ring=2)
            part_landed = signal("part_landed", 16, ring=2)
            exps_spread = signal("exps_spread")
            invs_spread = signal("invs_spread")
            message_done = signal("message_done")
            divided = signal("divided")
            relu_done = signal("relu_done")
            back_turned = signal("back_turned")
            x2e_done = signal("x2e_done")
            x2e_stored = signal("x2e_stored", 16, ring=2)
            h2c_done = signal("h2c_done")
            h2c_stored = signal("h2c_stored", 16, ring=2)
            gat = [sb(f"gat{i}", [P, H, GROUP]) for i in two]
            exps = [sb(f"exps{i}", [HEADS, GROUP]) for i in two]
            invs = [sb(f"invs{i}", [HEADS, GROUP]) for i in two]
            message = [sb(f"message{i}", [P, H, GROUP]) for i in two]
            ratio = [sb(f"ratio{i}", [P, H, GROUP]) for i in two]
            part = [sb(f"part{i}", [P, TILES, D]) for i in two]
            x2e = [sb(f"x2e{i}", [P, TILES, D]) for i in two]
            h2c = [sb(f"h2c{i}", [P, H, GROUP]) for i in two]
            sums = Sums(sb, "gat", message, message_done, [divided])
            norm = Norm(sb, "norm", x2e, x2e_done, psum_d, h2c_done)
            with nc.Block() as block:
                @block.scalar
                def _(act):
                    def relu(st):
                        i = st.parity
                        act.wait_ge(*divided.at(st))
                        sem, value = relu_done.at(st)
                        for k in range(H):
                            last = act.activation(ratio[i][:, k, :], ratio[i][:, k, :], ACT.Relu, bias=bias1_col[:, k:k + 1])
                        last.then_inc(sem, 1)

                    def h2_out(st):
                        act.wait_ge(*norm.turned.at(st))
                        if st.back(2):
                            act.wait_ge(*h2c_stored.at(st.back(2)))
                        act.activation(h2c[st.parity][:], psum_d[:], ACT.Copy).then_inc(h2c_done.sem(st), 1)

                    pipeline(act, n, [(5, lambda st: norm.normalise_relu(act, st)), (6, h2_out),
                                      (4, lambda st: norm.deviation(act, st)), (2, relu)])

                @block.vector
                def _(dve):
                    def weigh(st):
                        i = st.parity
                        dve.wait_ge(*gat_landed.at(st))
                        dve.wait_ge(*exps_spread.at(st))
                        dve.tensor_tensor(message[i][:], gat[i][:], psum_a[:], ALU.mult).then_inc(message_done.sem(st), 1)

                    def divide(st):
                        i = st.parity
                        dve.wait_ge(*sums.done.at(st))
                        dve.wait_ge(*invs_spread.at(st))
                        if st.back(2):
                            dve.wait_ge(*back_turned.at(st.back(2)))
                        dve.tensor_tensor(ratio[i][:], sums.columns[i][:], psum_b[:], ALU.mult).then_inc(divided.sem(st), 1)

                    def add_up(st):
                        i = st.parity
                        dve.wait_ge(*back_turned.at(st))
                        dve.wait_ge(*part_landed.at(st))
                        if st.back(2):
                            dve.wait_ge(*x2e_stored.at(st.back(2)))
                            dve.wait_ge(*norm.h_done.at(st.back(2)))
                        dve.tensor_tensor(x2e[i][:], pair_rows(psum_c), part[i][:], ALU.add).then_inc(x2e_done.sem(st), 1)

                    pipeline(dve, n, [(4, add_up), (4, lambda st: norm.moments_of(dve, st)), (2, divide),
                                      (1, weigh), (1, lambda st: sums.scan(dve, st)), (4, lambda st: norm.inverse(dve, st))])

                @block.tensor
                def _(pe):
                    def spread_heads(psum, rows, landed, used_up, done, st):
                        pe.wait_ge(*landed.at(st))
                        if st.back(1):
                            pe.wait_ge(*used_up.at(st.back(1)))
                        for k in range(H):
                            last = pe.matmul(psum[:, k, :], head_sel[:, k * P:(k + 1) * P], rows[st.parity][:], start=True, stop=True)
                        last.then_inc(done.sem(st), 1)

                    def back(st):
                        pe.wait_ge(*relu_done.at(st))
                        if st.back(1):
                            pe.wait_ge(*x2e_done.at(st.back(1)))
                        turn_back(pe, psum_c, ratio[st.parity]).then_inc(back_turned.sem(st), 1)

                    pipeline(pe, n, [(1, lambda st: spread_heads(psum_a, exps, exps_landed, message_done, exps_spread, st)),
                                     (2, lambda st: spread_heads(psum_b, invs, invs_landed, divided, invs_spread, st)),
                                     (6, lambda st: norm.turn(pe, st)), (3, back)])

                @block.sync
                def _(sp):
                    def load(st):
                        i = st.parity
                        if st.back(2):
                            sp.wait_ge(*message_done.at(st.back(2)))
                        sp.dma_start(exps[i][:], exp_rows[:, bass.ds(st.times(GROUP), GROUP)]).then_inc(exps_landed.sem(st), 16)
                        sp.dma_start(gat[i][:].rearrange("p k n -> p (k n)"), gat_columns[st.times(1)]).then_inc(gat_landed.sem(st), 16)

                    def load_inv(st):
                        if st.back(2):
                            sp.wait_ge(*invs_spread.at(st.back(2)))
                        sp.dma_start(invs[st.parity][:], inv_rows[:, bass.ds(st.times(GROUP), GROUP)]).then_inc(invs_landed.sem(st), 16)

                    def load_x1(st):
                        i = st.parity
                        if st.back(2):
                            sp.wait_ge(*x2e_done.at(st.back(2)))
                        sp.dma_start(part[i][:], edge_groups(x1_rows)[st.times(1)]).then_inc(part_landed.sem(st), 16)

                    def store(st):
                        i = st.parity
                        sp.wait_ge(*x2e_done.at(st))
                        sp.dma_start(edge_groups(x2_rows)[st.times(1)], x2e[i][:]).then_inc(x2e_stored.sem(st), 16)

                    def store_columns(st):
                        i = st.parity
                        sp.wait_ge(*h2c_done.at(st))
                        sp.dma_start(h2_columns[st.times(1)], h2c[i][:].rearrange("p k n -> p (k n)")).then_inc(h2c_stored.sem(st), 16)

                    pipeline(sp, n, [(0, load), (1, load_inv), (3, load_x1), (5, store), (7, store_columns)])
                    last_two(sp, x2e_stored, n)
                    last_two(sp, h2c_stored, n)
            close(n)

        with ExitStack() as own:
            sb = tensors(own)
            h2c_landed = signal("h2c_landed", 16, ring=RING)
            part_landed = signal("part_landed", 16, ring=2)
            side_done = signal("side_done")
            y_done = signal("y_done")
            x3_stored = signal("x3_stored", 16, ring=2)
            x3_sent = signal("x3_sent", 16 * TILES, ring=2)
            last_copied = signal("last_copied")
            h3c_done = signal("h3c_done")
            h3c_stored = signal("h3c_stored", 16, ring=2)
            h2c = [sb(f"h2c{i}", [P, H, GROUP]) for i in range(RING)]
            side = [sb(f"side{i}", [P, H, GROUP]) for i in two]
            part = [sb(f"part{i}", [P, TILES, D]) for i in two]
            h3c = [sb(f"h3c{i}", [P, H, GROUP]) for i in two]
            last_at = [sb(f"last_at{i}", [P, TILES], I32) for i in two]
            norm = Norm(sb, "norm", None, None, psum_a, None, weight=tile_weight)
            src_rows = Sources(sb, "src", xs_lone, [norm.h_done], over=x2_rows)
            norm.rows, norm.rows_ready = src_rows.rows, src_rows.ready
            sums = Sums(sb, "hop", psum_a, norm.turned, [side_done])
            norm.taken = sums.done
            norm3 = Norm(sb, "norm3", None, None, psum_c, h3c_done)
            tail = Tail(sb, y_done, part, part_landed, [x3_stored, x3_sent, norm3.h_done])
            norm3.rows, norm3.rows_ready = tail.x3, tail.x3_done
            with nc.Block() as block:
                @block.gpsimd
                def _(pool):
                    def send(st):
                        i = st.parity
                        if st.back(2):
                            pool.wait_ge(*x3_sent.at(st.back(2)))
                        pool.tensor_copy(last_at[i][:], last_col[:, bass.ds(st.times(TILES), TILES)]).then_inc(last_copied.sem(st), 1)
                        pool.wait_ge(*last_copied.at(st))
                        pool.wait_ge(*tail.x3_done.at(st))
                        pool.sem_inc(pool_turns, 1)
                        for j in range(TILES):
                            pool.indirect_dma_start(x3_nodes, bass.IndirectOffsetOnAxis(last_at[i][:, j:j + 1], 0),
                                                    tail.x3[i][:, j, :], None, bounds_check=N - 1, oob_is_err=False)\
                                .then_inc(x3_sent.sem(st), 16)

                    pipeline(pool, n, [(1, lambda st: src_rows.overlay(pool, st)), (8, send)])
                    last_two(pool, x3_sent, n)

                @block.scalar
                def _(act):
                    def h3_out(st):
                        act.wait_ge(*norm3.turned.at(st))
                        if st.back(2):
                            act.wait_ge(*h3c_stored.at(st.back(2)))
                        act.activation(h3c[st.parity][:], psum_c[:], ACT.Copy).then_inc(h3c_done.sem(st), 1)

                    pipeline(act, n, [(6, lambda st: tail.slope(act, st)), (9, h3_out),
                                      (3, lambda st: norm.normalise_relu(act, st)), (6, lambda st: tail.square_up(act, st)),
                                      (2, lambda st: norm.deviation(act, st)), (8, lambda st: norm3.normalise_relu(act, st)),
                                      (7, lambda st: norm3.deviation(act, st))])

                @block.vector
                def _(dve):
                    def interact(st):
                        i = st.parity
                        dve.wait_ge(*sums.done.at(st))
                        dve.wait_ge(*h2c_landed.at(st))
                        if st.back(2):
                            dve.wait_ge(*y_done.at(st.back(2)))
                        dve.scalar_tensor_tensor(side[i][:], h2c[st.offset % RING][:], 1.0, sums.columns[i][:], ALU.add, ALU.mult)\
                           .then_inc(side_done.sem(st), 1)

                    pipeline(dve, n, [(7, lambda st: tail.inverse(dve, st)), (6, lambda st: tail.leak(dve, st)),
                                      (7, lambda st: tail.residual(dve, st)), (7, lambda st: norm3.moments_of(dve, st)),
                                      (4, lambda st: sums.scan(dve, st)), (4, interact),
                                      (2, lambda st: norm.moments_of(dve, st)), (3, lambda st: norm.weigh(dve, st)),
                                      (7, lambda st: norm3.inverse(dve, st)), (2, lambda st: norm.inverse(dve, st))])

                @block.tensor
                def _(pe):
                    def product(st):
                        pe.wait_ge(*side_done.at(st))
                        if st.back(1):
                            pe.wait_ge(*tail.leaky_done.at(st.back(1)))
                        for half in range(2):
                            pe.matmul(psum_b[:, half, :], ones_cuts[:], bias_cuts[:], start=True, stop=False, skip_group_check=True)
                        rows_product(pe, psum_b, h2c[st.offset % RING], w1, start=False, stop=False)
                        rows_product(pe, psum_b, side[st.parity], w2, start=False).then_inc(y_done.sem(st), 1)

                    pipeline(pe, n, [(4, lambda st: norm.turn(pe, st)), (9, lambda st: norm3.turn(pe, st)), (5, product)])

                @block.sync
                def _(sp):
                    def load(st):
                        if st.back(RING):
                            sp.wait_ge(*y_done.at(st.back(RING)))
                        sp.dma_start(h2c[st.offset % RING][:].rearrange("p k n -> p (k n)"), h2_columns[st.times(1)]).then_inc(h2c_landed.sem(st), 16)

                    def load_x2(st):
                        i = st.parity
                        if st.back(2):
                            sp.wait_ge(*tail.x3_done.at(st.back(2)))
                        sp.dma_start(part[i][:], edge_groups(x2_rows)[st.times(1)]).then_inc(part_landed.sem(st), 16)

                    def store(st):
                        i = st.parity
                        sp.wait_ge(*tail.x3_done.at(st))
                        sp.dma_start(edge_groups(x3_rows)[st.times(1)], tail.x3[i][:]).then_inc(x3_stored.sem(st), 16)

                    def store_columns(st):
                        i = st.parity
                        sp.wait_ge(*h3c_done.at(st))
                        sp.dma_start(h3_columns[st.times(1)], h3c[i][:].rearrange("p k n -> p (k n)")).then_inc(h3c_stored.sem(st), 16)

                    pipeline(sp, n, [(0, lambda st: src_rows.load(sp, st)), (2, load), (6, load_x2), (8, store), (10, store_columns)])
                    last_two(sp, x3_stored, n)
                    last_two(sp, h3c_stored, n)
            close(n)

        with ExitStack() as own:
            sb = tensors(own)
            attr_landed = signal("attr_landed", 16, ring=2)
            attr_turned = signal("attr_turned")
            attr_out = signal("attr_out")
            hsc_done = signal("hsc_done")
            freq_done = signal("freq_done")
            attr_freq_out = signal("attr_freq_out")
            crossed = signal("crossed")
            multiplied = signal("multiplied")
            h3c_landed = signal("h3c_landed", 16, ring=2)
            g_done = signal("g_done")
            g_masked = signal("g_masked")
            g_counted = signal("g_counted")
            ge_stored = signal("ge_stored", 16, ring=2)
            attr = [sb(f"attr{i}", [P, TILES, D]) for i in two]
            attr_c = [sb(f"attr_c{i}", [P, H, GROUP]) for i in two]
            hsc = [sb(f"hsc{i}", [P, H, GROUP]) for i in two]
            attr_f = [sb(f"attr_f{i}", [P, H, GROUP]) for i in two]
            cross = sb("cross", [P, 2, GROUP])
            products = [sb(f"products{i}", [P, 3, GROUP]) for i in two]
            h3c = [sb(f"h3c{i}", [P, H, GROUP]) for i in two]
            ge = [sb(f"ge{i}", [P, H, GROUP]) for i in two]
            nxt = sb("next_wide", [P, EDGE_PAD], BF16)
            norm = Norm(sb, "norm3", None, None, psum_a, attr_out,
                        scale=lambda st: norm_col[:, bass.ds(st.times(TILES), TILES)])
            src_rows = Gather(sb, "src", x3_nodes, src_col, [norm.h_done], N - 1)
            norm.rows, norm.rows_ready = src_rows.rows, src_rows.ready
            sums = Sums(sb, "freq", products, multiplied, [g_done], parts=3)
            with nc.Block() as block:
                @block.sync
                def _(sp):
                    move(sp, (nxt[:], next_flags.to_broadcast([P, EDGE_PAD])))

                @block.vector
                def _(dve):
                    for i in two:
                        last = dve.memset(attr[i][:], 0.0)
                    link(dve, last)

            with nc.Block() as block:
                @block.gpsimd
                def _(pool):
                    pipeline(pool, n, [(0, lambda st: src_rows.fetch(pool, st))])

                @block.scalar
                def _(act):
                    def hs_out(st):
                        act.wait_ge(*norm.turned.at(st))
                        if st.back(2):
                            act.wait_ge(*freq_done.at(st.back(2)))
                        act.activation(hsc[st.parity][:], psum_a[:], ACT.Copy).then_inc(hsc_done.sem(st), 1)

                    def attr_back(st):
                        act.wait_ge(*attr_turned.at(st))
                        act.activation(attr_c[st.parity][:], psum_a[:], ACT.Copy).then_inc(attr_out.sem(st), 1)

                    def freq_out(st):
                        act.wait_ge(*freq_done.at(st))
                        if st.back(2):
                            act.wait_ge(*multiplied.at(st.back(2)))
                        act.activation(attr_f[st.parity][:], psum_d[:], ACT.Copy).then_inc(attr_freq_out.sem(st), 1)

                    pipeline(act, n, [(5, freq_out), (3, hs_out), (2, lambda st: norm.normalise_relu(act, st)), (3, attr_back),
                                      (1, lambda st: norm.deviation(act, st))])

                @block.vector
                def _(dve):
                    def multiply(st):
                        i = st.parity
                        dve.wait_ge(*attr_freq_out.at(st))
                        re, im = attr_f[i][:, 0, :], attr_f[i][:, 1, :]
                        dve.tensor_tensor(cross[:, 0, :], psum_c[:, 0, :], im, ALU.mult)
                        dve.tensor_tensor(cross[:, 1, :], psum_c[:, 1, :], re, ALU.mult).then_inc(crossed.sem(st), 1)
                        dve.tensor_tensor(products[i][:, 0, :], psum_c[:, 0, :], re, ALU.mult)
                        dve.tensor_tensor(products[i][:, 1, :], psum_c[:, 1, :], im, ALU.mult)
                        dve.wait_ge(*crossed.at(st))
                        dve.tensor_tensor(products[i][:, 2, :], cross[:, 0, :], cross[:, 1, :], ALU.subtract)\
                           .then_inc(multiplied.sem(st), 1)

                    def mask(st):
                        i = st.parity
                        dve.wait_ge(*g_done.at(st))
                        if st.back(2):
                            dve.wait_ge(*ge_stored.at(st.back(2)))
                        for k in range(H):
                            last = dve.scalar_tensor_tensor(ge[i][:, k, :], nxt[:, bass.ds(st.times(GROUP), GROUP)], 0.0,
                                                            psum_b[:, k, :], ALU.is_equal, ALU.mult)
                        last.then_inc(g_masked.sem(st), 1)

                    def stats(st):
                        i = st.parity
                        dve.wait_ge(*g_masked.at(st))
                        for k in range(H):
                            last = dve.bn_stats(node_stats[:, k, bass.ds(st.times(6, 6 * NODE_GROUPS), 6)], ge[i][:, k, :])
                        last.then_inc(g_counted.sem(st), 1)

                    pipeline(dve, n, [(7, mask), (5, multiply), (5, lambda st: sums.scan(dve, st)),
                                      (1, lambda st: norm.moments_of(dve, st)), (7, stats), (1, lambda st: norm.inverse(dve, st))])
                    dve.wait_ge(*g_counted.at(Step(0, n - 1)))

                @block.tensor
                def _(pe):
                    def turn_attr(st):
                        i = st.parity
                        pe.wait_ge(*attr_landed.at(st))
                        pe.wait_ge(*hsc_done.at(st))
                        for k in range(H):
                            for j in range(TILES):
                                last = pe.transpose(psum_a[:, k, j * P:(j + 1) * P], attr[i][:, j, k * P:(k + 1) * P], ident[:])
                        last.then_inc(attr_turned.sem(st), 1)

                    def transform(st):
                        i = st.parity
                        pe.wait_ge(*attr_out.at(st))
                        if st.back(1):
                            pe.wait_ge(*multiplied.at(st.back(1)))
                        columns_product(pe, psum_c, freq, hsc[i])
                        columns_product(pe, psum_d, freq, attr_c[i]).then_inc(freq_done.sem(st), 1)

                    def from_freq(st):
                        i = st.parity
                        pe.wait_ge(*sums.done.at(st))
                        pe.wait_ge(*h3c_landed.at(st))
                        if st.back(1):
                            pe.wait_ge(*g_masked.at(st.back(1)))
                        for half in range(H):
                            cut = slice(half * P, (half + 1) * P)
                            for k in range(3):
                                pe.matmul(psum_b[:, half, :], w_back[:, k, cut], sums.columns[i][:, k, :], start=k == 0, stop=False)
                            for k in range(H):
                                last = pe.matmul(psum_b[:, half, :], w_self[:, k, cut], h3c[i][:, k, :], start=False, stop=k == H - 1)
                        last.then_inc(g_done.sem(st), 1)

                    pipeline(pe, n, [(3, lambda st: norm.turn(pe, st)), (6, from_freq), (3, turn_attr), (4, transform)])

                @block.sync
                def _(sp):
                    def load(st):
                        i = st.parity
                        if st.back(2):
                            sp.wait_ge(*attr_turned.at(st.back(2)))
                        if isinstance(st.turn, int) and st.offset == n - 1:
                            at = (n - 1) * GROUP
                            whole = (E - at) // P
                            sp.dma_start(attr[i][:, 0:whole, :], edge_attr[at:at + whole * P].rearrange("(j p) d -> p j d", p=P))\
                              .then_inc(attr_landed.sem(st), 16)
                            sp.dma_start(attr[i][0:E - at - whole * P, whole, :], edge_attr[at + whole * P:E]).then_inc(attr_tail, 16)
                            sp.wait_ge(attr_tail, 16)
                        else:
                            sp.dma_start(attr[i][:], attr_groups[st.times(1)]).then_inc(attr_landed.sem(st), 16)

                    def load_h3(st):
                        i = st.parity
                        if st.back(2):
                            sp.wait_ge(*g_done.at(st.back(2)))
                        sp.dma_start(h3c[i][:].rearrange("p k n -> p (k n)"), h3_columns[st.times(1)]).then_inc(h3c_landed.sem(st), 16)

                    def store(st):
                        i = st.parity
                        sp.wait_ge(*g_masked.at(st))
                        sp.dma_start(g_edge_columns[st.times(1)], ge[i][:].rearrange("p k n -> p (k n)")).then_inc(ge_stored.sem(st), 16)

                    attr_groups = edge_groups(edge_attr[0:(n - 1) * GROUP])
                    pipeline(sp, n, [(2, load), (4, load_h3), (8, store)])
                    last_two(sp, ge_stored, n)
            close(n)

        with ExitStack() as own:
            sb = tensors(own)
            total = sb("bn_total", [P, H, 2])
            mean = sb("bn_mean", [P, H])
            square = sb("bn_square", [P, H])
            var = sb("bn_var", [P, H])
            rows = float(NODE_PAD + EDGE_PAD) / N
            with nc.Block() as block:
                @block.vector
                def _(dve):
                    for k in range(H):
                        last = dve.bn_aggr(total[:, k, :], node_stats[:, k, :])
                    link(dve, last)
                    link(dve, dve.tensor_tensor(square[:], total[:, :, 0], total[:, :, 0], ALU.mult))
                    link(dve, dve.tensor_tensor(var[:], total[:, :, 1], square[:], ALU.add))
                    link(dve, dve.tensor_scalar(var[:], var[:], rows, None, ALU.mult))
                    link(dve, dve.tensor_scalar(mean[:], total[:, :, 0], rows, None, ALU.mult))
                    link(dve, dve.tensor_tensor(square[:], mean[:], mean[:], ALU.mult))
                    link(dve, dve.tensor_tensor(var[:], var[:], square[:], ALU.subtract))
                    link(dve, dve.tensor_tensor(mean[:], mean[:], wbias_col[:], ALU.add))

            with nc.Block() as block:
                @block.scalar
                def _(act):
                    link(act, act.activation(var[:], var[:], ACT.Sqrt, bias=eps_bn[:]))

            with nc.Block() as block:
                @block.vector
                def _(dve):
                    link(dve, dve.reciprocal(var[:], var[:]))
                    link(dve, dve.tensor_tensor(bn_scale[:], var[:], gamma_col[:], ALU.mult))
                    link(dve, dve.tensor_tensor(mean[:], wbias_col[:], mean[:], ALU.subtract))
                    link(dve, dve.tensor_tensor(mean[:], mean[:], bn_scale[:], ALU.mult))
                    link(dve, dve.tensor_tensor(bn_shift[:], mean[:], beta_col[:], ALU.add))

        def last_pass(n, columns, load_rows, finish, scatter):
            with ExitStack() as own:
                sb = tensors(own)
                c_landed = signal("c_landed", 16, ring=2)
                r_landed = signal("r_landed", 16, ring=2)
                tanh_done = signal("tanh_done")
                out_turned = signal("out_turned")
                out_done = signal("out_done")
                out_stored = signal("nodes_stored" if not scatter else "out_sent", 16 * TILES if scatter else 16, ring=2)
                last_copied = signal("last_copied")
                c_in = [sb(f"c_in{i}", [P, H, GROUP]) for i in two]
                r_in = [sb(f"r_in{i}", [P, TILES, D]) for i in two]
                act_c = [sb(f"act_c{i}", [P, H, GROUP]) for i in two]
                o_rows = [sb(f"o_rows{i}", [P, TILES, D]) for i in two]
                last_at = [sb(f"last_at{i}", [P, TILES], I32) for i in two]
                psums = [psum_a, psum_b]
                with nc.Block() as block:
                    @block.sync
                    def _(sp):
                        def load(st):
                            i = st.parity
                            if st.back(2):
                                sp.wait_ge(*tanh_done.at(st.back(2)))
                            sp.dma_start(c_in[i][:].rearrange("p k n -> p (k n)"), columns[st.times(1)]).then_inc(c_landed.sem(st), 16)
                            if st.back(2):
                                sp.wait_ge(*out_done.at(st.back(2)))
                            load_rows(sp, st, r_in[i]).then_inc(r_landed.sem(st), 16)

                        pipeline(sp, n, [(0, load)])

                    @block.scalar
                    def _(act):
                        def tanh(st):
                            i = st.parity
                            act.wait_ge(*c_landed.at(st))
                            if st.back(2):
                                act.wait_ge(*out_turned.at(st.back(2)))
                            for k in range(H):
                                last = act.activation(act_c[i][:, k, :], c_in[i][:, k, :], ACT.Tanh,
                                                      bias=bn_shift[:, k:k + 1], scale=bn_scale[:, k:k + 1])
                            last.then_inc(tanh_done.sem(st), 1)

                        pipeline(act, n, [(1, tanh)])

                    @block.tensor
                    def _(pe):
                        def back(st):
                            pe.wait_ge(*tanh_done.at(st))
                            if st.back(2):
                                pe.wait_ge(*out_done.at(st.back(2)))
                            turn_back(pe, psums[st.parity], act_c[st.parity]).then_inc(out_turned.sem(st), 1)

                        pipeline(pe, n, [(1, back)])

                    @block.vector
                    def _(dve):
                        def add(st):
                            i = st.parity
                            dve.wait_ge(*out_turned.at(st))
                            dve.wait_ge(*r_landed.at(st))
                            if st.back(2):
                                dve.wait_ge(*out_stored.at(st.back(2)))
                            dve.tensor_tensor(o_rows[i][:], pair_rows(psums[i]), r_in[i][:], ALU.add).then_inc(out_done.sem(st), 1)

                        pipeline(dve, n, [(2, add)])

                    @block.gpsimd
                    def _(pool):
                        def send(st):
                            i = st.parity
                            if scatter:
                                if st.back(2):
                                    pool.wait_ge(*out_stored.at(st.back(2)))
                                pool.tensor_copy(last_at[i][:], last_col[:, bass.ds(st.times(TILES), TILES)]).then_inc(last_copied.sem(st), 1)
                                pool.wait_ge(*last_copied.at(st))
                            pool.wait_ge(*out_done.at(st))
                            finish(pool, st, o_rows[i], last_at[i], out_stored)

                        pipeline(pool, n, [(2, send)])
                        last_two(pool, out_stored, n)
                if not scatter:
                    used.remove(last_copied)
                close(n)

        def load_nodes(sp, st, to):
            flat = to[:].rearrange("p j d -> p (j d)")
            if isinstance(st.turn, int) and st.offset == NODE_GROUPS - 1:
                return sp.dma_start(flat[0:TAIL_PARTS], tail_group(x3_nodes))
            return sp.dma_start(flat, by_group(x3_nodes)[st.times(1)])

        def store_nodes(pool, st, rows, _, stored):
            flat = rows[:].rearrange("p j d -> p (j d)")
            if isinstance(st.turn, int) and st.offset == NODE_GROUPS - 1:
                pool.dma_start(tail_group(out), flat[0:TAIL_PARTS]).then_inc(stored.sem(st), 16)
            else:
                pool.dma_start(by_group(out)[st.times(1)], flat).then_inc(stored.sem(st), 16)

        def send_edges(pool, st, rows, at, sent):
            pool.sem_inc(pool_turns, 1)
            for j in range(TILES):
                pool.indirect_dma_start(out, bass.IndirectOffsetOnAxis(at[:, j:j + 1], 0), rows[:, j, :], None,
                                        bounds_check=N - 1, oob_is_err=False).then_inc(sent.sem(st), 16)

        last_pass(NODE_GROUPS, g_node_columns, load_nodes, store_nodes, scatter=False)
        last_pass(EDGE_GROUPS, g_edge_columns,
                  lambda sp, st, to: sp.dma_start(to[:], edge_groups(x3_rows)[st.times(1)]), send_edges, scatter=True)


def constants():
    k, i = np.arange(P)[:, None], np.arange(D)[None, :]
    cos, sin = np.cos(2 * np.pi * k * i / D), np.sin(2 * np.pi * k * i / D)
    nyquist = (-1.0) ** i
    imaginary = -sin
    imaginary[0] = nyquist
    to_freq = np.concatenate([cos, imaginary]).T
    by_real = 2 * cos / D
    by_real[0] /= 2
    by_imaginary = 2 * cos / D
    by_imaginary[0] = nyquist / D
    from_freq = np.concatenate([by_real, by_imaginary, -2 * sin / D])
    heads = np.repeat(np.eye(HEADS), D // HEADS, axis=1)
    return {"identity": np.eye(P), "to_freq": to_freq, "from_freq_t": from_freq.T, "head_rows": heads}


def kernel(**inputs):
    from concourse import bacc
    from concourse.bass_utils import run_bass_kernel_spmd

    a = {k: np.asarray(v) for k, v in inputs.items()}
    row = lambda v: v.reshape(1, -1)
    arrays = {
        "x": a["x"], "src": a["src"], "dst": a["dst"], "edge_attr": a["edge_attr_256"], "edge_weight": a["edge_weight"],
        "w_hops": a["L0_gnn_W"], "bias0": row(a["L0_gnn_bias"]), "w_gat": a["L1_gnn_W"].reshape(D, D),
        "att_src": row(a["L1_gnn_att_src"]), "att_dst": row(a["L1_gnn_att_dst"]), "bias1": row(a["L1_gnn_bias"]),
        "w1_t": a["L2_gnn_W1"].T, "b1": row(a["L2_gnn_b1"]), "w2_t": a["L2_gnn_W2"].T, "b2": row(a["L2_gnn_b2"]),
        "w_loop": a["L3_gnn_w_loop"], "w_in": a["L3_gnn_w_in"], "loop_rel": a["L3_gnn_loop_rel"],
        "w_bias": row(a["L3_gnn_w_bias"]), "bn_gamma": row(a["L3_gnn_bn_gamma"]), "bn_beta": row(a["L3_gnn_bn_beta"]),
    }
    arrays |= {k: v.astype(np.float32) for k, v in constants().items()}
    nc = bacc.Bacc("TRN2", target_bir_lowering=False, num_devices=1)
    feed, args = {}, []
    for name, value in arrays.items():
        value = np.ascontiguousarray(value)
        feed[f"in_{name}"] = value
        args.append(nc.dram_tensor(f"in_{name}", value.shape, mybir.dt.from_np(value.dtype), kind="ExternalInput").ap())
    out = nc.dram_tensor("out_rows", (N, D), F32, kind="ExternalOutput").ap()
    gnn_kernel(nc, *args, out)
    result = run_bass_kernel_spmd(nc, [feed], core_ids=[0])
    return result.results[0]["out_rows"]
```

```python
from contextlib import ExitStack

import concourse.bass as bass
import numpy as np
from concourse import mybir
from concourse.alu_op_type import AluOpType as ALU

P = 128
N = 50000
E = 12500
D = 256
H = D // P
HEADS = 8
TILES = 4
GROUP = TILES * P
NODE_GROUPS = -(-N // GROUP)
EDGE_GROUPS = -(-E // GROUP)
NODE_PAD = NODE_GROUPS * GROUP
EDGE_PAD = EDGE_GROUPS * GROUP
EDGE_TILES = EDGE_PAD // P
TAIL_NODES = N - (NODE_GROUPS - 1) * GROUP
TAIL_PARTS = TAIL_NODES // TILES
RING = 4
NO_SLOT = 20000
NO_NODE = 60000
LN_EPS = 1e-5
BN_EPS = 1e-5
SLOPE = 0.2
FAR = 1.0e30

F32 = mybir.dt.float32
BF16 = mybir.dt.bfloat16
I32 = mybir.dt.int32
ACT = mybir.ActivationFunctionType
AX_X = mybir.AxisListType.X


class Step:

    def __init__(self, turn, offset, span=RING):
        self.turn, self.offset, self.span = turn, offset, span
        self.parity = offset % 2

    def times(self, per, plus=0):
        return self.turn * (self.span * per) + (self.offset * per + plus)

    def back(self, k):
        if isinstance(self.turn, int) and self.offset < k:
            return None
        return Step(self.turn, self.offset - k, self.span)


class Signal:

    def __init__(self, nc, ctx, name, per, ring):
        self.per, self.ring = per, ring
        self.sems = [ctx.enter_context(nc.semaphore(f"{name}_{i}")) for i in range(ring)]
        self.base = [0] * ring

    def sem(self, step):
        return self.sems[step.offset % self.ring]

    def at(self, step):
        i = step.offset % self.ring
        return self.sems[i], step.turn * (self.per * step.span // self.ring) + (
            self.base[i] + self.per * (step.offset // self.ring + 1))

    def close(self, n):
        for i in range(self.ring):
            self.base[i] += self.per * len(range(i, n, self.ring))


def pipeline(eng, n, stages, span=RING):
    most = max(lag for lag, _ in stages)
    lead = -(-(most + RING) // span) * span
    turns = (n - lead) // span

    def tick(turn, i):
        for lag, stage in stages:
            if not isinstance(turn, int) or 0 <= i - lag < n:
                stage(Step(turn, i - lag, span))

    for i in range(lead):
        tick(0, i)
    turns -= lead + turns * span == n
    with eng.Fori(0, turns) as q:
        for i in range(span):
            tick(q, lead + i)
    for i in range(lead + span * turns, n + most):
        tick(0, i)


def gnn_kernel(nc, x, src, dst, edge_attr, edge_weight, w_hops, bias0, w_gat, att_src, att_dst, bias1,
               w1_t, b1, w2_t, b2, w_loop, w_in, loop_rel, w_bias, bn_gamma, bn_beta,
               identity, to_freq, attr_to_freq, from_freq_t, head_rows, out):
    def dram(name, shape, dt=F32):
        return nc.dram_tensor(name, shape, dt).ap()

    slot_of_node = dram("slot_of_node", (NODE_PAD, 1), I32)
    same_flags = dram("same_flags", (1, EDGE_PAD), BF16)
    next_flags = dram("next_flags", (1, EDGE_PAD), BF16)
    reset_flags = dram("reset_flags", (1, EDGE_PAD), BF16)
    reset_back_flags = dram("reset_back_flags", (1, EDGE_PAD), BF16)
    limit_flags = dram("limit_flags", (1, EDGE_PAD), BF16)
    rel_twice = dram("rel_twice", (1, 2 * D))
    row_cuts = dram("row_cuts", (3, D), BF16)
    xs_rows = dram("xs_rows", (EDGE_PAD, D))
    xd_rows = dram("xd_rows", (EDGE_PAD, D))
    xs_gat = dram("xs_gat", (EDGE_PAD, D))
    xs_lone = dram("xs_lone", (EDGE_PAD, D))
    hop1_rows = dram("hop1_rows", (EDGE_PAD, D))
    x1_part = dram("x1_part", (EDGE_PAD, D))
    x1_rows = dram("x1_rows", (EDGE_PAD, D))
    x2_rows = dram("x2_rows", (EDGE_PAD, D))
    x3_rows = dram("x3_rows", (EDGE_PAD, D))
    gat_columns = dram("gat_columns", (EDGE_GROUPS, P, H * GROUP))
    h2_columns = dram("h2_columns", (EDGE_GROUPS, P, H * GROUP))
    h3_columns = dram("h3_columns", (EDGE_GROUPS, P, H * GROUP))
    g_edge_columns = dram("g_edge_columns", (EDGE_GROUPS, P, H * GROUP))
    score_dst = dram("score_dst", (HEADS, EDGE_PAD))
    score_src = dram("score_src", (HEADS, EDGE_PAD))
    score_max = dram("score_max", (HEADS, EDGE_PAD))
    spread_rows = dram("spread_rows", (2 * HEADS, EDGE_PAD))
    exp_rows = dram("exp_rows", (HEADS, EDGE_PAD))
    inv_rows = dram("inv_rows", (HEADS, EDGE_PAD))
    exp_cuts = dram("exp_cuts", (3 * HEADS, EDGE_PAD), BF16)
    inv_cuts = dram("inv_cuts", (3 * HEADS, EDGE_PAD), BF16)
    norm_row = dram("norm_row", (EDGE_TILES, P))
    attr_freq = dram("attr_freq", (EDGE_GROUPS, P, 3 * GROUP))
    x3_nodes = dram("x3_nodes", (N, D))
    g_node_columns = dram("g_node_columns", (NODE_GROUPS, P, H * GROUP))

    def by_group(rows):
        full = NODE_GROUPS - 1
        return rows[0:full * GROUP].rearrange("(g p j) d -> g p (j d)", p=P, j=TILES)

    def tail_group(rows):
        at = (NODE_GROUPS - 1) * GROUP
        return rows[at:at + TAIL_NODES].rearrange("(p j) d -> p (j d)", j=TILES)

    def edge_tiles(rows):
        return rows.rearrange("(t p) d -> t p d", p=P)

    def edge_groups(rows):
        return rows.rearrange("(g j p) d -> g p j d", p=P, j=TILES)

    ctx = ExitStack()
    with ctx:
        signals = {}
        chain = ctx.enter_context(nc.semaphore("setup_chain"))
        loads = ctx.enter_context(nc.semaphore("setup_loads"))
        pool_turns = ctx.enter_context(nc.semaphore("pool_turns"))
        attr_tail = ctx.enter_context(nc.semaphore("attr_tail"))
        count = {"chain": 0, "loads": 0, "phase": 0}

        def link(eng, ins):
            count["chain"] += 1
            ins.then_inc(chain, 1)
            eng.wait_ge(chain, count["chain"])

        def move(eng, *pairs):
            for to, of in pairs:
                eng.dma_start(to, of).then_inc(loads, 16)
                count["loads"] += 16
            eng.wait_ge(loads, count["loads"])

        def tensors(stack):
            count["phase"] += 1
            phase = count["phase"]

            def sb(name, shape, dt=F32):
                return stack.enter_context(nc.sbuf_tensor(f"{name}_p{phase}", shape, dt))
            return sb

        sb = tensors(ctx)
        psum_a = ctx.enter_context(nc.psum_tensor("psum_a", [P, H, GROUP], F32))
        psum_b = ctx.enter_context(nc.psum_tensor("psum_b", [P, H, GROUP], F32))
        psum_c = ctx.enter_context(nc.psum_tensor("psum_c", [P, H, GROUP], F32))
        psum_d = ctx.enter_context(nc.psum_tensor("psum_d", [P, H, GROUP], F32))

        ident = sb("ident", [P, P])
        eps_ln = sb("eps_ln", [P, 1])
        eps_bn = sb("eps_bn", [P, 1])
        src_col = sb("src_col", [P, EDGE_TILES], I32)
        dst_col = sb("dst_col", [P, EDGE_TILES], I32)
        last_col = sb("last_col", [P, EDGE_TILES], I32)
        slot_col = sb("slot_col", [P, EDGE_TILES], I32)
        src_slot = sb("src_slot", [P, EDGE_TILES], I32)
        weight_col = sb("weight_col", [P, EDGE_TILES])
        norm_col = sb("norm_col", [P, EDGE_TILES])
        lone = sb("lone", [P, NODE_GROUPS * TILES])
        same = sb("same", [P, EDGE_PAD], BF16)
        w_hop0 = sb("w_hop0", [P, H, D])
        w_hop1 = sb("w_hop1", [P, H, D])
        gat_w = sb("gat_w", [P, H, D])
        gat_vs = sb("gat_vs", [P, H, HEADS])
        gat_vd = sb("gat_vd", [P, H, HEADS])
        head_sel = sb("head_sel", [3 * HEADS, D], BF16)
        w1 = sb("w1", [P, H, D])
        w2 = sb("w2", [P, H, D])
        w_back = sb("w_back", [P, H, D])
        w_self = sb("w_self", [P, H, D])
        freq = sb("freq", [P, H, D])
        bias0_row = sb("bias0_row", [P, D])
        lone_row = sb("lone_row", [P, D])
        bias1_col = sb("bias1_col", [P, H])
        bias_cuts = sb("bias_cuts", [3, 2 * D], BF16)
        ones_cuts = sb("ones_cuts", [3, P], BF16)
        wbias_col = sb("wbias_col", [P, H])
        gamma_col = sb("gamma_col", [P, H])
        beta_col = sb("beta_col", [P, H])
        node_stats = sb("node_stats", [P, H, (NODE_GROUPS + EDGE_GROUPS) * 6])
        bn_scale = sb("bn_scale", [P, H])
        bn_shift = sb("bn_shift", [P, H])

        with ExitStack() as own:
            sb = tensors(own)
            dst_i, next_i, prev_i, src_i = (sb(n, [EDGE_TILES, P], I32) for n in ("dst_i", "next_i", "prev_i", "src_i"))
            dst_f, next_f, prev_f, src_f, w_f, near_f, last_f = (
                sb(n, [EDGE_TILES, P]) for n in ("dst_f", "next_f", "prev_f", "src_f", "w_f", "near_f", "last_f"))
            same_b = sb("same_b", [EDGE_TILES, P], BF16)
            next_b = sb("next_b", [EDGE_TILES, P], BF16)
            reset_b = sb("reset_b", [EDGE_TILES, P], BF16)
            reset_back_b = sb("reset_back_b", [EDGE_TILES, P], BF16)
            limit_b = sb("limit_b", [EDGE_TILES, P], BF16)
            fill = sb("fill", [P, NODE_PAD // P], I32)
            zero_i = sb("zero_i", [1, NODE_PAD - N], I32)
            node_slot = sb("node_slot", [P, NODE_GROUPS * TILES], I32)
            node_slot_f = sb("node_slot_f", [P, NODE_GROUPS * TILES])
            index4 = [sb(f"index4_{b}", [P, TILES], I32) for b in range(2)]
            value4 = [sb(f"value4_{b}", [P, TILES], I32) for b in range(2)]
            att_s = sb("att_s", [P, D])
            att_d = sb("att_d", [P, D])
            prod = sb("prod", [P, D])
            circ = sb("circ", [P, H, D])
            loop_w = sb("loop_w", [P, H, D])
            in_w = sb("in_w", [P, H, D])
            back_t = sb("back_t", [P, H, D])
            attr_to = sb("attr_to", [P, H, 3 * P])
            b_row = sb("b_row", [1, 2, D])
            b_rest = sb("b_rest", [1, D])
            b_cut = sb("b_cut", [1, 3, D], BF16)
            b_wide = sb("b_wide", [1, D])
            ones_row = sb("ones_row", [1, P])
            bias1_row = sb("bias1_row", [P, D])
            head_wide = sb("head_wide", [3 * HEADS, D])
            pieces = 5
            ones_wide = sb("ones_wide", [1, EDGE_PAD // pieces], BF16)
            reset_back = sb("reset_back", [1, EDGE_PAD], BF16)
            degree = sb("degree", [1, EDGE_PAD])
            norm_t = sb("norm_t", [EDGE_TILES, P])
            attr = [sb(f"attr{i}", [P, TILES, D]) for i in range(2)]
            attr_c = [sb(f"attr_c{i}", [P, H, GROUP]) for i in range(2)]
            attr_f = [sb(f"attr_f{i}", [P, 3, GROUP]) for i in range(2)]
            full = E // P
            rest = E - full * P

            with nc.Block() as block:
                @block.vector
                def _(dve):
                    dve.memset(eps_ln[:], LN_EPS)
                    dve.memset(eps_bn[:], BN_EPS)
                    dve.memset(ones_cuts[:], 1.0)
                    dve.memset(dst_i[:], NO_NODE)
                    dve.memset(next_i[:], NO_NODE)
                    dve.memset(prev_i[:], NO_NODE)
                    dve.memset(src_i[:], 0)
                    dve.memset(w_f[:], 0.0)
                    dve.memset(ones_wide[:], 1.0)
                    for i in range(2):
                        dve.memset(attr[i][:], 0.0)
                    dve.memset(fill[:], NO_SLOT)
                    link(dve, dve.memset(zero_i[:], 0))

                @block.gpsimd
                def _(pool):
                    pool.iota(slot_col[:], [[P, EDGE_TILES]], base=0, channel_multiplier=1)

            with nc.Block() as block:
                @block.sync
                def _(sp):
                    def edge_rows(to, of):
                        return ((to[0:full, :], of[0:full * P].rearrange("(t p) -> t p", p=P)),
                                (to[full:full + 1, 0:rest], of[full * P:E].rearrange("(t p) -> t p", t=1)))

                    move(sp, (ident[:], identity),
                         *edge_rows(dst_i, dst), *edge_rows(src_i, src), *edge_rows(w_f, edge_weight),
                         (next_i[0:full, :], dst[1:full * P + 1].rearrange("(t p) -> t p", p=P)),
                         (next_i[full:full + 1, 0:rest - 1], dst[full * P + 1:E].rearrange("(t p) -> t p", t=1)),
                         (prev_i[0:1, 1:P], dst[0:P - 1].rearrange("(t p) -> t p", t=1)),
                         (prev_i[1:full, :], dst[P - 1:full * P - 1].rearrange("(t p) -> t p", p=P)),
                         (prev_i[full:full + 1, 0:rest], dst[full * P - 1:E - 1].rearrange("(t p) -> t p", t=1)),
                         (slot_of_node.rearrange("(p q) o -> p (q o)", p=P), fill[:]),
                         (xs_rows[NODE_GROUPS * P:EDGE_PAD], x[0:EDGE_PAD - NODE_GROUPS * P]),
                         (xd_rows[NODE_GROUPS * P:EDGE_PAD], x[0:EDGE_PAD - NODE_GROUPS * P]),
                         (rel_twice[:, 0:D], loop_rel), (rel_twice[:, D:2 * D], loop_rel),
                         *((to[:], of.rearrange("(k p) n -> p k n", p=P)) for to, of in (
                             (w_hop0, w_hops[0]), (w_hop1, w_hops[1]), (gat_w, w_gat), (w1, w1_t), (w2, w2_t),
                             (freq, to_freq), (loop_w, w_loop), (in_w, w_in), (back_t, from_freq_t), (attr_to, attr_to_freq))),
                         (head_wide[:], head_rows),
                         (b_row[:, 0, :], b1), (b_row[:, 1, :], b2),
                         *((to[:], of.to_broadcast([P, D])) for to, of in (
                             (att_s, att_src), (att_d, att_dst), (bias0_row, bias0), (bias1_row, bias1))))

                @block.scalar
                def _(act):
                    with nc.allow_non_contiguous_dma(reason="one value per partition"):
                        for to, of in ((bias1_col, bias1), (wbias_col, w_bias), (gamma_col, bn_gamma), (beta_col, bn_beta)):
                            act.dma_start(to[:], of.rearrange("o (k p) -> p (o k)", p=P)).then_inc(chain, 16)
                            count["chain"] += 16
                    act.wait_ge(chain, count["chain"])

            with nc.Block() as block:
                @block.sync
                def _(sp):
                    move(sp, (slot_of_node[N:NODE_PAD].rearrange("(o q) i -> o (q i)", o=1), zero_i[:]),
                         *((circ[:, k, :], bass.AP(rel_twice.tensor, k * P, [[1, P], [1, D]])) for k in range(H)))

                @block.vector
                def _(dve):
                    dve.tensor_copy(dst_f[:], dst_i[:])
                    dve.tensor_copy(next_f[:], next_i[:])
                    dve.tensor_copy(prev_f[:], prev_i[:])
                    link(dve, dve.tensor_copy(src_f[:], src_i[:]))
                    dve.tensor_tensor(same_b[:], dst_f[:], prev_f[:], ALU.is_equal)
                    dve.tensor_tensor(next_b[:], dst_f[:], next_f[:], ALU.is_equal)
                    link(dve, dve.tensor_scalar(near_f[:], dst_f[:], float(N - 1), None, ALU.min))
                    dve.tensor_scalar(reset_b[:], same_b[:], FAR, -FAR, ALU.mult, ALU.add)
                    dve.tensor_scalar(reset_back_b[:], next_b[:], FAR, -FAR, ALU.mult, ALU.add)
                    dve.tensor_scalar(limit_b[:], next_b[:], -2 * FAR, FAR, ALU.mult, ALU.add)
                    link(dve, dve.scalar_tensor_tensor(last_f[:], next_b[:], float(NO_NODE), dst_f[:], ALU.mult, ALU.add))
                    for att, v in ((att_s, gat_vs), (att_d, gat_vd)):
                        for k in range(H):
                            link(dve, dve.tensor_tensor(prod[:], gat_w[:, k, :], att[:], ALU.mult))
                            link(dve, dve.tensor_reduce(v[:, k, :], prod[:].rearrange("p (h d) -> p h d", h=HEADS), AX_X, ALU.add))
                    dve.tensor_copy(head_sel[:], head_wide[:])
                    link(dve, dve.tensor_scalar(prod[:], bias1_row[:], 0.0, None, ALU.max))
                    link(dve, dve.tensor_tensor(lone_row[:], prod[:], bias0_row[:], ALU.add))
                    link(dve, dve.tensor_tensor(b_rest[:], b_row[:, 0, :], b_row[:, 1, :], ALU.add))
                    for cut in range(3):
                        link(dve, dve.tensor_copy(b_cut[:, cut, :], b_rest[:]))
                        link(dve, dve.tensor_copy(b_wide[:], b_cut[:, cut, :]))
                        link(dve, dve.tensor_tensor(b_rest[:], b_rest[:], b_wide[:], ALU.subtract))

            with nc.Block() as block:
                @block.tensor
                def _(pe):
                    for i, rows in enumerate((src_f, near_f, last_f, w_f)):
                        pe.transpose(psum_a[:, 0, i * P:i * P + EDGE_TILES], rows[:], ident[0:EDGE_TILES, 0:EDGE_TILES])
                    for half in range(H):
                        for k in range(H):
                            pe.matmul(psum_b[:, half, 0:D], circ[:, k, half * P:(half + 1) * P], loop_w[:, k, :],
                                      start=k == 0, stop=k == H - 1)
                    for part in range(H):
                        for k in range(H):
                            last = pe.matmul(psum_c[:, part, 0:D],
                                             back_t[:, k, part * P:(part + 1) * P], in_w[:, k, :],
                                             start=k == 0, stop=k == H - 1)
                    link(pe, last)

                @block.sync
                def _(sp):
                    move(sp, *((flags.rearrange("o (t p) -> (o t) p", p=P), rows[:]) for flags, rows in (
                             (same_flags, same_b), (next_flags, next_b), (reset_flags, reset_b),
                             (reset_back_flags, reset_back_b), (limit_flags, limit_b))),
                         (row_cuts.rearrange("(o c) d -> o c d", o=1), b_cut[:]))

            with nc.Block() as block:
                @block.vector
                def _(dve):
                    for i, to in enumerate((src_col, dst_col, last_col, weight_col)):
                        dve.tensor_copy(to[:], psum_a[:, 0, i * P:i * P + EDGE_TILES])
                    for half in range(H):
                        dve.tensor_copy(w_self[:, half, :], psum_b[:, half, 0:D])
                    for part in range(H):
                        last = dve.tensor_copy(w_back[:, part, :], psum_c[:, part, 0:D])
                    link(dve, last)

                @block.sync
                def _(sp):
                    move(sp, (same[:], same_flags.to_broadcast([P, EDGE_PAD])), (reset_back[:], reset_back_flags),
                         (bias_cuts[:, 0:D], row_cuts), (bias_cuts[:, D:2 * D], row_cuts))

            def signal(name, per=1, ring=1):
                if name not in signals:
                    signals[name] = Signal(nc, ctx, name, per, ring)
                assert (signals[name].per, signals[name].ring) == (per, ring), name
                used.append(signals[name])
                return signals[name]

            def close(n):
                for s in used:
                    s.close(n)
                used.clear()

            used = []
            slots_sent = signal("slots_sent", 16 * TILES, ring=2)
            index_copied = signal("index_copied", 2)
            attr_landed = signal("attr_landed", 16, ring=2)
            attr_turned = signal("attr_turned")
            attr_out = signal("attr_out")
            attr_transformed = signal("attr_transformed")
            attr_freq_out = signal("attr_freq_out")
            attr_stored = signal("attr_stored", 16, ring=2)
            with nc.Block() as block:
                @block.gpsimd
                def _(pool):
                    def scatter(st):
                        b = st.parity
                        if st.back(2):
                            pool.wait_ge(*slots_sent.at(st.back(2)))
                        pool.tensor_copy(index4[b][:], last_col[:, bass.ds(st.times(TILES), TILES)]).then_inc(index_copied.sem(st), 1)
                        pool.tensor_copy(value4[b][:], slot_col[:, bass.ds(st.times(TILES), TILES)]).then_inc(index_copied.sem(st), 1)
                        pool.wait_ge(*index_copied.at(st))
                        pool.sem_inc(pool_turns, 1)
                        for j in range(TILES):
                            pool.indirect_dma_start(
                                slot_of_node, bass.IndirectOffsetOnAxis(index4[b][:, j:j + 1], 0), value4[b][:, j:j + 1], None,
                                bounds_check=N - 1, oob_is_err=False).then_inc(slots_sent.sem(st), 16)

                    pipeline(pool, EDGE_GROUPS, [(0, scatter)])
                    pool.wait_ge(*slots_sent.at(Step(0, EDGE_GROUPS - 1)))
                    pool.wait_ge(*slots_sent.at(Step(0, EDGE_GROUPS - 2)))

                @block.vector
                def _(dve):
                    for i in range(pieces):
                        at = i * EDGE_PAD // pieces
                        piece = slice(at, at + EDGE_PAD // pieces)
                        link(dve, dve.tensor_tensor_scan(degree[:, piece], same[0:1, piece], ones_wide[:],
                                                         degree[:, at - 1:at] if i else 0.0, ALU.mult, ALU.add))
                    link(dve, dve.tensor_tensor_scan(degree[:, ::-1], reset_back[:, ::-1], degree[:, ::-1], 0.0, ALU.add, ALU.max))

                @block.sync
                def _(sp):
                    attr_groups = edge_groups(edge_attr[0:(EDGE_GROUPS - 1) * GROUP])

                    def load(st):
                        i = st.parity
                        if st.back(2):
                            sp.wait_ge(*attr_turned.at(st.back(2)))
                        if isinstance(st.turn, int) and st.offset == EDGE_GROUPS - 1:
                            at = (EDGE_GROUPS - 1) * GROUP
                            whole = (E - at) // P
                            sp.dma_start(attr[i][0:E - at - whole * P, whole, :], edge_attr[at + whole * P:E]).then_inc(attr_tail, 16)
                            sp.wait_ge(attr_tail, 16)
                            sp.dma_start(attr[i][:, 0:whole, :], edge_attr[at:at + whole * P].rearrange("(j p) d -> p j d", p=P))\
                              .then_inc(attr_landed.sem(st), 16)
                        else:
                            sp.dma_start(attr[i][:], attr_groups[st.times(1)]).then_inc(attr_landed.sem(st), 16)

                    def store(st):
                        sp.wait_ge(*attr_freq_out.at(st))
                        sp.dma_start(attr_freq[st.times(1)], attr_f[st.parity][:].rearrange("p k n -> p (k n)"))\
                          .then_inc(attr_stored.sem(st), 16)

                    pipeline(sp, EDGE_GROUPS, [(0, load), (4, store)])
                    sp.wait_ge(*attr_stored.at(Step(0, EDGE_GROUPS - 1)))
                    sp.wait_ge(*attr_stored.at(Step(0, EDGE_GROUPS - 2)))

                @block.tensor
                def _(pe):
                    def turn_attr(st):
                        pe.wait_ge(*attr_landed.at(st))
                        if st.back(1):
                            pe.wait_ge(*attr_out.at(st.back(1)))
                        for k in range(H):
                            for j in range(TILES):
                                last = pe.transpose(psum_a[:, k, j * P:(j + 1) * P], attr[st.parity][:, j, k * P:(k + 1) * P], ident[:])
                        last.then_inc(attr_turned.sem(st), 1)

                    def transform(st):
                        pe.wait_ge(*attr_out.at(st))
                        if st.back(2):
                            pe.wait_ge(*attr_freq_out.at(st.back(2)))
                        for part in range(3):
                            for k in range(H):
                                last = pe.matmul((psum_b, psum_d)[st.parity][:, part, :] if part < 2 else psum_c[:, st.parity, :], attr_to[:, k, part * P:(part + 1) * P],
                                                 attr_c[st.parity][:, k, :], start=k == 0, stop=k == H - 1)
                        last.then_inc(attr_transformed.sem(st), 1)

                    pipeline(pe, EDGE_GROUPS, [(1, turn_attr), (2, transform)])

                @block.scalar
                def _(act):
                    def columns_out(st):
                        act.wait_ge(*attr_turned.at(st))
                        if st.back(2):
                            act.wait_ge(*attr_transformed.at(st.back(2)))
                        act.activation(attr_c[st.parity][:], psum_a[:], ACT.Copy).then_inc(attr_out.sem(st), 1)

                    def freq_out(st):
                        act.wait_ge(*attr_transformed.at(st))
                        if st.back(2):
                            act.wait_ge(*attr_stored.at(st.back(2)))
                        act.activation(attr_f[st.parity][:, 0:2, :], (psum_b, psum_d)[st.parity][:], ACT.Copy)
                        act.activation(attr_f[st.parity][:, 2, :], psum_c[:, st.parity, :], ACT.Copy).then_inc(attr_freq_out.sem(st), 1)

                    pipeline(act, EDGE_GROUPS, [(3, freq_out), (1, columns_out)])
            close(EDGE_GROUPS)

            with nc.Block() as block:
                @block.sync
                def _(sp):
                    move(sp, (norm_row.rearrange("(o t) p -> o (t p)", o=1), degree[:]))
                    move(sp, (norm_t[:], norm_row))

            with nc.Block() as block:
                @block.scalar
                def _(act):
                    link(act, act.activation(norm_t[:], norm_t[:], ACT.Sqrt))

            with nc.Block() as block:
                @block.vector
                def _(dve):
                    link(dve, dve.tensor_scalar(norm_t[:], norm_t[:], 1.0, None, ALU.max))
                    link(dve, dve.reciprocal(norm_t[:], norm_t[:]))

            with nc.Block() as block:
                @block.tensor
                def _(pe):
                    link(pe, pe.transpose(psum_a[:, 0, 0:EDGE_TILES], norm_t[:], ident[0:EDGE_TILES, 0:EDGE_TILES]))

            with nc.Block() as block:
                @block.vector
                def _(dve):
                    link(dve, dve.tensor_copy(norm_col[:], psum_a[:, 0, 0:EDGE_TILES]))

            with nc.Block() as block:
                @block.vector
                def _(dve):
                    link(dve, dve.memset(src_slot[:], NO_SLOT))

                @block.sync
                def _(sp):
                    move(sp, (node_slot[:].rearrange("p (g j) -> p g j", j=TILES),
                              slot_of_node.rearrange("(g p j) o -> p g (j o)", p=P, j=TILES)))

            with nc.Block() as block:
                @block.vector
                def _(dve):
                    link(dve, dve.tensor_copy(node_slot_f[:], node_slot[:]))
                    link(dve, dve.tensor_scalar(lone[:], node_slot_f[:], float(NO_SLOT), None, ALU.is_equal))

        class Norm:

            def __init__(self, sb, name, rows, rows_ready, psum, taken, scale=None, weight=None):
                self.rows, self.rows_ready, self.psum, self.taken = rows, rows_ready, psum, taken
                self.scale, self.weight = scale, weight
                two = range(2)
                self.stats = [sb(f"{name}_stats{b}", [P, TILES, 6]) for b in two]
                self.mean2 = [sb(f"{name}_mean2_{b}", [P, TILES]) for b in two]
                self.apart = [sb(f"{name}_apart{b}", [P, TILES]) for b in two]
                self.var = [sb(f"{name}_var{b}", [P, TILES]) for b in two]
                self.dev = [sb(f"{name}_dev{b}", [P, TILES]) for b in two]
                self.inv = [sb(f"{name}_inv{b}", [P, TILES]) for b in two]
                self.off = [sb(f"{name}_off{b}", [P, TILES]) for b in two]
                self.h = [sb(f"{name}_h{b}", [P, TILES, D]) for b in two]
                self.pair_done = signal(f"{name}_pair_done", 3)
                self.moments_done = signal(f"{name}_moments_done")
                self.dev_done = signal(f"{name}_dev_done")
                self.inv_done = signal(f"{name}_scaled_inv_done", 3) if scale else signal(f"{name}_inv_done", 2)
                self.h_done = signal(f"{name}_h_done")
                if weight:
                    self.weighted = signal(f"{name}_weighted")
                self.turned = signal(f"{name}_turned")

            def halves(self, dve, st):
                dve.wait_ge(*self.rows_ready.at(st))
                for j in range(TILES):
                    last = dve.bn_stats(self.stats[st.parity][:, j, :], self.rows[st.offset % len(self.rows)][:, j, :])
                last.then_inc(self.pair_done.sem(st), 1)

            def add_halves(self, dve, st):
                b = st.parity
                sem, value = self.pair_done.at(st)
                even, odd = self.stats[b][:, :, 0:3], self.stats[b][:, :, 3:6]
                dve.wait_ge(sem, value - 2)
                dve.tensor_tensor(self.apart[b][:], even[:, :, 1], odd[:, :, 1], ALU.subtract)
                dve.tensor_tensor(self.mean2[b][:], even[:, :, 1], odd[:, :, 1], ALU.add)
                dve.tensor_tensor(self.var[b][:], even[:, :, 2], odd[:, :, 2], ALU.add).then_inc(sem, 1)

            def square_apart(self, dve, st):
                b = st.parity
                sem, value = self.pair_done.at(st)
                dve.wait_ge(sem, value - 1)
                dve.scalar_tensor_tensor(self.apart[b][:], self.apart[b][:], D / 4.0, self.apart[b][:], ALU.mult, ALU.mult)\
                   .then_inc(sem, 1)

            def variance(self, dve, st):
                b = st.parity
                dve.wait_ge(*self.pair_done.at(st))
                dve.tensor_tensor(self.var[b][:], self.var[b][:], self.apart[b][:], ALU.add).then_inc(self.moments_done.sem(st), 1)

            def moments(self, dve, lag):
                return [(lag, lambda st, step=step: step(dve, st))
                        for step in (self.halves, self.add_halves, self.square_apart, self.variance)]

            def deviation(self, act, st):
                b = st.parity
                act.wait_ge(*self.moments_done.at(st))
                act.activation(self.dev[b][:], self.var[b][:], ACT.Sqrt, bias=eps_ln[:], scale=1.0 / D).then_inc(self.dev_done.sem(st), 1)

            def invert(self, dve, st):
                b = st.parity
                dve.wait_ge(*self.dev_done.at(st))
                if st.back(2):
                    dve.wait_ge(*self.h_done.at(st.back(2)))
                dve.reciprocal(self.inv[b][:], self.dev[b][:]).then_inc(self.inv_done.sem(st), 1)

            def scale_inverse(self, dve, st):
                b, (sem, value) = st.parity, self.inv_done.at(st)
                dve.wait_ge(sem, value - 2)
                dve.tensor_tensor(self.inv[b][:], self.inv[b][:], self.scale(st), ALU.mult).then_inc(sem, 1)

            def offset(self, dve, st):
                b, (sem, value) = st.parity, self.inv_done.at(st)
                dve.wait_ge(sem, value - 1)
                dve.scalar_tensor_tensor(self.off[b][:], self.mean2[b][:], -0.5, self.inv[b][:], ALU.mult, ALU.mult)\
                   .then_inc(sem, 1)

            def inverse(self, dve, lag):
                steps = (self.invert, self.scale_inverse, self.offset) if self.scale else (self.invert, self.offset)
                return [(lag, lambda st, step=step: step(dve, st)) for step in steps]

            def normalise(self, dve, st):
                b = st.parity
                dve.wait_ge(*self.inv_done.at(st))
                if st.back(2):
                    dve.wait_ge(*self.turned.at(st.back(2)))
                rows = self.rows[st.offset % len(self.rows)]
                for j in range(TILES):
                    last = dve.tensor_scalar(self.h[b][:, j, :], rows[:, j, :], self.inv[b][:, j:j + 1],
                                             self.off[b][:, j:j + 1], ALU.mult, ALU.add)
                last.then_inc(self.h_done.sem(st), 1)

            def normalise_relu(self, act, st):
                b = st.parity
                act.wait_ge(*self.inv_done.at(st))
                if st.back(2):
                    act.wait_ge(*self.turned.at(st.back(2)))
                for j in range(TILES):
                    last = act.activation(self.h[b][:, j, :], self.rows[st.offset % len(self.rows)][:, j, :], ACT.Relu,
                                          bias=self.off[b][:, j:j + 1], scale=self.inv[b][:, j:j + 1])
                last.then_inc(self.h_done.sem(st), 1)

            def weigh(self, dve, st):
                b = st.parity
                dve.wait_ge(*self.h_done.at(st))
                w = self.weight(st)
                for j in range(TILES):
                    last = dve.tensor_scalar(self.h[b][:, j, :], self.h[b][:, j, :], w(j), None, ALU.mult)
                last.then_inc(self.weighted.sem(st), 1)

            def turn(self, pe, st):
                b = st.parity
                pe.wait_ge(*(self.weighted if self.weight else self.h_done).at(st))
                if st.back(1):
                    pe.wait_ge(*self.taken.at(st.back(1)))
                for k in range(H):
                    for j in range(TILES):
                        last = pe.transpose(self.psum[:, k, j * P:(j + 1) * P], self.h[b][:, j, k * P:(k + 1) * P], ident[:])
                last.then_inc(self.turned.sem(st), 1)

        def woven(a, b):
            out = []
            for i in range(max(len(a), len(b))):
                out += a[i:i + 1] + b[i:i + 1]
            return out

        def rows_product(pe, to, columns, weights, start=True, stop=True):
            for j in range(TILES):
                for k in range(H):
                    last = pe.matmul(to[:, j // 2, (j % 2) * D:(j % 2 + 1) * D], columns[:, k, j * P:(j + 1) * P],
                                     weights[:, k, :], start=start and k == 0, stop=stop and k == H - 1,
                                     skip_group_check=True)
            return last

        def columns_product(pe, to, weights, columns, start=True, stop=True):
            parts = columns.shape[1]
            for half in range(H):
                for k in range(parts):
                    last = pe.matmul(to[:, half, :], weights[:, k, half * P:(half + 1) * P], columns[:, k, :],
                                     start=start and k == 0, stop=stop and k == parts - 1, skip_group_check=True)
            return last

        def last_two(eng, sig, n):
            eng.wait_ge(*sig.at(Step(0, n - 2)))
            eng.wait_ge(*sig.at(Step(0, n - 1)))

        def tile_rows(t):
            return t[:].rearrange("p (j d) -> p j d", j=TILES)

        def pair_rows(psum):
            return psum[:].rearrange("p h (j d) -> p (h j) d", j=2)

        class Tail:

            def __init__(self, sb, product_done, base, base_ready, out_free):
                two = range(2)
                self.product_done, self.base, self.base_ready, self.out_free = product_done, base, base_ready, out_free
                self.leaky = [sb(f"tail_leaky{b}", [P, TILES, D]) for b in two]
                self.square = [sb(f"tail_square{b}", [P, TILES, D]) for b in two]
                self.total = [sb(f"tail_total{b}", [P, TILES]) for b in two]
                self.length = [sb(f"tail_length{b}", [P, TILES]) for b in two]
                self.inv = [sb(f"tail_inv{b}", [P, TILES]) for b in two]
                self.x3 = [sb(f"tail_x3{b}", [P, TILES, D]) for b in two]
                self.slope_done = signal("tail_slope_done")
                self.leaky_done = signal("tail_leaky_done")
                self.length_done = signal("tail_length_done", 2)
                self.inv_done = signal("tail_inv_done", 2)
                self.x3_done = signal("tail_x3_done")

            def slope(self, act, st):
                b = st.parity
                act.wait_ge(*self.product_done.at(st))
                if st.back(2):
                    act.wait_ge(*self.x3_done.at(st.back(2)))
                act.activation(self.leaky[b][:], pair_rows(psum_b), ACT.Copy, scale=SLOPE).then_inc(self.slope_done.sem(st), 1)

            def leak(self, dve, st):
                b = st.parity
                dve.wait_ge(*self.slope_done.at(st))
                dve.tensor_tensor(self.leaky[b][:], pair_rows(psum_b), self.leaky[b][:], ALU.max).then_inc(self.leaky_done.sem(st), 1)

            def square_up(self, act, st):
                b = st.parity
                act.wait_ge(*self.leaky_done.at(st))
                sem, value = self.length_done.at(st)
                for j in range(TILES):
                    last = act.activation(self.square[b][:, j, :], self.leaky[b][:, j, :], ACT.Square, accum_out=self.total[b][:, j:j + 1])
                last.then_inc(sem, 1)
                act.wait_ge(sem, value - 1)
                act.activation(self.length[b][:], self.total[b][:], ACT.Sqrt).then_inc(sem, 1)

            def bound_length(self, dve, st):
                b = st.parity
                dve.wait_ge(*self.length_done.at(st))
                if st.back(2):
                    dve.wait_ge(*self.x3_done.at(st.back(2)))
                dve.tensor_scalar(self.inv[b][:], self.length[b][:], 1e-12, None, ALU.max).then_inc(self.inv_done.sem(st), 1)

            def invert(self, dve, st):
                b, (sem, value) = st.parity, self.inv_done.at(st)
                dve.wait_ge(sem, value - 1)
                dve.reciprocal(self.inv[b][:], self.inv[b][:]).then_inc(sem, 1)

            def inverse(self, dve, lag):
                return [(lag, lambda st: self.bound_length(dve, st)), (lag, lambda st: self.invert(dve, st))]

            def residual(self, dve, st):
                b = st.parity
                dve.wait_ge(*self.inv_done.at(st))
                if self.base_ready:
                    dve.wait_ge(*self.base_ready.at(st))
                for sig in self.out_free:
                    if st.back(2):
                        dve.wait_ge(*sig.at(st.back(2)))
                for j in range(TILES):
                    last = dve.scalar_tensor_tensor(self.x3[b][:, j, :], self.leaky[b][:, j, :], self.inv[b][:, j:j + 1],
                                                    self.base[b][:, j, :], ALU.mult, ALU.add)
                last.then_inc(self.x3_done.sem(st), 1)

        with ExitStack() as own:
            sb = tensors(own)
            two = range(2)
            n = NODE_GROUPS
            x_in = [sb(f"x_in{b}", [P, TILES * D]) for b in two]
            x2 = [sb(f"x2_{b}", [P, TILES, D]) for b in range(RING)]
            h2c = [sb(f"h2c{b}", [P, H, GROUP]) for b in two]
            h3c = [sb(f"h3c{b}", [P, H, GROUP]) for b in two]
            gc = [sb(f"gc{b}", [P, H, GROUP]) for b in two]
            x_landed = signal("x_landed", 16, ring=2)
            x2_done = signal("x2_done")
            h2c_done = signal("h2c_done")
            y_done = signal("y_done")
            x3_stored = signal("x3_stored", 16, ring=2)
            h3c_done = signal("h3c_done")
            g_done = signal("g_done")
            g_stats = signal("g_stats")
            gc_done = signal("gc_done")
            g_stored = signal("g_stored", 16, ring=2)
            norm2 = Norm(sb, "norm", x2, x2_done, psum_a, h2c_done)
            norm3 = Norm(sb, "norm3", None, None, psum_c, h3c_done,
                         scale=lambda st: lone[:, bass.ds(st.times(TILES), TILES)])
            tail = Tail(sb, y_done, x2, None, [x3_stored, norm3.h_done])
            scaled = signal("scaled")
            norm3.rows, norm3.rows_ready = tail.x3, tail.x3_done

            x_groups, x3_groups = by_group(x), by_group(x3_nodes)
            edges_copied = signal("edges_copied", 2)
            edges_fetched = signal("edges_fetched", 48, ring=RING)
            edges_stored = signal("edges_stored", 32, ring=RING)
            slot_kept = signal("slot_kept")
            src_at, dst_at, slot_of = ([sb(f"{name}{b}", [P, 1], I32) for b in range(RING)] for name in ("src_at", "dst_at", "slot_of"))
            x_src, x_dst = ([sb(f"{name}{b}", [P, D]) for b in range(RING)] for name in ("x_src", "x_dst"))

            with nc.Block() as block:
                @block.sync
                def _(sp):
                    def load(st):
                        if st.back(2):
                            sp.wait_ge(*x2_done.at(st.back(2)))
                        if isinstance(st.turn, int) and st.offset == n - 1:
                            sp.dma_start(x_in[st.parity][0:TAIL_PARTS, :], tail_group(x)).then_inc(x_landed.sem(st), 16)
                        else:
                            sp.dma_start(x_in[st.parity][:], x_groups[st.times(1)]).then_inc(x_landed.sem(st), 16)

                    def store_edges(st):
                        b = st.offset % RING
                        sp.wait_ge(*edges_fetched.at(st))
                        sp.dma_start(edge_tiles(xs_rows)[st.times(1)], x_src[b][:]).then_inc(edges_stored.sem(st), 16)
                        sp.dma_start(edge_tiles(xd_rows)[st.times(1)], x_dst[b][:]).then_inc(edges_stored.sem(st), 16)

                    def store_x3(st):
                        sp.wait_ge(*tail.x3_done.at(st))
                        rows = tail.x3[st.parity][:].rearrange("p j d -> p (j d)")
                        if isinstance(st.turn, int) and st.offset == n - 1:
                            sp.dma_start(tail_group(x3_nodes), rows[0:TAIL_PARTS]).then_inc(x3_stored.sem(st), 16)
                        else:
                            sp.dma_start(x3_groups[st.times(1)], rows).then_inc(x3_stored.sem(st), 16)

                    def store_g(st):
                        sp.wait_ge(*gc_done.at(st))
                        sp.dma_start(g_node_columns[st.times(1)], gc[st.parity][:].rearrange("p k n -> p (k n)"))\
                          .then_inc(g_stored.sem(st), 16)

                    pipeline(sp, n, [(0, load), (6, store_x3), (2, store_edges), (10, store_g)])
                    last_two(sp, x3_stored, n)
                    last_two(sp, g_stored, n)
                    for i in range(RING):
                        sp.wait_ge(*edges_stored.at(Step(0, n - 1 - i)))

                @block.gpsimd
                def _(pool):
                    def add(st):
                        pool.wait_ge(*x_landed.at(st))
                        if st.back(RING):
                            pool.wait_ge(*tail.x3_done.at(st.back(RING)))
                        pool.tensor_tensor(x2[st.offset % RING][:], tile_rows(x_in[st.parity]), lone_row[:].unsqueeze(1).to_broadcast([P, TILES, D]), ALU.add)\
                            .then_inc(x2_done.sem(st), 1)

                    def residual(st):
                        b = st.parity
                        pool.wait_ge(*scaled.at(st))
                        if st.back(2):
                            pool.wait_ge(*x3_stored.at(st.back(2)))
                            pool.wait_ge(*norm3.h_done.at(st.back(2)))
                        pool.tensor_tensor(tail.x3[b][:], tail.leaky[b][:], x2[st.offset % RING][:], ALU.add)\
                            .then_inc(tail.x3_done.sem(st), 1)

                    def fetch_edges(st):
                        b = st.offset % RING
                        if st.back(RING):
                            pool.wait_ge(*edges_stored.at(st.back(RING)))
                            pool.wait_ge(*slot_kept.at(st.back(RING)))
                        pool.tensor_copy(src_at[b][:], src_col[:, bass.ds(st.times(1), 1)]).then_inc(edges_copied.sem(st), 1)
                        pool.tensor_copy(dst_at[b][:], dst_col[:, bass.ds(st.times(1), 1)]).then_inc(edges_copied.sem(st), 1)
                        pool.wait_ge(*edges_copied.at(st))
                        pool.sem_inc(pool_turns, 1)
                        for to, at, table in ((x_src[b], src_at[b], x), (x_dst[b], dst_at[b], x), (slot_of[b], src_at[b], slot_of_node)):
                            pool.indirect_dma_start(to[:], None, table, bass.IndirectOffsetOnAxis(at[:], 0),
                                                    bounds_check=N - 1, oob_is_err=False).then_inc(edges_fetched.sem(st), 16)

                    pipeline(pool, n, [(0, fetch_edges), (5, residual), (1, add)])

                @block.scalar
                def _(act):
                    def h2_out(st):
                        act.wait_ge(*norm2.turned.at(st))
                        if st.back(2):
                            act.wait_ge(*y_done.at(st.back(2)))
                        act.activation(h2c[st.parity][:], psum_a[:], ACT.Relu).then_inc(h2c_done.sem(st), 1)

                    def g_out(st):
                        act.wait_ge(*g_done.at(st))
                        if st.back(2):
                            act.wait_ge(*g_stored.at(st.back(2)))
                            act.wait_ge(*g_stats.at(st.back(2)))
                        act.activation(gc[st.parity][:], psum_d[:], ACT.Copy).then_inc(gc_done.sem(st), 1)

                    def h3_out(st):
                        act.wait_ge(*norm3.turned.at(st))
                        if st.back(2):
                            act.wait_ge(*g_done.at(st.back(2)))
                        act.activation(h3c[st.parity][:], psum_c[:], ACT.Relu).then_inc(h3c_done.sem(st), 1)

                    def shorten(st):
                        b = st.parity
                        act.wait_ge(*tail.inv_done.at(st))
                        for j in range(TILES):
                            last = act.activation(tail.leaky[b][:, j, :], tail.leaky[b][:, j, :], ACT.Copy,
                                                  scale=tail.inv[b][:, j:j + 1])
                        last.then_inc(scaled.sem(st), 1)

                    pipeline(act, n, [(9, g_out), (8, h3_out), (5, shorten),
                                      (4, lambda st: tail.slope(act, st)),
                                      (4, lambda st: tail.square_up(act, st)),
                                      (3, h2_out),
                                      (2, lambda st: norm2.deviation(act, st)),
                                      (6, lambda st: norm3.deviation(act, st))])

                @block.vector
                def _(dve):
                    def stats(st):
                        dve.wait_ge(*gc_done.at(st))
                        for k in range(H):
                            last = dve.bn_stats(node_stats[:, k, bass.ds(st.times(6), 6)], gc[st.parity][:, k, :])
                        last.then_inc(g_stats.sem(st), 1)

                    def keep_slots(st):
                        dve.wait_ge(*edges_fetched.at(st))
                        dve.tensor_copy(src_slot[:, bass.ds(st.times(1), 1)], slot_of[st.offset % RING][:]).then_inc(slot_kept.sem(st), 1)

                    pipeline(dve, n, [*woven(tail.inverse(dve, 5), woven(norm2.inverse(dve, 3), norm3.inverse(dve, 7))),
                                      (3, lambda st: norm2.normalise(dve, st)),
                                      (7, lambda st: norm3.normalise(dve, st)),
                                      *woven(norm2.moments(dve, 2), [(4, lambda st: tail.leak(dve, st)), *norm3.moments(dve, 6)]),
                                      (9, stats), (2, keep_slots)])
                    dve.wait_ge(*g_stats.at(Step(0, n - 1)))
                    dve.wait_ge(*slot_kept.at(Step(0, n - 1)))

                @block.tensor
                def _(pe):
                    def product(st):
                        pe.wait_ge(*h2c_done.at(st))
                        if st.back(1):
                            pe.wait_ge(*tail.leaky_done.at(st.back(1)))
                        for half in range(2):
                            pe.matmul(psum_b[:, half, :], ones_cuts[:], bias_cuts[:], start=True, stop=False, skip_group_check=True)
                        rows_product(pe, psum_b, h2c[st.parity], w1, start=False).then_inc(y_done.sem(st), 1)

                    def self_product(st):
                        pe.wait_ge(*h3c_done.at(st))
                        if st.back(1):
                            pe.wait_ge(*gc_done.at(st.back(1)))
                        columns_product(pe, psum_d, w_self, h3c[st.parity]).then_inc(g_done.sem(st), 1)

                    pipeline(pe, n, [(4, product), (8, self_product), (3, lambda st: norm2.turn(pe, st)), (7, lambda st: norm3.turn(pe, st))])
            close(n)

        class Gather:

            def __init__(self, sb, name, table, index, free, bound, zero=False):
                self.table, self.index, self.free, self.bound, self.zero = table, index, free, bound, zero
                self.rows = [sb(f"{name}_rows{b}", [P, TILES, D]) for b in range(RING)]
                self.at = [sb(f"{name}_at{b}", [P, TILES], I32) for b in range(RING)]
                self.index_done = signal("index_done")
                self.ready = signal("gathered", 16 * TILES, ring=RING)
                if zero:
                    self.zeroed = signal(f"{name}_zeroed")

            def fetch(self, pool, st):
                b = st.offset % RING
                for sig in self.free:
                    if st.back(RING):
                        pool.wait_ge(*sig.at(st.back(RING)))
                pool.tensor_copy(self.at[b][:], self.index[:, bass.ds(st.times(TILES), TILES)]).then_inc(self.index_done.sem(st), 1)
                if self.zero:
                    pool.memset(self.rows[b][:], 0.0).then_inc(self.zeroed.sem(st), 1)
                    pool.wait_ge(*self.zeroed.at(st))
                pool.wait_ge(*self.index_done.at(st))
                pool.sem_inc(pool_turns, 1)
                for j in range(TILES):
                    pool.indirect_dma_start(self.rows[b][:, j, :], None, self.table,
                                            bass.IndirectOffsetOnAxis(self.at[b][:, j:j + 1], 0),
                                            bounds_check=self.bound, oob_is_err=False).then_inc(self.ready.sem(st), 16)

        class Sources:

            def __init__(self, sb, name, table, free, over=None):
                self.table, self.free, self.over = table, free, over
                self.rows = [sb(f"{name}_rows{b}", [P, TILES, D]) for b in range(RING)]
                self.landed = self.ready = signal(f"{name}_loaded", 16, ring=RING)
                if over is not None:
                    self.over_at = [sb(f"{name}_over_at{b}", [P, TILES], I32) for b in range(RING)]
                    self.over_index_done = signal("index_done")
                    self.ready = signal("gathered", 16 * TILES, ring=RING)

            def load(self, sp, st):
                for sig in self.free:
                    if st.back(RING):
                        sp.wait_ge(*sig.at(st.back(RING)))
                sp.dma_start(self.rows[st.offset % RING][:], edge_groups(self.table)[st.times(1)]).then_inc(self.landed.sem(st), 16)

            def overlay(self, pool, st):
                b = st.offset % RING
                if st.back(RING):
                    pool.wait_ge(*self.ready.at(st.back(RING)))
                pool.tensor_copy(self.over_at[b][:], src_slot[:, bass.ds(st.times(TILES), TILES)])\
                    .then_inc(self.over_index_done.sem(st), 1)
                pool.wait_ge(*self.over_index_done.at(st))
                pool.wait_ge(*self.landed.at(st))
                pool.sem_inc(pool_turns, 1)
                for j in range(TILES):
                    pool.indirect_dma_start(self.rows[b][:, j, :], None, self.over,
                                            bass.IndirectOffsetOnAxis(self.over_at[b][:, j:j + 1], 0),
                                            bounds_check=EDGE_PAD - 1, oob_is_err=False).then_inc(self.ready.sem(st), 16)

        class Sums:

            def __init__(self, sb, name, source, ready, free, parts=H):
                self.source, self.ready, self.free, self.parts = source, ready, free, parts
                self.columns = [sb(f"{name}_sums{b}", [P, parts, GROUP]) for b in range(2)]
                self.done = signal(f"{name}_sums_done")

            def scan(self, dve, st):
                b = st.parity
                dve.wait_ge(*self.ready.at(st))
                for sig in self.free:
                    if st.back(2):
                        dve.wait_ge(*sig.at(st.back(2)))
                if st.back(1):
                    dve.wait_ge(*self.done.at(st.back(1)))
                for k in range(self.parts):
                    carry = self.columns[1 - b][:, k, GROUP - 1:GROUP] if st.back(1) else 0.0
                    source = self.source[b][:, k, :] if isinstance(self.source, list) else self.source[:, k, :]
                    last = dve.tensor_tensor_scan(self.columns[b][:, k, :], same[:, bass.ds(st.times(GROUP), GROUP)], source,
                                                  carry, ALU.mult, ALU.add)
                last.then_inc(self.done.sem(st), 1)

        def tile_weight(st):
            return lambda j: weight_col[:, bass.ds(st.times(TILES, j), 1)]

        def turn_back(pe, psum, columns):
            for j in range(TILES):
                for k in range(H):
                    last = pe.transpose(psum[:, j // 2, (j % 2) * D + k * P:(j % 2) * D + (k + 1) * P],
                                        columns[:, k, j * P:(j + 1) * P], ident[:])
            return last

        n = EDGE_GROUPS
        two = range(2)

        with ExitStack() as own:
            sb = tensors(own)
            back_done = signal("back_done")
            part_done = signal("part_done")
            hop_stored = signal("hop_stored", 16, ring=2)
            part_stored = signal("part_stored", 16, ring=2)
            rows_back = [sb(f"rows_back{b}", [P, TILES, D]) for b in two]
            part = [sb(f"part{b}", [P, TILES, D]) for b in two]
            product_done = signal("product_done")
            back_turned = signal("back_turned")
            added_up = signal("added_up")
            norm = Norm(sb, "norm", None, None, psum_a, None, weight=tile_weight)
            bases_done = signal("bases_done", 2)
            bases_stored = signal("bases_stored", 32, ring=2)
            src_rows = Sources(sb, "src", xs_rows, [norm.h_done])
            dst_rows = Sources(sb, "dst", xd_rows, [part_done])
            base_gat = [sb(f"base_gat{b}", [P, TILES, D]) for b in two]
            base_lone = [sb(f"base_lone{b}", [P, TILES, D]) for b in two]
            norm.rows, norm.rows_ready = src_rows.rows, src_rows.ready
            sums = Sums(sb, "hop", psum_a, norm.turned, [product_done])
            norm.taken = sums.done
            with nc.Block() as block:
                @block.gpsimd
                def _(pool):
                    def bases(st):
                        b = st.parity
                        pool.wait_ge(*src_rows.ready.at(st))
                        if st.back(2):
                            pool.wait_ge(*bases_stored.at(st.back(2)))
                        for to, row in ((base_gat[b], bias0_row), (base_lone[b], lone_row)):
                            pool.tensor_tensor(to[:], src_rows.rows[st.offset % RING][:],
                                               row[:].unsqueeze(1).to_broadcast([P, TILES, D]), ALU.add).then_inc(bases_done.sem(st), 1)

                    pipeline(pool, n, [(1, bases)])

                @block.scalar
                def _(act):
                    def back(st):
                        act.wait_ge(*back_turned.at(st))
                        if st.back(2):
                            act.wait_ge(*hop_stored.at(st.back(2)))
                        act.activation(rows_back[st.parity][:], pair_rows(psum_c), ACT.Copy).then_inc(back_done.sem(st), 1)

                    pipeline(act, n, [(2, lambda st: norm.normalise_relu(act, st)), (5, back), (1, lambda st: norm.deviation(act, st))])

                @block.vector
                def _(dve):
                    def add_up(st):
                        b = st.parity
                        dve.wait_ge(*product_done.at(st))
                        dve.wait_ge(*dst_rows.ready.at(st))
                        if st.back(2):
                            dve.wait_ge(*part_stored.at(st.back(2)))
                        dve.tensor_tensor(part[b][:], pair_rows(psum_b), dst_rows.rows[st.offset % RING][:], ALU.add).then_inc(added_up.sem(st), 1)
                        dve.wait_ge(*added_up.at(st))
                        dve.tensor_tensor(part[b][:], part[b][:], bias0_row[:].unsqueeze(1).to_broadcast([P, TILES, D]), ALU.add)\
                           .then_inc(part_done.sem(st), 1)

                    pipeline(dve, n, [*norm.inverse(dve, 2),
                                      *woven(norm.moments(dve, 1), [(5, add_up), (3, lambda st: sums.scan(dve, st)),
                                                                    (2, lambda st: norm.weigh(dve, st))])])

                @block.tensor
                def _(pe):
                    def product(st):
                        pe.wait_ge(*sums.done.at(st))
                        if st.back(1):
                            pe.wait_ge(*back_done.at(st.back(1)))
                            pe.wait_ge(*added_up.at(st.back(1)))
                        turn_back(pe, psum_c, sums.columns[st.parity]).then_inc(back_turned.sem(st), 1)
                        rows_product(pe, psum_b, sums.columns[st.parity], w_hop0).then_inc(product_done.sem(st), 1)

                    pipeline(pe, n, [(3, lambda st: norm.turn(pe, st)), (4, product)])

                @block.sync
                def _(sp):
                    def store(st):
                        sp.wait_ge(*back_done.at(st))
                        sp.dma_start(edge_groups(hop1_rows)[st.times(1)], rows_back[st.parity][:]).then_inc(hop_stored.sem(st), 16)
                        sp.wait_ge(*part_done.at(st))
                        sp.dma_start(edge_groups(x1_part)[st.times(1)], part[st.parity][:]).then_inc(part_stored.sem(st), 16)

                    def store_bases(st):
                        sp.wait_ge(*bases_done.at(st))
                        for to, rows in ((xs_gat, base_gat), (xs_lone, base_lone)):
                            sp.dma_start(edge_groups(to)[st.times(1)], rows[st.parity][:]).then_inc(bases_stored.sem(st), 16)

                    pipeline(sp, n, [(0, lambda st: src_rows.load(sp, st)), (3, lambda st: dst_rows.load(sp, st)),
                                     (2, store_bases), (6, store)])
                    last_two(sp, bases_stored, n)
                    last_two(sp, hop_stored, n)
                    last_two(sp, part_stored, n)
            close(n)

        with ExitStack() as own:
            sb = tensors(own)
            weighted = signal("weighted")
            turned = signal("turned")
            product_done = signal("product_done")
            part_landed = signal("part_landed", 16, ring=2)
            x1_done = signal("x1_done")
            x1_stored = signal("x1_stored", 16, ring=2)
            h1c_done = signal("h1c_done")
            score_done = signal("score_done")
            score_out = signal("score_out")
            score_stored = signal("score_stored", 16, ring=2)
            part = [sb(f"part{b}", [P, TILES, D]) for b in two]
            x1 = [sb(f"x1_{b}", [P, TILES, D]) for b in two]
            scaled = [sb(f"scaled{b}", [P, TILES, D]) for b in two]
            h1c = [sb(f"h1c{b}", [P, H, GROUP]) for b in two]
            score = [sb(f"score{b}", [HEADS, GROUP]) for b in two]
            limit = sb("limit", [HEADS, EDGE_PAD], BF16)
            hop_rows = Gather(sb, "src", hop1_rows, src_slot, [weighted], EDGE_PAD - 1, zero=True)
            sums = Sums(sb, "hop", psum_a, turned, [product_done])
            norm = Norm(sb, "norm", x1, x1_done, psum_c, h1c_done)
            with nc.Block() as block:
                @block.sync
                def _(sp):
                    move(sp, (limit[:], limit_flags.to_broadcast([HEADS, EDGE_PAD])))

            with nc.Block() as block:
                @block.gpsimd
                def _(pool):
                    pipeline(pool, n, [(0, lambda st: hop_rows.fetch(pool, st))])

                @block.scalar
                def _(act):
                    def h1_out(st):
                        act.wait_ge(*norm.turned.at(st))
                        if st.back(2):
                            act.wait_ge(*score_done.at(st.back(2)))
                        act.activation(h1c[st.parity][:], psum_c[:], ACT.Copy).then_inc(h1c_done.sem(st), 1)

                    pipeline(act, n, [(5, lambda st: norm.normalise_relu(act, st)), (6, h1_out),
                                      (4, lambda st: norm.deviation(act, st))])

                @block.vector
                def _(dve):
                    def weigh(st):
                        b = st.parity
                        dve.wait_ge(*hop_rows.ready.at(st))
                        if st.back(2):
                            dve.wait_ge(*turned.at(st.back(2)))
                        for j in range(TILES):
                            last = dve.tensor_scalar(scaled[b][:, j, :], hop_rows.rows[st.offset % RING][:, j, :], tile_weight(st)(j), None, ALU.mult)
                        last.then_inc(weighted.sem(st), 1)

                    def add_up(st):
                        b = st.parity
                        dve.wait_ge(*product_done.at(st))
                        dve.wait_ge(*part_landed.at(st))
                        if st.back(2):
                            dve.wait_ge(*x1_stored.at(st.back(2)))
                            dve.wait_ge(*norm.h_done.at(st.back(2)))
                        dve.tensor_tensor(x1[b][:], pair_rows(psum_b), part[b][:], ALU.add).then_inc(x1_done.sem(st), 1)

                    def out_score(st):
                        dve.wait_ge(*score_done.at(st))
                        if st.back(2):
                            dve.wait_ge(*score_stored.at(st.back(2)))
                        dve.tensor_tensor(score[st.parity][:], psum_d[0:HEADS, 0, :], limit[:, bass.ds(st.times(GROUP), GROUP)], ALU.min)\
                           .then_inc(score_out.sem(st), 1)

                    pipeline(dve, n, [(8, out_score), *norm.inverse(dve, 5), (4, add_up),
                                      *woven(norm.moments(dve, 4), [(2, lambda st: sums.scan(dve, st)), (1, weigh)])])

                @block.tensor
                def _(pe):
                    def turn(st):
                        pe.wait_ge(*weighted.at(st))
                        if st.back(1):
                            pe.wait_ge(*sums.done.at(st.back(1)))
                        for k in range(H):
                            for j in range(TILES):
                                last = pe.transpose(psum_a[:, k, j * P:(j + 1) * P], scaled[st.parity][:, j, k * P:(k + 1) * P], ident[:])
                        last.then_inc(turned.sem(st), 1)

                    def product(st):
                        pe.wait_ge(*sums.done.at(st))
                        if st.back(1):
                            pe.wait_ge(*x1_done.at(st.back(1)))
                        rows_product(pe, psum_b, sums.columns[st.parity], w_hop1).then_inc(product_done.sem(st), 1)

                    def scores(st):
                        pe.wait_ge(*h1c_done.at(st))
                        if st.back(1):
                            pe.wait_ge(*score_out.at(st.back(1)))
                        for k in range(H):
                            last = pe.matmul(psum_d[0:HEADS, 0, :], gat_vd[:, k, :], h1c[st.parity][:, k, :], start=k == 0, stop=k == H - 1)
                        last.then_inc(score_done.sem(st), 1)

                    pipeline(pe, n, [(2, turn), (6, lambda st: norm.turn(pe, st)), (7, scores), (3, product)])

                @block.sync
                def _(sp):
                    def load(st):
                        if st.back(2):
                            sp.wait_ge(*x1_done.at(st.back(2)))
                        sp.dma_start(part[st.parity][:], edge_groups(x1_part)[st.times(1)]).then_inc(part_landed.sem(st), 16)

                    def store(st):
                        sp.wait_ge(*x1_done.at(st))
                        sp.dma_start(edge_groups(x1_rows)[st.times(1)], x1[st.parity][:]).then_inc(x1_stored.sem(st), 16)

                    def store_score(st):
                        sp.wait_ge(*score_out.at(st))
                        sp.dma_start(score_dst[:, bass.ds(st.times(GROUP), GROUP)], score[st.parity][:]).then_inc(score_stored.sem(st), 16)

                    pipeline(sp, n, [(3, load), (5, store), (9, store_score)])
                    last_two(sp, x1_stored, n)
                    last_two(sp, score_stored, n)
            close(n)

        with ExitStack() as own:
            sb = tensors(own)
            h1c_done = signal("h1c_done")
            gat_done = signal("gat_done")
            gat_out = signal("gat_out")
            gat_stored = signal("gat_stored", 16, ring=2)
            score_out = signal("score_out")
            score_stored = signal("score_stored", 16, ring=2)
            h1c = [sb(f"h1c{b}", [P, H, GROUP]) for b in two]
            gat = [sb(f"gat{b}", [P, H, GROUP]) for b in two]
            score = [sb(f"score{b}", [HEADS, GROUP]) for b in two]
            highest = [sb(f"highest{b}", [HEADS, GROUP]) for b in two]
            reset = sb("reset", [HEADS, EDGE_PAD], BF16)
            highest_done = signal("highest_done")
            highest_stored = signal("highest_stored", 16, ring=2)
            norm = Norm(sb, "norm", None, None, psum_a, h1c_done)
            src_rows = Sources(sb, "src", xs_gat, [norm.h_done], over=x1_rows)
            norm.rows, norm.rows_ready = src_rows.rows, src_rows.ready
            with nc.Block() as block:
                @block.sync
                def _(sp):
                    move(sp, (reset[:], reset_flags.to_broadcast([HEADS, EDGE_PAD])))

            with nc.Block() as block:
                @block.gpsimd
                def _(pool):
                    pipeline(pool, n, [(1, lambda st: src_rows.overlay(pool, st))])

                @block.scalar
                def _(act):
                    def h1_out(st):
                        act.wait_ge(*norm.turned.at(st))
                        if st.back(2):
                            act.wait_ge(*gat_done.at(st.back(2)))
                        act.activation(h1c[st.parity][:], psum_a[:], ACT.Copy).then_inc(h1c_done.sem(st), 1)

                    def out_score(st):
                        act.wait_ge(*gat_done.at(st))
                        if st.back(2):
                            act.wait_ge(*score_stored.at(st.back(2)))
                            act.wait_ge(*highest_done.at(st.back(2)))
                        act.activation(score[st.parity][:], psum_d[0:HEADS, 0, :], ACT.Copy).then_inc(score_out.sem(st), 1)

                    pipeline(act, n, [(6, out_score), (3, lambda st: norm.normalise_relu(act, st)), (4, h1_out),
                                      (2, lambda st: norm.deviation(act, st))])

                @block.vector
                def _(dve):
                    def out_gat(st):
                        dve.wait_ge(*gat_done.at(st))
                        if st.back(2):
                            dve.wait_ge(*gat_stored.at(st.back(2)))
                        dve.tensor_copy(gat[st.parity][:], psum_b[:]).then_inc(gat_out.sem(st), 1)

                    def highest_so_far(st):
                        b = st.parity
                        dve.wait_ge(*score_out.at(st))
                        if st.back(2):
                            dve.wait_ge(*highest_stored.at(st.back(2)))
                        if st.back(1):
                            dve.wait_ge(*highest_done.at(st.back(1)))
                        dve.tensor_tensor_scan(highest[b][:], reset[:, bass.ds(st.times(GROUP), GROUP)], score[b][:],
                                               highest[1 - b][:, GROUP - 1:GROUP] if st.back(1) else -FAR, ALU.add, ALU.max)\
                           .then_inc(highest_done.sem(st), 1)

                    pipeline(dve, n, [*norm.inverse(dve, 3), *woven(norm.moments(dve, 2), [(6, out_gat), (7, highest_so_far)])])

                @block.tensor
                def _(pe):
                    def product(st):
                        pe.wait_ge(*h1c_done.at(st))
                        if st.back(1):
                            pe.wait_ge(*gat_out.at(st.back(1)))
                            pe.wait_ge(*score_out.at(st.back(1)))
                        for k in range(H):
                            pe.matmul(psum_d[0:HEADS, 0, :], gat_vs[:, k, :], h1c[st.parity][:, k, :], start=k == 0, stop=k == H - 1)
                        columns_product(pe, psum_b, gat_w, h1c[st.parity]).then_inc(gat_done.sem(st), 1)

                    pipeline(pe, n, [(4, lambda st: norm.turn(pe, st)), (5, product)])

                @block.sync
                def _(sp):
                    def store(st):
                        sp.wait_ge(*score_out.at(st))
                        sp.dma_start(score_src[:, bass.ds(st.times(GROUP), GROUP)], score[st.parity][:]).then_inc(score_stored.sem(st), 16)
                        sp.wait_ge(*gat_out.at(st))
                        sp.dma_start(gat_columns[st.times(1)], gat[st.parity][:].rearrange("p k n -> p (k n)"))\
                          .then_inc(gat_stored.sem(st), 16)

                    def store_highest(st):
                        sp.wait_ge(*highest_done.at(st))
                        sp.dma_start(score_max[:, bass.ds(st.times(GROUP), GROUP)], highest[st.parity][:]).then_inc(highest_stored.sem(st), 16)

                    pipeline(sp, n, [(0, lambda st: src_rows.load(sp, st)), (7, store), (8, store_highest)])
                    last_two(sp, highest_stored, n)
                    last_two(sp, gat_stored, n)
                    last_two(sp, score_stored, n)
            close(n)

        with ExitStack() as own:
            sb = tensors(own)
            cuts = P // HEADS
            both = sb("softmax_both", [2 * HEADS, EDGE_PAD])
            reset_back = sb("softmax_reset", [2 * HEADS, EDGE_PAD], BF16)
            e, high, gain = (sb(f"softmax_{name}", [P, EDGE_PAD // cuts]) for name in ("e", "high", "gain"))

            cut_up = [sb(f"softmax_cut{i}", [P, EDGE_PAD // cuts], BF16) for i in range(3)]

            def split(dve):
                link(dve, dve.tensor_copy(cut_up[0][:], e[:]))
                rest = e
                for i in range(2):
                    link(dve, dve.tensor_copy(high[:], cut_up[i][:]))
                    link(dve, dve.tensor_tensor(gain[:], rest[:], high[:], ALU.subtract))
                    link(dve, dve.tensor_copy(cut_up[i + 1][:], gain[:]))
                    rest = gain

            def in_cuts(rows):
                return rows.rearrange("h (c i) -> (h c) i", c=cuts)

            with nc.Block() as block:
                @block.sync
                def _(sp):
                    move(sp, (both[0:HEADS, :], score_max), (both[HEADS:2 * HEADS, :], score_dst),
                         (reset_back[:], reset_back_flags.to_broadcast([2 * HEADS, EDGE_PAD])))

            with nc.Block() as block:
                @block.vector
                def _(dve):
                    link(dve, dve.tensor_tensor_scan(both[:, ::-1], reset_back[:, ::-1], both[:, ::-1], -FAR, ALU.add, ALU.max))

            with nc.Block() as block:
                @block.sync
                def _(sp):
                    move(sp, (spread_rows, both[:]))
                    move(sp, (e[:], in_cuts(score_src)), (high[:], in_cuts(spread_rows[0:HEADS])),
                         (gain[:], in_cuts(spread_rows[HEADS:2 * HEADS])))

            with nc.Block() as block:
                @block.vector
                def _(dve):
                    dve.tensor_tensor(e[:], e[:], gain[:], ALU.add)
                    link(dve, dve.tensor_tensor(high[:], high[:], gain[:], ALU.add))
                    dve.scalar_tensor_tensor(e[:], e[:], SLOPE, e[:], ALU.mult, ALU.max)
                    link(dve, dve.scalar_tensor_tensor(high[:], high[:], SLOPE, high[:], ALU.mult, ALU.max))
                    link(dve, dve.tensor_tensor(e[:], e[:], high[:], ALU.subtract))

            with nc.Block() as block:
                @block.scalar
                def _(act):
                    link(act, act.activation(e[:], e[:], ACT.Exp))

            with nc.Block() as block:
                @block.sync
                def _(sp):
                    move(sp, (in_cuts(exp_rows), e[:]))
                    move(sp, (both[0:HEADS, :], exp_rows))

                @block.vector
                def _(dve):
                    split(dve)

            with nc.Block() as block:
                @block.sync
                def _(sp):
                    move(sp, *((in_cuts(exp_cuts[i * HEADS:(i + 1) * HEADS]), cut_up[i][:]) for i in range(3)))

                @block.vector
                def _(dve):
                    link(dve, dve.tensor_tensor_scan(both[0:HEADS, :], same[0:HEADS, :], both[0:HEADS, :], 0.0, ALU.mult, ALU.add))

            with nc.Block() as block:
                @block.sync
                def _(sp):
                    move(sp, (inv_rows, both[0:HEADS, :]))
                    move(sp, (e[:], in_cuts(inv_rows)))

            with nc.Block() as block:
                @block.vector
                def _(dve):
                    link(dve, dve.tensor_scalar(e[:], e[:], 1e-16, None, ALU.add))
                    link(dve, dve.reciprocal(e[:], e[:]))
                    split(dve)

            with nc.Block() as block:
                @block.sync
                def _(sp):
                    move(sp, *((in_cuts(inv_cuts[i * HEADS:(i + 1) * HEADS]), cut_up[i][:]) for i in range(3)))

        with ExitStack() as own:
            sb = tensors(own)
            gat_landed = signal("gat_landed", 16, ring=2)
            exps_landed = signal("exps_landed", 16, ring=2)
            invs_landed = signal("invs_landed", 16, ring=2)
            part_landed = signal("part_landed", 16, ring=2)
            exps_spread = signal("exps_spread")
            invs_spread = signal("invs_spread")
            message_done = signal("message_done")
            divided = signal("divided")
            relu_done = signal("relu_done")
            back_turned = signal("back_turned")
            x2e_done = signal("x2e_done")
            x2e_stored = signal("x2e_stored", 16, ring=2)
            h2c_done = signal("h2c_done")
            h2c_stored = signal("h2c_stored", 16, ring=2)
            gat = [sb(f"gat{i}", [P, H, GROUP]) for i in two]
            exps = [sb(f"exps{i}", [3 * HEADS, GROUP], BF16) for i in two]
            invs = [sb(f"invs{i}", [3 * HEADS, GROUP], BF16) for i in two]
            message = [sb(f"message{i}", [P, H, GROUP]) for i in two]
            ratio = [sb(f"ratio{i}", [P, H, GROUP]) for i in two]
            part = [sb(f"part{i}", [P, TILES, D]) for i in two]
            x2e = [sb(f"x2e{i}", [P, TILES, D]) for i in two]
            h2c = [sb(f"h2c{i}", [P, H, GROUP]) for i in two]
            sums = Sums(sb, "gat", message, message_done, [divided])
            norm = Norm(sb, "norm", x2e, x2e_done, psum_d, h2c_done)
            with nc.Block() as block:
                @block.scalar
                def _(act):
                    def relu(st):
                        i = st.parity
                        act.wait_ge(*divided.at(st))
                        sem, value = relu_done.at(st)
                        for k in range(H):
                            last = act.activation(ratio[i][:, k, :], ratio[i][:, k, :], ACT.Relu, bias=bias1_col[:, k:k + 1])
                        last.then_inc(sem, 1)

                    def h2_out(st):
                        act.wait_ge(*norm.turned.at(st))
                        if st.back(2):
                            act.wait_ge(*h2c_stored.at(st.back(2)))
                        act.activation(h2c[st.parity][:], psum_d[:], ACT.Copy).then_inc(h2c_done.sem(st), 1)

                    pipeline(act, n, [(5, lambda st: norm.normalise_relu(act, st)), (6, h2_out),
                                      (2, relu), (4, lambda st: norm.deviation(act, st))])

                @block.vector
                def _(dve):
                    def weigh(st):
                        i = st.parity
                        dve.wait_ge(*gat_landed.at(st))
                        dve.wait_ge(*exps_spread.at(st))
                        dve.tensor_tensor(message[i][:], gat[i][:], psum_a[:], ALU.mult).then_inc(message_done.sem(st), 1)

                    def divide(st):
                        i = st.parity
                        dve.wait_ge(*sums.done.at(st))
                        dve.wait_ge(*invs_spread.at(st))
                        if st.back(2):
                            dve.wait_ge(*back_turned.at(st.back(2)))
                        dve.tensor_tensor(ratio[i][:], sums.columns[i][:], psum_b[:], ALU.mult).then_inc(divided.sem(st), 1)

                    def add_up(st):
                        i = st.parity
                        dve.wait_ge(*back_turned.at(st))
                        dve.wait_ge(*part_landed.at(st))
                        if st.back(2):
                            dve.wait_ge(*x2e_stored.at(st.back(2)))
                            dve.wait_ge(*norm.h_done.at(st.back(2)))
                        dve.tensor_tensor(x2e[i][:], pair_rows(psum_c), part[i][:], ALU.add).then_inc(x2e_done.sem(st), 1)

                    pipeline(dve, n, [*norm.inverse(dve, 5), (4, add_up),
                                      *woven(norm.moments(dve, 4), [(2, divide), (1, weigh), (1, lambda st: sums.scan(dve, st))])])

                @block.tensor
                def _(pe):
                    def spread_heads(psum, rows, landed, used_up, done, st):
                        pe.wait_ge(*landed.at(st))
                        if st.back(1):
                            pe.wait_ge(*used_up.at(st.back(1)))
                        for k in range(H):
                            last = pe.matmul(psum[:, k, :], head_sel[:, k * P:(k + 1) * P], rows[st.parity][:], start=True, stop=True)
                        last.then_inc(done.sem(st), 1)

                    def back(st):
                        pe.wait_ge(*relu_done.at(st))
                        if st.back(1):
                            pe.wait_ge(*x2e_done.at(st.back(1)))
                        turn_back(pe, psum_c, ratio[st.parity]).then_inc(back_turned.sem(st), 1)

                    pipeline(pe, n, [(1, lambda st: spread_heads(psum_a, exps, exps_landed, message_done, exps_spread, st)),
                                     (2, lambda st: spread_heads(psum_b, invs, invs_landed, divided, invs_spread, st)),
                                     (6, lambda st: norm.turn(pe, st)), (3, back)])

                @block.sync
                def _(sp):
                    def load(st):
                        i = st.parity
                        if st.back(2):
                            sp.wait_ge(*message_done.at(st.back(2)))
                        sp.dma_start(exps[i][:], exp_cuts[:, bass.ds(st.times(GROUP), GROUP)]).then_inc(exps_landed.sem(st), 16)
                        sp.dma_start(gat[i][:].rearrange("p k n -> p (k n)"), gat_columns[st.times(1)]).then_inc(gat_landed.sem(st), 16)

                    def load_inv(st):
                        if st.back(2):
                            sp.wait_ge(*invs_spread.at(st.back(2)))
                        sp.dma_start(invs[st.parity][:], inv_cuts[:, bass.ds(st.times(GROUP), GROUP)]).then_inc(invs_landed.sem(st), 16)

                    def load_x1(st):
                        i = st.parity
                        if st.back(2):
                            sp.wait_ge(*x2e_done.at(st.back(2)))
                        sp.dma_start(part[i][:], edge_groups(x1_rows)[st.times(1)]).then_inc(part_landed.sem(st), 16)

                    def store(st):
                        i = st.parity
                        sp.wait_ge(*x2e_done.at(st))
                        sp.dma_start(edge_groups(x2_rows)[st.times(1)], x2e[i][:]).then_inc(x2e_stored.sem(st), 16)

                    def store_columns(st):
                        i = st.parity
                        sp.wait_ge(*h2c_done.at(st))
                        sp.dma_start(h2_columns[st.times(1)], h2c[i][:].rearrange("p k n -> p (k n)")).then_inc(h2c_stored.sem(st), 16)

                    pipeline(sp, n, [(0, load), (1, load_inv), (3, load_x1), (5, store), (7, store_columns)])
                    last_two(sp, x2e_stored, n)
                    last_two(sp, h2c_stored, n)
            close(n)

        with ExitStack() as own:
            sb = tensors(own)
            h2c_landed = signal("h2c_landed", 16, ring=RING)
            part_landed = signal("part_landed", 16, ring=2)
            side_done = signal("side_done")
            y_done = signal("y_done")
            x3_stored = signal("x3_stored", 16, ring=2)
            x3_sent = signal("x3_sent", 16 * TILES, ring=2)
            last_copied = signal("last_copied")
            h3c_done = signal("h3c_done")
            h3c_stored = signal("h3c_stored", 16, ring=2)
            h2c = [sb(f"h2c{i}", [P, H, GROUP]) for i in range(RING)]
            side = [sb(f"side{i}", [P, H, GROUP]) for i in two]
            part = [sb(f"part{i}", [P, TILES, D]) for i in two]
            h3c = [sb(f"h3c{i}", [P, H, GROUP]) for i in two]
            last_at = [sb(f"last_at{i}", [P, TILES], I32) for i in two]
            norm = Norm(sb, "norm", None, None, psum_a, None, weight=tile_weight)
            src_rows = Sources(sb, "src", xs_lone, [norm.h_done], over=x2_rows)
            norm.rows, norm.rows_ready = src_rows.rows, src_rows.ready
            sums = Sums(sb, "hop", psum_a, norm.turned, [side_done])
            norm.taken = sums.done
            norm3 = Norm(sb, "norm3", None, None, psum_c, h3c_done)
            tail = Tail(sb, y_done, part, part_landed, [x3_stored, x3_sent, norm3.h_done])
            norm3.rows, norm3.rows_ready = tail.x3, tail.x3_done
            with nc.Block() as block:
                @block.gpsimd
                def _(pool):
                    def send(st):
                        i = st.parity
                        if st.back(2):
                            pool.wait_ge(*x3_sent.at(st.back(2)))
                        pool.tensor_copy(last_at[i][:], last_col[:, bass.ds(st.times(TILES), TILES)]).then_inc(last_copied.sem(st), 1)
                        pool.wait_ge(*last_copied.at(st))
                        pool.wait_ge(*tail.x3_done.at(st))
                        pool.sem_inc(pool_turns, 1)
                        for j in range(TILES):
                            pool.indirect_dma_start(x3_nodes, bass.IndirectOffsetOnAxis(last_at[i][:, j:j + 1], 0),
                                                    tail.x3[i][:, j, :], None, bounds_check=N - 1, oob_is_err=False)\
                                .then_inc(x3_sent.sem(st), 16)

                    pipeline(pool, n, [(1, lambda st: src_rows.overlay(pool, st)), (8, send)])
                    last_two(pool, x3_sent, n)

                @block.scalar
                def _(act):
                    def h3_out(st):
                        act.wait_ge(*norm3.turned.at(st))
                        if st.back(2):
                            act.wait_ge(*h3c_stored.at(st.back(2)))
                        act.activation(h3c[st.parity][:], psum_c[:], ACT.Copy).then_inc(h3c_done.sem(st), 1)

                    pipeline(act, n, [(6, lambda st: tail.slope(act, st)), (9, h3_out),
                                      (3, lambda st: norm.normalise_relu(act, st)), (6, lambda st: tail.square_up(act, st)),
                                      (8, lambda st: norm3.normalise_relu(act, st)), (2, lambda st: norm.deviation(act, st)),
                                      (7, lambda st: norm3.deviation(act, st))])

                @block.vector
                def _(dve):
                    def interact(st):
                        i = st.parity
                        dve.wait_ge(*sums.done.at(st))
                        dve.wait_ge(*h2c_landed.at(st))
                        if st.back(2):
                            dve.wait_ge(*y_done.at(st.back(2)))
                        dve.scalar_tensor_tensor(side[i][:], h2c[st.offset % RING][:], 1.0, sums.columns[i][:], ALU.add, ALU.mult)\
                           .then_inc(side_done.sem(st), 1)

                    pipeline(dve, n, [*woven(norm.inverse(dve, 3), woven(norm3.inverse(dve, 8), tail.inverse(dve, 7))),
                                      (6, lambda st: tail.leak(dve, st)),
                                      (7, lambda st: tail.residual(dve, st)),
                                      (4, lambda st: sums.scan(dve, st)), (4, interact),
                                      (3, lambda st: norm.weigh(dve, st)),
                                      *woven(norm3.moments(dve, 7), norm.moments(dve, 2))])

                @block.tensor
                def _(pe):
                    def product(st):
                        pe.wait_ge(*side_done.at(st))
                        if st.back(1):
                            pe.wait_ge(*tail.leaky_done.at(st.back(1)))
                        for half in range(2):
                            pe.matmul(psum_b[:, half, :], ones_cuts[:], bias_cuts[:], start=True, stop=False, skip_group_check=True)
                        rows_product(pe, psum_b, h2c[st.offset % RING], w1, start=False, stop=False)
                        rows_product(pe, psum_b, side[st.parity], w2, start=False).then_inc(y_done.sem(st), 1)

                    pipeline(pe, n, [(4, lambda st: norm.turn(pe, st)), (9, lambda st: norm3.turn(pe, st)), (5, product)])

                @block.sync
                def _(sp):
                    def load(st):
                        if st.back(RING):
                            sp.wait_ge(*y_done.at(st.back(RING)))
                        sp.dma_start(h2c[st.offset % RING][:].rearrange("p k n -> p (k n)"), h2_columns[st.times(1)]).then_inc(h2c_landed.sem(st), 16)

                    def load_x2(st):
                        i = st.parity
                        if st.back(2):
                            sp.wait_ge(*tail.x3_done.at(st.back(2)))
                        sp.dma_start(part[i][:], edge_groups(x2_rows)[st.times(1)]).then_inc(part_landed.sem(st), 16)

                    def store(st):
                        i = st.parity
                        sp.wait_ge(*tail.x3_done.at(st))
                        sp.dma_start(edge_groups(x3_rows)[st.times(1)], tail.x3[i][:]).then_inc(x3_stored.sem(st), 16)

                    def store_columns(st):
                        i = st.parity
                        sp.wait_ge(*h3c_done.at(st))
                        sp.dma_start(h3_columns[st.times(1)], h3c[i][:].rearrange("p k n -> p (k n)")).then_inc(h3c_stored.sem(st), 16)

                    pipeline(sp, n, [(0, lambda st: src_rows.load(sp, st)), (2, load), (6, load_x2), (8, store), (10, store_columns)])
                    last_two(sp, x3_stored, n)
                    last_two(sp, h3c_stored, n)
            close(n)

        with ExitStack() as own:
            sb = tensors(own)
            hsc_done = signal("hsc_done")
            freq_done = signal("freq_done")
            freq_landed = signal("freq_landed", 16, ring=2)
            multiplied = signal("multiplied")
            combined = signal("combined")
            h3c_landed = signal("h3c_landed", 16, ring=2)
            g_done = signal("g_done")
            g_masked = signal("g_masked")
            g_counted = signal("g_counted")
            ge_stored = signal("ge_stored", 16, ring=2)
            hsc = [sb(f"hsc{i}", [P, H, GROUP]) for i in two]
            attr_f = [sb(f"attr_f{i}", [P, 3, GROUP]) for i in two]
            for_real = [sb(f"for_real{i}", [P, 2, GROUP]) for i in two]
            for_imaginary = [sb(f"for_imaginary{i}", [P, 2, GROUP]) for i in two]
            products = [sb(f"products{i}", [P, 2, GROUP]) for i in two]
            h3c = [sb(f"h3c{i}", [P, H, GROUP]) for i in two]
            ge = [sb(f"ge{i}", [P, H, GROUP]) for i in two]
            nxt = sb("next_wide", [P, EDGE_PAD], BF16)
            norm = Norm(sb, "norm3", None, None, psum_a, hsc_done,
                        scale=lambda st: norm_col[:, bass.ds(st.times(TILES), TILES)])
            src_rows = Gather(sb, "src", x3_nodes, src_col, [norm.h_done], N - 1)
            norm.rows, norm.rows_ready = src_rows.rows, src_rows.ready
            sums = Sums(sb, "freq", products, combined, [g_done])
            with nc.Block() as block:
                @block.sync
                def _(sp):
                    move(sp, (nxt[:], next_flags.to_broadcast([P, EDGE_PAD])))

            with nc.Block() as block:
                @block.gpsimd
                def _(pool):
                    def combine(st):
                        i = st.parity
                        pool.wait_ge(*multiplied.at(st))
                        if st.back(2):
                            pool.wait_ge(*sums.done.at(st.back(2)))
                        pool.tensor_tensor(products[i][:, 0, :], for_real[i][:, 0, :], for_real[i][:, 1, :], ALU.add)
                        pool.tensor_tensor(products[i][:, 1, :], for_imaginary[i][:, 0, :], for_imaginary[i][:, 1, :], ALU.subtract)\
                            .then_inc(combined.sem(st), 1)

                    pipeline(pool, n, [(6, combine), (0, lambda st: src_rows.fetch(pool, st))])

                @block.scalar
                def _(act):
                    def hs_out(st):
                        act.wait_ge(*norm.turned.at(st))
                        if st.back(2):
                            act.wait_ge(*freq_done.at(st.back(2)))
                        act.activation(hsc[st.parity][:], psum_a[:], ACT.Copy).then_inc(hsc_done.sem(st), 1)

                    pipeline(act, n, [(3, hs_out), (2, lambda st: norm.normalise_relu(act, st)),
                                      (1, lambda st: norm.deviation(act, st))])

                @block.vector
                def _(dve):
                    def multiply(st):
                        i = st.parity
                        dve.wait_ge(*freq_done.at(st))
                        dve.wait_ge(*freq_landed.at(st))
                        if st.back(2):
                            dve.wait_ge(*combined.at(st.back(2)))
                        dve.tensor_tensor(for_real[i][:], psum_c[:], attr_f[i][:, 0:2, :], ALU.mult)
                        dve.tensor_tensor(for_imaginary[i][:], psum_c[:], attr_f[i][:, 1:3, :], ALU.mult).then_inc(multiplied.sem(st), 1)

                    def mask(st):
                        i = st.parity
                        dve.wait_ge(*g_done.at(st))
                        if st.back(2):
                            dve.wait_ge(*ge_stored.at(st.back(2)))
                        for k in range(H):
                            last = dve.scalar_tensor_tensor(ge[i][:, k, :], nxt[:, bass.ds(st.times(GROUP), GROUP)], 0.0,
                                                            psum_b[:, k, :], ALU.is_equal, ALU.mult)
                        last.then_inc(g_masked.sem(st), 1)

                    def stats(st):
                        i = st.parity
                        dve.wait_ge(*g_masked.at(st))
                        for k in range(H):
                            last = dve.bn_stats(node_stats[:, k, bass.ds(st.times(6, 6 * NODE_GROUPS), 6)], ge[i][:, k, :])
                        last.then_inc(g_counted.sem(st), 1)

                    pipeline(dve, n, [*norm.inverse(dve, 2), (9, mask), (5, multiply),
                                      *woven(norm.moments(dve, 1), [(7, lambda st: sums.scan(dve, st)), (9, stats)])])
                    dve.wait_ge(*g_counted.at(Step(0, n - 1)))

                @block.tensor
                def _(pe):
                    def transform(st):
                        pe.wait_ge(*hsc_done.at(st))
                        if st.back(1):
                            pe.wait_ge(*multiplied.at(st.back(1)))
                        columns_product(pe, psum_c, freq, hsc[st.parity]).then_inc(freq_done.sem(st), 1)

                    def from_freq(st):
                        i = st.parity
                        pe.wait_ge(*sums.done.at(st))
                        pe.wait_ge(*h3c_landed.at(st))
                        if st.back(1):
                            pe.wait_ge(*g_masked.at(st.back(1)))
                        columns_product(pe, psum_b, w_back, sums.columns[i], stop=False)
                        columns_product(pe, psum_b, w_self, h3c[i], start=False).then_inc(g_done.sem(st), 1)

                    pipeline(pe, n, [(3, lambda st: norm.turn(pe, st)), (8, from_freq), (4, transform)])

                @block.sync
                def _(sp):
                    def load(st):
                        if st.back(2):
                            sp.wait_ge(*multiplied.at(st.back(2)))
                        sp.dma_start(attr_f[st.parity][:].rearrange("p k n -> p (k n)"), attr_freq[st.times(1)])\
                          .then_inc(freq_landed.sem(st), 16)

                    def load_h3(st):
                        i = st.parity
                        if st.back(2):
                            sp.wait_ge(*g_done.at(st.back(2)))
                        sp.dma_start(h3c[i][:].rearrange("p k n -> p (k n)"), h3_columns[st.times(1)]).then_inc(h3c_landed.sem(st), 16)

                    def store(st):
                        i = st.parity
                        sp.wait_ge(*g_masked.at(st))
                        sp.dma_start(g_edge_columns[st.times(1)], ge[i][:].rearrange("p k n -> p (k n)")).then_inc(ge_stored.sem(st), 16)

                    pipeline(sp, n, [(4, load), (7, load_h3), (10, store)])
                    last_two(sp, ge_stored, n)
            close(n)

        with ExitStack() as own:
            sb = tensors(own)
            total = sb("bn_total", [P, H, 2])
            mean = sb("bn_mean", [P, H])
            square = sb("bn_square", [P, H])
            var = sb("bn_var", [P, H])
            rows = float(NODE_PAD + EDGE_PAD) / N
            with nc.Block() as block:
                @block.vector
                def _(dve):
                    for k in range(H):
                        last = dve.bn_aggr(total[:, k, :], node_stats[:, k, :])
                    link(dve, last)
                    link(dve, dve.tensor_tensor(square[:], total[:, :, 0], total[:, :, 0], ALU.mult))
                    link(dve, dve.tensor_tensor(var[:], total[:, :, 1], square[:], ALU.add))
                    link(dve, dve.tensor_scalar(var[:], var[:], rows, None, ALU.mult))
                    link(dve, dve.tensor_scalar(mean[:], total[:, :, 0], rows, None, ALU.mult))
                    link(dve, dve.tensor_tensor(square[:], mean[:], mean[:], ALU.mult))
                    link(dve, dve.tensor_tensor(var[:], var[:], square[:], ALU.subtract))
                    link(dve, dve.tensor_tensor(mean[:], mean[:], wbias_col[:], ALU.add))

            with nc.Block() as block:
                @block.scalar
                def _(act):
                    link(act, act.activation(var[:], var[:], ACT.Sqrt, bias=eps_bn[:]))

            with nc.Block() as block:
                @block.vector
                def _(dve):
                    link(dve, dve.reciprocal(var[:], var[:]))
                    link(dve, dve.tensor_tensor(bn_scale[:], var[:], gamma_col[:], ALU.mult))
                    link(dve, dve.tensor_tensor(mean[:], wbias_col[:], mean[:], ALU.subtract))
                    link(dve, dve.tensor_tensor(mean[:], mean[:], bn_scale[:], ALU.mult))
                    link(dve, dve.tensor_tensor(bn_shift[:], mean[:], beta_col[:], ALU.add))

        def last_pass(n, columns, load_rows, finish, scatter):
            with ExitStack() as own:
                sb = tensors(own)
                c_landed = signal("c_landed", 16, ring=2)
                r_landed = signal("r_landed", 16, ring=2)
                tanh_done = signal("tanh_done")
                out_turned = signal("out_turned")
                out_done = signal("out_done")
                out_stored = signal("nodes_stored" if not scatter else "out_sent", 16 * TILES if scatter else 16, ring=2)
                last_copied = signal("last_copied")
                c_in = [sb(f"c_in{i}", [P, H, GROUP]) for i in two]
                r_in = [sb(f"r_in{i}", [P, TILES, D]) for i in two]
                act_c = [sb(f"act_c{i}", [P, H, GROUP]) for i in two]
                o_rows = [sb(f"o_rows{i}", [P, TILES, D]) for i in two]
                last_at = [sb(f"last_at{i}", [P, TILES], I32) for i in two]
                psums = [psum_a, psum_b]
                with nc.Block() as block:
                    @block.sync
                    def _(sp):
                        def load(st):
                            i = st.parity
                            if st.back(2):
                                sp.wait_ge(*tanh_done.at(st.back(2)))
                            sp.dma_start(c_in[i][:].rearrange("p k n -> p (k n)"), columns[st.times(1)]).then_inc(c_landed.sem(st), 16)
                            if st.back(2):
                                sp.wait_ge(*out_done.at(st.back(2)))
                            load_rows(sp, st, r_in[i]).then_inc(r_landed.sem(st), 16)

                        pipeline(sp, n, [(0, load)])

                    @block.scalar
                    def _(act):
                        def tanh(st):
                            i = st.parity
                            act.wait_ge(*c_landed.at(st))
                            if st.back(2):
                                act.wait_ge(*out_turned.at(st.back(2)))
                            for k in range(H):
                                last = act.activation(act_c[i][:, k, :], c_in[i][:, k, :], ACT.Tanh,
                                                      bias=bn_shift[:, k:k + 1], scale=bn_scale[:, k:k + 1])
                            last.then_inc(tanh_done.sem(st), 1)

                        pipeline(act, n, [(1, tanh)])

                    @block.tensor
                    def _(pe):
                        def back(st):
                            pe.wait_ge(*tanh_done.at(st))
                            if st.back(2):
                                pe.wait_ge(*out_done.at(st.back(2)))
                            turn_back(pe, psums[st.parity], act_c[st.parity]).then_inc(out_turned.sem(st), 1)

                        pipeline(pe, n, [(1, back)])

                    @block.vector
                    def _(dve):
                        def add(st):
                            i = st.parity
                            dve.wait_ge(*out_turned.at(st))
                            dve.wait_ge(*r_landed.at(st))
                            if st.back(2):
                                dve.wait_ge(*out_stored.at(st.back(2)))
                            dve.tensor_tensor(o_rows[i][:], pair_rows(psums[i]), r_in[i][:], ALU.add).then_inc(out_done.sem(st), 1)

                        pipeline(dve, n, [(2, add)])

                    @block.gpsimd
                    def _(pool):
                        def send(st):
                            i = st.parity
                            if scatter:
                                if st.back(2):
                                    pool.wait_ge(*out_stored.at(st.back(2)))
                                pool.tensor_copy(last_at[i][:], last_col[:, bass.ds(st.times(TILES), TILES)]).then_inc(last_copied.sem(st), 1)
                                pool.wait_ge(*last_copied.at(st))
                            pool.wait_ge(*out_done.at(st))
                            finish(pool, st, o_rows[i], last_at[i], out_stored)

                        pipeline(pool, n, [(2, send)])
                        last_two(pool, out_stored, n)
                if not scatter:
                    used.remove(last_copied)
                close(n)

        def load_nodes(sp, st, to):
            flat = to[:].rearrange("p j d -> p (j d)")
            if isinstance(st.turn, int) and st.offset == NODE_GROUPS - 1:
                return sp.dma_start(flat[0:TAIL_PARTS], tail_group(x3_nodes))
            return sp.dma_start(flat, by_group(x3_nodes)[st.times(1)])

        def store_nodes(pool, st, rows, _, stored):
            flat = rows[:].rearrange("p j d -> p (j d)")
            if isinstance(st.turn, int) and st.offset == NODE_GROUPS - 1:
                pool.dma_start(tail_group(out), flat[0:TAIL_PARTS]).then_inc(stored.sem(st), 16)
            else:
                pool.dma_start(by_group(out)[st.times(1)], flat).then_inc(stored.sem(st), 16)

        def send_edges(pool, st, rows, at, sent):
            pool.sem_inc(pool_turns, 1)
            for j in range(TILES):
                pool.indirect_dma_start(out, bass.IndirectOffsetOnAxis(at[:, j:j + 1], 0), rows[:, j, :], None,
                                        bounds_check=N - 1, oob_is_err=False).then_inc(sent.sem(st), 16)

        last_pass(NODE_GROUPS, g_node_columns, load_nodes, store_nodes, scatter=False)
        last_pass(EDGE_GROUPS, g_edge_columns,
                  lambda sp, st, to: sp.dma_start(to[:], edge_groups(x3_rows)[st.times(1)]), send_edges, scatter=True)


def constants():
    k, i = np.arange(P)[:, None], np.arange(D)[None, :]
    cos, sin = np.cos(2 * np.pi * k * i / D), np.sin(2 * np.pi * k * i / D)
    nyquist = (-1.0) ** i
    imaginary = -sin
    imaginary[0] = nyquist
    to_freq = np.concatenate([cos, imaginary]).T
    real = cos.copy()
    real[0] = -nyquist
    attr_to_freq = np.concatenate([cos, -sin, real]).T
    by_sum = 2 * cos / D
    by_sum[0] /= 2
    by_difference = -2 * sin / D
    by_difference[0] = nyquist / D
    from_freq = np.concatenate([by_sum, by_difference])
    heads = np.tile(np.repeat(np.eye(HEADS), D // HEADS, axis=1), (3, 1))
    return {"identity": np.eye(P), "to_freq": to_freq, "attr_to_freq": attr_to_freq, "from_freq_t": from_freq.T, "head_rows": heads}


def kernel(**inputs):
    from concourse import bacc
    from concourse.bass_utils import run_bass_kernel_spmd

    a = {k: np.asarray(v) for k, v in inputs.items()}
    row = lambda v: v.reshape(1, -1)
    arrays = {
        "x": a["x"], "src": a["src"], "dst": a["dst"], "edge_attr": a["edge_attr_256"], "edge_weight": a["edge_weight"],
        "w_hops": a["L0_gnn_W"], "bias0": row(a["L0_gnn_bias"]), "w_gat": a["L1_gnn_W"].reshape(D, D),
        "att_src": row(a["L1_gnn_att_src"]), "att_dst": row(a["L1_gnn_att_dst"]), "bias1": row(a["L1_gnn_bias"]),
        "w1_t": a["L2_gnn_W1"].T, "b1": row(a["L2_gnn_b1"]), "w2_t": a["L2_gnn_W2"].T, "b2": row(a["L2_gnn_b2"]),
        "w_loop": a["L3_gnn_w_loop"], "w_in": a["L3_gnn_w_in"], "loop_rel": a["L3_gnn_loop_rel"],
        "w_bias": row(a["L3_gnn_w_bias"]), "bn_gamma": row(a["L3_gnn_bn_gamma"]), "bn_beta": row(a["L3_gnn_bn_beta"]),
    }
    arrays |= {k: v.astype(np.float32) for k, v in constants().items()}
    nc = bacc.Bacc("TRN2", target_bir_lowering=False, num_devices=1)
    feed, args = {}, []
    for name, value in arrays.items():
        value = np.ascontiguousarray(value)
        feed[f"in_{name}"] = value
        args.append(nc.dram_tensor(f"in_{name}", value.shape, mybir.dt.from_np(value.dtype), kind="ExternalInput").ap())
    out = nc.dram_tensor("out_rows", (N, D), F32, kind="ExternalOutput").ap()
    gnn_kernel(nc, *args, out)
    result = run_bass_kernel_spmd(nc, [feed], core_ids=[0])
    return result.results[0]["out_rows"]
```
